# Optimizing a Trainium2 kernel written in Bass

```python
import numpy as np
import jax
import jax.numpy as jnp

def _softmax(x, axis=-1):
    return jax.nn.softmax(x, axis=axis)

def _gelu(x):
    return jax.nn.gelu(x, approximate=True)

def _silu(x):
    return jax.nn.silu(x)

def _sigmoid(x):
    return jax.nn.sigmoid(x)

def _layernorm(x, axis=-1, eps=1e-05):
    m = jnp.mean(x, axis=axis, keepdims=True)
    v = jnp.var(x, axis=axis, keepdims=True)
    return (x - m) / jnp.sqrt(v + eps)

def _scatter_add(tgt, idx, src, axis=0):
    return tgt.at[idx].add(src)

def _segment_sum(src, seg, n):
    return jax.ops.segment_sum(src, seg, n)
kernel_name = 'mk_decoder_preln_d1_seqx_r4_4d487b'

def setup_inputs(seed: int=0):
    np.random.seed(seed)
    _w = jnp.asarray

    def _rec_inputs():
        import jax
        import jax.numpy as jnp
        _rk = jax.random.key(seed)
        x = -0.0003929 + 0.9999 * jax.random.normal(jax.random.fold_in(_rk, 1), (8, 256, 256), jnp.float32)
        _lenS = 256 - jax.random.randint(jax.random.fold_in(_rk, 7), (8,), 0, max(1, 256 // 4) + 1, jnp.int32)
        _lenS2 = 256 - jax.random.randint(jax.random.fold_in(_rk, 8), (8,), 0, max(1, 256 // 4) + 1, jnp.int32)
        _ctx_1024P = jax.random.normal(jax.random.fold_in(_rk, 11), (8, 16, 256), jnp.float32)
        _ctx_1024c = jax.random.dirichlet(jax.random.fold_in(_rk, 511), 0.3 * jnp.ones((16,), jnp.float32), (8, 256))
        _ctx_1024t = jnp.einsum('bsk,bkd->bsd', _ctx_1024c, _ctx_1024P)
        _ctx_1024t = _ctx_1024t * jax.lax.rsqrt(jnp.mean(jnp.square(_ctx_1024t)) + 1e-12) * 0.953939
        ctx_1024 = 2.81802e-05 + 1.00001 * (_ctx_1024t + 0.3 * jax.random.normal(jax.random.fold_in(_rk, 611), (8, 256, 256), jnp.float32))
        itok_SxS2_0_2016 = jax.random.randint(jax.random.fold_in(_rk, 12), (256, 256), 0, 2017, jnp.int32)
        return (x, ctx_1024, itok_SxS2_0_2016)
    x, ctx_1024, itok_SxS2_0_2016 = _rec_inputs()

    def _L0_attn_setup():
        import jax, jax.numpy as jnp
        import numpy as np
        H = 16
        key = jax.random.key(seed)
        ks = jax.random.split(key, 7)
        B, L, D, d = (1, 256, 256, 256 // H)
        s = 0.02
        return {'x': jax.random.normal(ks[0], (B, L, D), jnp.float32), 'Wq': jax.random.normal(ks[1], (D, D), jnp.float32) * s, 'Wk': jax.random.normal(ks[2], (D, D), jnp.float32) * s, 'Wv': jax.random.normal(ks[3], (D, D), jnp.float32) * s, 'Wo': jax.random.normal(ks[4], (D, D), jnp.float32) * s, 'gw': jax.random.normal(ks[5], (1, d), jnp.float32) * s, 'sw': jax.random.normal(ks[6], (1, d), jnp.float32) * s}
    _L0_attn_all = _L0_attn_setup()
    _L0_attn_in = {k: v for k, v in _L0_attn_all.items() if k in ('Wq', 'Wk', 'Wv', 'Wo', 'gw', 'sw')}
    del _L0_attn_all

    def _L0_xattn_setup():
        import jax, jax.numpy as jnp
        import numpy as np
        B, S, DIM, NH = (64, 64, 256, 8)
        DH = DIM // NH
        EPS = 1e-06
        LN_EPS = 1e-05

        def _make_hops(n):
            hops = np.zeros((n, n), dtype=np.int64)
            cur = 1
            for i in range(n):
                for j in range(i + 1, n):
                    hops[i, j] = cur
                    hops[j, i] = cur
                    cur += 1
            return (hops, cur)

        def _mlstm_forward(q, k, v, igate_w, igate_b, fgate_w, fgate_b, rpe, ln_w, ln_b, hops):
            Bq, Sq, _ = q.shape
            pos_emb = rpe[hops]
            gate_in = jnp.concatenate([q, k, v], axis=-1)
            ig = gate_in @ igate_w.T + igate_b
            fg = gate_in @ fgate_w.T + fgate_b
            ig = jnp.transpose(ig, (0, 2, 1))
            fg = jnp.transpose(fg, (0, 2, 1))
            qh = q.reshape(Bq, Sq, NH, DH).transpose(0, 2, 1, 3)
            kh = k.reshape(Bq, Sq, NH, DH).transpose(0, 2, 1, 3)
            vh = v.reshape(Bq, Sq, NH, DH).transpose(0, 2, 1, 3)
            log_f = jax.nn.log_sigmoid(fg)
            csum = jnp.cumsum(log_f, axis=-1)
            csum = jnp.concatenate([jnp.zeros((Bq, NH, 1), csum.dtype), csum], axis=-1)
            lfm = csum[:, :, :, None] - csum[:, :, None, :]
            ltr = jnp.tril(jnp.ones((Sq, Sq), dtype=bool))
            log_fg_matrix = jnp.where(ltr, lfm[:, :, 1:, 1:], -jnp.inf)
            log_D = log_fg_matrix + ig[:, :, None, :]
            max_log_D = jnp.max(log_D, axis=-1, keepdims=True)
            D = jnp.exp(log_D - max_log_D)
            k_scaled = kh / np.sqrt(DH).astype(np.float32)
            pe = pos_emb.reshape(Sq, Sq, NH, DH)
            k_hop = jnp.einsum('bhvc,vmhc->bhvm', qh, pe)
            qk = jnp.einsum('bhsd,bhtd->bhst', qh, k_scaled)
            C = (qk + k_hop) * D
            normalizer = jnp.maximum(jnp.abs(jnp.sum(C, axis=-1, keepdims=True)), jnp.exp(-max_log_D))
            Cn = C / (normalizer + EPS)
            h = Cn @ vh
            mu = jnp.mean(h, axis=-1, keepdims=True)
            var = jnp.mean(jnp.square(h - mu), axis=-1, keepdims=True)
            hn = (h - mu) / jnp.sqrt(var + LN_EPS)
            w = (1.0 + ln_w).reshape(NH, DH)
            b = ln_b.reshape(NH, DH)
            hn = hn * w[None, :, None, :] + b[None, :, None, :]
            return hn.transpose(0, 2, 1, 3).reshape(Bq, Sq, DIM)
        key = jax.random.key(seed)
        ks = jax.random.split(key, 8)
        hops_np, curnum = _make_hops(S)
        return {'q': jax.random.normal(ks[0], (B, S, DIM), dtype=jnp.float32), 'k': jax.random.normal(ks[1], (B, S, DIM), dtype=jnp.float32), 'v': jax.random.normal(ks[2], (B, S, DIM), dtype=jnp.float32), 'igate_w': jax.random.normal(ks[3], (NH, 3 * DIM), dtype=jnp.float32) * 0.02, 'igate_b': jax.random.normal(ks[4], (NH,), dtype=jnp.float32) * 0.1, 'fgate_w': jax.random.normal(ks[5], (NH, 3 * DIM), dtype=jnp.float32) * 0.02, 'fgate_b': jnp.linspace(3.0, 6.0, NH, dtype=jnp.float32), 'rpe': jax.random.normal(ks[6], (curnum, DIM), dtype=jnp.float32) * 0.02, 'ln_w': jax.random.normal(ks[7], (DIM,), dtype=jnp.float32) * 0.1, 'ln_b': jnp.zeros((DIM,), dtype=jnp.float32), 'hops': jnp.asarray(hops_np)}
    _L0_xattn_all = _L0_xattn_setup()
    _L0_xattn_in = {k: v for k, v in _L0_xattn_all.items() if k in ('igate_w', 'igate_b', 'fgate_w', 'fgate_b', 'rpe', 'ln_w', 'ln_b')}
    del _L0_xattn_all

    def _L0_ffn_setup():
        import jax, jax.numpy as jnp
        import numpy as np
        B, L, D, I, E, K = (2, 512, 256, 1024, 8, 2)
        LN_EPS = 1e-05

        def _layernorm(x, g, b):
            m = jnp.mean(x, axis=-1, keepdims=True)
            v = jnp.mean(jnp.square(x - m), axis=-1, keepdims=True)
            return (x - m) * jax.lax.rsqrt(v + LN_EPS) * g + b
        key = jax.random.key(seed)
        ks = jax.random.split(key, 4)
        return {'hidden_states': jax.random.normal(ks[0], (B, L, D), dtype=jnp.float32), 'rn_g': jnp.ones((D,), jnp.float32), 'rn_b': jnp.zeros((D,), jnp.float32), 'router_w': jax.random.normal(ks[1], (E, D), jnp.float32) * 0.02, 'router_b': jnp.zeros((E,), jnp.float32), 'ln_g': jnp.ones((E, D), jnp.float32), 'ln_b': jnp.zeros((E, D), jnp.float32), 'w1': jax.random.normal(ks[2], (E, D, I), jnp.float32) * 0.02, 'b1': jnp.zeros((E, I), jnp.float32), 'w2': jax.random.normal(ks[3], (E, I, D), jnp.float32) * 0.02, 'b2': jnp.zeros((E, D), jnp.float32)}
    _L0_ffn_all = _L0_ffn_setup()
    _L0_ffn_in = {k: v for k, v in _L0_ffn_all.items() if k in ('rn_g', 'rn_b', 'router_w', 'router_b', 'ln_g', 'ln_b', 'w1', 'b1', 'w2', 'b2')}
    del _L0_ffn_all
    return {'x': x, 'ctx_1024': ctx_1024, 'itok_SxS2_0_2016': itok_SxS2_0_2016, 'L0_attn_Wq': _L0_attn_in['Wq'], 'L0_attn_Wk': _L0_attn_in['Wk'], 'L0_attn_Wv': _L0_attn_in['Wv'], 'L0_attn_Wo': _L0_attn_in['Wo'], 'L0_attn_gw': _L0_attn_in['gw'], 'L0_attn_sw': _L0_attn_in['sw'], 'L0_xattn_igate_w': _L0_xattn_in['igate_w'], 'L0_xattn_igate_b': _L0_xattn_in['igate_b'], 'L0_xattn_fgate_w': _L0_xattn_in['fgate_w'], 'L0_xattn_fgate_b': _L0_xattn_in['fgate_b'], 'L0_xattn_rpe': _L0_xattn_in['rpe'], 'L0_xattn_ln_w': _L0_xattn_in['ln_w'], 'L0_xattn_ln_b': _L0_xattn_in['ln_b'], 'L0_ffn_rn_g': _L0_ffn_in['rn_g'], 'L0_ffn_rn_b': _L0_ffn_in['rn_b'], 'L0_ffn_router_w': _L0_ffn_in['router_w'], 'L0_ffn_router_b': _L0_ffn_in['router_b'], 'L0_ffn_ln_g': _L0_ffn_in['ln_g'], 'L0_ffn_ln_b': _L0_ffn_in['ln_b'], 'L0_ffn_w1': _L0_ffn_in['w1'], 'L0_ffn_b1': _L0_ffn_in['b1'], 'L0_ffn_w2': _L0_ffn_in['w2'], 'L0_ffn_b2': _L0_ffn_in['b2']}

def reference(x, ctx_1024, itok_SxS2_0_2016, L0_attn_Wq, L0_attn_Wk, L0_attn_Wv, L0_attn_Wo, L0_attn_gw, L0_attn_sw, L0_xattn_igate_w, L0_xattn_igate_b, L0_xattn_fgate_w, L0_xattn_fgate_b, L0_xattn_rpe, L0_xattn_ln_w, L0_xattn_ln_b, L0_ffn_rn_g, L0_ffn_rn_b, L0_ffn_router_w, L0_ffn_router_b, L0_ffn_ln_g, L0_ffn_ln_b, L0_ffn_w1, L0_ffn_b1, L0_ffn_w2, L0_ffn_b2):
    import jax
    import jax.numpy as jnp

    def _L0_attn_ref(x, Wq, Wk, Wv, Wo, gw, sw):
        import jax, jax.numpy as jnp
        import numpy as np
        H = 16
        B, L, D = x.shape
        d = D // H
        Q = (x @ Wq.T).reshape(B, L, H, d)
        K = (x @ Wk.T).reshape(B, L, H, d)
        V = (x @ Wv.T).reshape(B, L, H, d)
        KV = jnp.einsum('blhd,blhe->blhde', K, V)
        g = jax.nn.sigmoid(x.reshape(B, L, H, d) @ gw.T)
        g = jnp.clip(g, 1e-06, None)
        log_c = jnp.clip(jnp.cumsum(jnp.log(g), axis=1), -30.0, 30.0)
        Gc = (jnp.exp(log_c) + 1e-06)[..., None]
        R = jax.nn.silu(K @ sw.T)[..., None]
        S = jnp.cumsum(KV * R / Gc, axis=1) * Gc
        out = jnp.einsum('blhd,blhde->blhe', Q, S).reshape(B, L, D)
        return out @ Wo.T

    def _L0_xattn_ref(q, k, v, igate_w, igate_b, fgate_w, fgate_b, rpe, ln_w, ln_b, hops):
        import jax, jax.numpy as jnp
        import numpy as np
        B, S, DIM, NH = (64, 64, 256, 8)
        DH = DIM // NH
        EPS = 1e-06
        LN_EPS = 1e-05

        def _make_hops(n):
            hops = np.zeros((n, n), dtype=np.int64)
            cur = 1
            for i in range(n):
                for j in range(i + 1, n):
                    hops[i, j] = cur
                    hops[j, i] = cur
                    cur += 1
            return (hops, cur)

        def _mlstm_forward(q, k, v, igate_w, igate_b, fgate_w, fgate_b, rpe, ln_w, ln_b, hops):
            Bq, Sq, _ = q.shape
            pos_emb = rpe[hops]
            gate_in = jnp.concatenate([q, k, v], axis=-1)
            ig = gate_in @ igate_w.T + igate_b
            fg = gate_in @ fgate_w.T + fgate_b
            ig = jnp.transpose(ig, (0, 2, 1))
            fg = jnp.transpose(fg, (0, 2, 1))
            qh = q.reshape(Bq, Sq, NH, DH).transpose(0, 2, 1, 3)
            kh = k.reshape(Bq, Sq, NH, DH).transpose(0, 2, 1, 3)
            vh = v.reshape(Bq, Sq, NH, DH).transpose(0, 2, 1, 3)
            log_f = jax.nn.log_sigmoid(fg)
            csum = jnp.cumsum(log_f, axis=-1)
            csum = jnp.concatenate([jnp.zeros((Bq, NH, 1), csum.dtype), csum], axis=-1)
            lfm = csum[:, :, :, None] - csum[:, :, None, :]
            ltr = jnp.tril(jnp.ones((Sq, Sq), dtype=bool))
            log_fg_matrix = jnp.where(ltr, lfm[:, :, 1:, 1:], -jnp.inf)
            log_D = log_fg_matrix + ig[:, :, None, :]
            max_log_D = jnp.max(log_D, axis=-1, keepdims=True)
            D = jnp.exp(log_D - max_log_D)
            k_scaled = kh / np.sqrt(DH).astype(np.float32)
            pe = pos_emb.reshape(Sq, Sq, NH, DH)
            k_hop = jnp.einsum('bhvc,vmhc->bhvm', qh, pe)
            qk = jnp.einsum('bhsd,bhtd->bhst', qh, k_scaled)
            C = (qk + k_hop) * D
            normalizer = jnp.maximum(jnp.abs(jnp.sum(C, axis=-1, keepdims=True)), jnp.exp(-max_log_D))
            Cn = C / (normalizer + EPS)
            h = Cn @ vh
            mu = jnp.mean(h, axis=-1, keepdims=True)
            var = jnp.mean(jnp.square(h - mu), axis=-1, keepdims=True)
            hn = (h - mu) / jnp.sqrt(var + LN_EPS)
            w = (1.0 + ln_w).reshape(NH, DH)
            b = ln_b.reshape(NH, DH)
            hn = hn * w[None, :, None, :] + b[None, :, None, :]
            return hn.transpose(0, 2, 1, 3).reshape(Bq, Sq, DIM)
        return _mlstm_forward(q, k, v, igate_w, igate_b, fgate_w, fgate_b, rpe, ln_w, ln_b, hops)

    def _L0_ffn_ref(hidden_states, rn_g, rn_b, router_w, router_b, ln_g, ln_b, w1, b1, w2, b2):
        import jax, jax.numpy as jnp
        import numpy as np
        B, L, D, I, E, K = (2, 512, 256, 1024, 8, 2)
        LN_EPS = 1e-05

        def _layernorm(x, g, b):
            m = jnp.mean(x, axis=-1, keepdims=True)
            v = jnp.mean(jnp.square(x - m), axis=-1, keepdims=True)
            return (x - m) * jax.lax.rsqrt(v + LN_EPS) * g + b
        normed = _layernorm(hidden_states, rn_g, rn_b)
        logits = (jnp.einsum('bld,ed->ble', normed, router_w) + router_b).astype(jnp.float32)
        top_w, top_idx = jax.lax.top_k(logits, K)
        top_w = jax.nn.softmax(top_w, axis=-1).astype(hidden_states.dtype)
        onehot = jax.nn.one_hot(top_idx, E, dtype=top_w.dtype)
        combine = jnp.einsum('blke,blk->ble', onehot, top_w)
        out = jnp.zeros_like(hidden_states)
        for e in range(E):
            h = _layernorm(hidden_states, ln_g[e], ln_b[e])
            h = jax.nn.gelu(jnp.einsum('bld,di->bli', h, w1[e]) + b1[e], approximate=False)
            h = jnp.einsum('bli,id->bld', h, w2[e]) + b2[e]
            out = out + combine[..., e:e + 1] * h
        return out
    x = x + _L0_attn_ref(_layernorm(x, axis=-1), L0_attn_Wq, L0_attn_Wk, L0_attn_Wv, L0_attn_Wo, L0_attn_gw, L0_attn_sw)
    x = x + _L0_xattn_ref(_layernorm(x, axis=-1), ctx_1024, ctx_1024, L0_xattn_igate_w, L0_xattn_igate_b, L0_xattn_fgate_w, L0_xattn_fgate_b, L0_xattn_rpe, L0_xattn_ln_w, L0_xattn_ln_b, itok_SxS2_0_2016)
    x = x + _L0_ffn_ref(_layernorm(x, axis=-1), L0_ffn_rn_g, L0_ffn_rn_b, L0_ffn_router_w, L0_ffn_router_b, L0_ffn_ln_g, L0_ffn_ln_b, L0_ffn_w1, L0_ffn_b1, L0_ffn_w2, L0_ffn_b2)
    return x

_drawn_inputs = setup_inputs


def setup_inputs(seed=0):
    import zlib

    import numpy as np

    out = dict(_drawn_inputs(seed))
    spreads = {'L0_xattn_ln_b': (0.0, 0.1),
     'L0_ffn_rn_g': (1.0, 0.2),
     'L0_ffn_rn_b': (0.0, 0.1),
     'L0_ffn_router_b': (0.0, 0.1),
     'L0_ffn_ln_g': (1.0, 0.2),
     'L0_ffn_ln_b': (0.0, 0.1),
     'L0_ffn_b1': (0.0, 0.1),
     'L0_ffn_b2': (0.0, 0.1)}
    factors = {}
    for name, (base, spread) in spreads.items():
        noise = np.random.default_rng([zlib.crc32(name.encode()), seed]).standard_normal(out[name].shape)
        drawn = base * np.exp(spread * noise) if base else spread * noise
        out[name] = jnp.asarray(drawn.astype(out[name].dtype))
    for name, factor in factors.items():
        out[name] = (out[name] * factor).astype(out[name].dtype)
    return out
```

```python
from contextlib import ExitStack

import numpy as np

import concourse.bass as bass
from concourse import mybir
from concourse.bass import ds

F32 = mybir.dt.float32
I32 = mybir.dt.int32
ALU = mybir.AluOpType
ACT = mybir.ActivationFunctionType
AX = mybir.AxisListType.X

P = 128
B, S, D = 8, 256, 256
T = B * S // P
HA, DA = 16, 16
HX, DX = 8, 32
E, I = 8, 1024
KC = D // P
HC = HA // KC
XC = HX // KC
LN_EPS = 1e-5
MLSTM_EPS = 1e-6

C_ID, C_TRI, C_TRIREV, C_ONE, C_BLK = 0, 128, 256, 384, 512
C_HM16, C_HM32, C_IOTA = 640, 648, 652
C_W = 660

NBLK = 257
GRP = 8
NPRE = 64
NRING = 24
U_W = 17400
NGS = (NPRE + NRING) // GRP


def constants():
    c = np.zeros((P, C_W), np.float32)
    p = np.arange(P)
    c[:, C_ID:C_ID + P] = np.eye(P)
    c[:, C_TRI:C_TRI + P] = p[:, None] <= p[None, :]
    c[:, C_TRIREV:C_TRIREV + P] = p[:, None] >= P - 1 - p[None, :]
    c[:, C_ONE:C_ONE + P] = 1.0
    c[:, C_BLK:C_BLK + P] = p[:, None] // DA == p[None, :] // DA
    c[:, C_HM16:C_HM16 + HC] = p[:, None] // DA == np.arange(HC)[None, :]
    c[:, C_HM32:C_HM32 + XC] = p[:, None] // DX == np.arange(XC)[None, :]
    c[:, C_IOTA:C_IOTA + E] = np.arange(E)[None, :] - E
    return c


def hop_layout(hops):
    h = np.asarray(hops)
    idx = np.empty((P, NBLK), np.int32)
    idx[:, 0] = h[S - 1, S - 1:P - 1:-1]
    for n in range(1, P):
        idx[:n, n] = h[n - 1, :n]
        idx[n:, n] = h[S - 1 - n, S - 1 - np.arange(n, P)]
    idx[:, P] = h[P - 1, :P]
    idx[:, P + 1:] = h[P:, :P].T
    return idx


class Chain:

    def __init__(self, eng, sem, base=0):
        self.eng, self.sem, self.n, self.base = eng, sem, 0, base

    def __call__(self, ins):
        self.n += 1
        ins.then_inc(self.sem, 1)
        self.eng.wait_ge(self.sem, self.base + self.n)


def build(nc, x_d, ctx_d, ctxr_d, idx_d, cst_d, wqT_d, wkT_d, wvT_d, woT_d, wk_d, gw_d, sw_d, wg_d, gb_d,
          rpe_d, lnw_d, lnb_d, rng_d, rnb_d, rw_d, rb_d, lg_d, lb_d, w1_d, b1_d, w2_d, b2_d, out_d):
    ctx = ExitStack()
    with ctx:
        phase = ExitStack()
        held = []

        def sem(name):
            h = phase.enter_context(nc.semaphore(name))
            held.append(h)
            return h

        def prime(sp, *groups):
            for g in groups:
                for h in g:
                    sp.sem_inc(h, 1)

        def next_phase():
            with nc.Block() as block:
                @block.sync
                def _(sp):
                    for h in held:
                        sp.sem_clear(h)
            held.clear()
            phase.close()

        def sems(name, n=2):
            return [sem(f"{name}{k}") for k in range(n)]

        def sb(name, shape, dt=F32):
            return ctx.enter_context(nc.sbuf_tensor(name, shape, dt))

        cst = sb("cst", [P, C_W])
        ident = cst[:, C_ID:C_ID + P]
        tri = cst[:, C_TRI:C_TRI + P]
        trirev = cst[:, C_TRIREV:C_TRIREV + P]
        ones = cst[:, C_ONE:C_ONE + P]
        blkm = cst[:, C_BLK:C_BLK + P]
        hm16 = cst[:, C_HM16:C_HM16 + HC]
        hm32 = cst[:, C_HM32:C_HM32 + XC]
        X = sb("X", [P, T, D])
        QT = sb("QT", [P, KC, B, S])
        KH = sb("KH", [P, (NBLK + 1) * HX * B])
        RING = sb("RING", [P, NRING * D])
        U = sb("U", [P, U_W])
        eps_ap = sb("eps", [P, 1])
        pad_v = sb("pad_v", [P, 8])
        PET = sb("PET", [P, 3, 512])
        GT = sb("GT", [P, 2, 2, HX, B])
        hopi = sb("hopi", [P, NBLK], I32)
        EX = sb("EX", [P, 2, HX * B])
        AT = sb("AT", [P, 2, HX * B])

        psum = [ctx.enter_context(nc.psum_tensor(f"ps{k}", [P, 512], F32)) for k in range(8)]
        negm_dram = nc.dram_tensor("negm", [HX * B, S], F32).ap()

        class Carve:
            def __init__(self, t, size):
                self.t, self.at, self.size = t, 0, size

            def __call__(self, *shape):
                n = int(np.prod(shape))
                a = self.t[:, self.at:self.at + n]
                self.at += n
                assert self.at <= self.size, (self.at, self.size)
                names = [f"d{k}" for k in range(len(shape))]
                if len(shape) == 1:
                    return a
                kw = {k: s for k, s in zip(names, shape)}
                return a.rearrange(f"p ({' '.join(names)}) -> p {' '.join(names)}", **kw)

        def bank(k, *shape):
            n = int(np.prod(shape))
            a = psum[k][:, 0:n]
            if len(shape) == 1:
                return a
            names = [f"d{j}" for j in range(len(shape))]
            return a.rearrange(f"p ({' '.join(names)}) -> p {' '.join(names)}", **dict(zip(names, shape)))

        cu = Carve(U, U_W)
        wqT, wkT, woT = cu(KC, D), cu(KC, D), cu(KC, D)
        wvx = cu(KC, D + 2 * HA)
        wg6 = cu(6, 2 * HX)
        gbias = cu(2 * HX)
        gwc, swc, swb = cu(1), cu(1), cu(HC)
        xn = [cu(2, D) for _ in range(2)]
        xnT = [cu(KC, S) for _ in range(2)]
        qT = [cu(KC, S) for _ in range(2)]
        kT = [cu(KC, S) for _ in range(2)]
        ktok = [cu(D) for _ in range(2)]
        vx = [cu(2, D + 2 * HA) for _ in range(2)]
        am = [cu(2, 4, P) for _ in range(2)]
        sm = [cu(KC, P) for _ in range(2)]
        qblk = [cu(2, HC, P) for _ in range(2)]
        cx = [cu(2, D) for _ in range(2)]
        st = [cu(2, 6) for _ in range(2)]
        mv = [cu(2, 2) for _ in range(2)]
        rstd = [cu(2) for _ in range(2)]
        eg = [cu(2, 2 * HA) for _ in range(2)]
        lgg = [cu(2, HA) for _ in range(2)]
        gc = [cu(2, HA) for _ in range(2)]
        coef = [cu(2, HA) for _ in range(2)]
        wkN = qblk[0][:, 0, 0:4, :].rearrange("p a (b c) -> p (a b c)", b=1).rearrange("p (k n) -> p k n", k=KC)

        sp_on = ctx.enter_context(nc.semaphore("sp_on"))
        gat = [ctx.enter_context(nc.semaphore(f"gathered{k}")) for k in range(NGS)]
        ld_idx, ld_cst, ld_x, ld_w = sem("ld_idx"), sem("ld_cst"), sem("ld_x"), sem("ld_w")
        w_ready, w_full = sem("w_ready"), sem("w_full")
        ch_v, ch_a = sem("ch_v"), sem("ch_a")
        mv_r, rstd_r, xn_r = sems("mv_r"), sems("rstd_r"), sems("xn_r")
        mv2_r, rstd2_r, q_r = sems("mv2_r"), sems("rstd2_r"), sems("q_r")
        eg_r, g_r, lg_r, gc_r, vp_r = sems("eg_r"), sems("g_r"), sems("lg_r"), sems("gc_r"), sems("vp_r")
        qb_r, av_d, att_r, cx_r = sems("qb_r"), sems("av_d"), sems("att_r"), sems("cx_r")
        T_full, T_cp, P_full, P_cp = sems("T_full"), sems("T_cp"), sems("P_full"), sems("P_cp")
        S_full, S_cp = sems("S_full"), sems("S_cp")
        TU, PU, SU = 4, 9, 8
        T_XN, T_ATT, T_Q, T_CX = range(TU)
        P_QT, P_KT, P_V0, P_V1, P_KTOK, P_CUM, P_STATE, P_OUT, P_GATE = range(PU)

        def gather(pool, n):
            dst = KH[:, n * D:(n + 1) * D] if n < NPRE else RING[:, (n - NPRE) % NRING * D:((n - NPRE) % NRING + 1) * D]
            pool.indirect_dma_start(out=dst, out_offset=None, in_=rpe_d,
                                    in_offset=bass.IndirectOffsetOnAxis(ap=hopi[:, n:n + 1], axis=0)) \
                .then_inc(gat[n // GRP % NGS], 16)

        with nc.Block() as block:
            @block.sync
            def _(sp):
                sp.dma_start(hopi[:, :], idx_d).then_inc(ld_idx, 16)
                prime(sp, T_cp, P_cp, S_cp, att_r)
                sp.dma_start(X[:, 0:2], x_d[0].rearrange("(c p) d -> p c d", p=P)).then_inc(ld_x, 16)
                sp.dma_start(cst[:, :], cst_d).then_inc(ld_cst, 16)
                for dst, src in ((wqT, wqT_d), (wkT, wkT_d), (wvx[:, :, 0:D], wvT_d), (woT, woT_d), (wkN, wk_d)):
                    sp.dma_start(dst, src.rearrange("(k p) n -> p k n", p=P)).then_inc(ld_w, 16)
                sp.dma_start(wg6, wg_d.rearrange("(k p) n -> p k n", p=P)).then_inc(ld_w, 16)
                sp.dma_start(gbias, gb_d.partition_broadcast(P)).then_inc(ld_w, 16)
                sp.dma_start(gwc, gw_d).then_inc(ld_w, 16)
                sp.dma_start(swc, sw_d).then_inc(ld_w, 16)
                sp.dma_start(X[:, 2:T], x_d[1:B].rearrange("b (c p) d -> p (b c) d", p=P)).then_inc(ld_x, 16)
                with sp.Fori(0, B // 2) as i:
                    for u in range(2):
                        sp.wait_ge(T_cp[u], TU * i + 1)
                        sp.sem_inc(sp_on, 1)
                        sp.dma_start(cx[u], ctx_d[ds(2 * i + u, 1)].rearrange("o (c p) d -> p (o c) d", p=P)) \
                            .then_inc(cx_r[u], 16)

            @block.gpsimd
            def _(pool):
                pool.wait_ge(ld_idx, 16)
                for n in range(NPRE + NRING):
                    gather(pool, n)

            @block.tensor
            def _(pe):
                pe.wait_ge(ld_w, 16 * 9)
                pe.wait_ge(ld_cst, 16)
                pe.wait_ge(w_ready, 1)
                for k in range(KC):
                    for o in range(KC):
                        mm = pe.matmul(bank(0, 512)[:, k * HA + o * HC:k * HA + (o + 1) * HC],
                                       wkN[:, o, k * P:(k + 1) * P], swb, start=True, stop=True)
                mm.then_inc(w_full, 1)
                pe.wait_ge(w_ready, 2)

                def turn(dst, src, last_sem):
                    for k in range(KC):
                        for c in range(2):
                            mm = pe.transpose(dst[:, k, c * P:(c + 1) * P], src[:, c, k * P:(k + 1) * P], ident)
                    mm.then_inc(last_sem, 1)

                with pe.Fori(0, B // 2) as i:
                    def t_xn(u):
                        pe.wait_ge(xn_r[u], i + 1)
                        pe.wait_ge(T_cp[u], TU * i + T_XN + 1)
                        turn(bank(4 * u, KC, S), xn[u], T_full[u])

                    def p_feat(u, w, use):
                        pe.wait_ge(T_cp[u], TU * i + T_XN + 1 + 1)
                        pe.wait_ge(P_cp[u], PU * i + use + 1)
                        o = bank(4 * u + 1, KC, S)
                        for j in range(KC):
                            for k in range(KC):
                                mm = pe.matmul(o[:, j, :], w[:, k, j * P:(j + 1) * P], xnT[u][:, k, :],
                                               start=(k == 0), stop=(k == KC - 1))
                        mm.then_inc(P_full[u], 1)

                    def p_tok(u, w, n, c, use):
                        pe.wait_ge(P_cp[u], PU * i + use + 1)
                        for k in range(KC):
                            mm = pe.matmul(bank(4 * u + 1, n), xnT[u][:, k, c * P:(c + 1) * P], w[:, k, 0:n],
                                           start=(k == 0), stop=(k == KC - 1))
                        mm.then_inc(P_full[u], 1)

                    def cum(u):
                        pe.wait_ge(lg_r[u], i + 1)
                        pe.wait_ge(P_cp[u], PU * i + P_CUM + 1)
                        o = bank(4 * u + 1, 2, HA)
                        pe.matmul(o[:, 0, :], tri, lgg[u][:, 0, :], start=True, stop=True)
                        pe.matmul(o[:, 1, :], ones, lgg[u][:, 0, :], start=True, stop=False)
                        pe.matmul(o[:, 1, :], tri, lgg[u][:, 1, :], start=False, stop=True).then_inc(P_full[u], 1)

                    def state(u):
                        pe.wait_ge(vp_r[u], i + 1)
                        pe.wait_ge(P_cp[u], PU * i + P_STATE + 1)
                        o = bank(4 * u + 1, KC, P)
                        for j in range(KC):
                            mm = pe.matmul(o[:, j, :], ktok[u][:, j * P:(j + 1) * P], vx[u][:, 0, j * P:(j + 1) * P],
                                           start=True, stop=True)
                        mm.then_inc(P_full[u], 1)

                    def score(u, n):
                        c, j, half = n // 4, n // 2 % 2, n % 2
                        pe.wait_ge(qb_r[u], 4 * i + n // 2 + 1)
                        if n == 0:
                            pe.wait_ge(P_cp[u], PU * i + P_KT + 1 + 1)
                        pe.wait_ge(S_cp[u], SU * i + n + 1)
                        pe.matmul(bank(4 * u + 2, 512), kT[u][:, j, c * P:(c + 1) * P],
                                  qblk[u][:, n // 2 % 2, half * 4:half * 4 + 4, :],
                                  start=True, stop=True).then_inc(S_full[u], 1)

                    def values(u, n):
                        c, j, half = n // 4, n // 2 % 2, n % 2
                        if n == 0:
                            pe.wait_ge(att_r[u], i + 1)
                        o = bank(4 * u + 3, 2, D)
                        if c == 1 and half == 0:
                            if j == 0:
                                pe.wait_ge(P_cp[u], PU * i + P_STATE + 1 + 1)
                            pe.matmul(o[:, 1, j * P:(j + 1) * P], qT[u][:, j, P:S], sm[u][:, j, :],
                                      start=True, stop=False, skip_group_check=True)
                        pe.wait_ge(S_cp[u], SU * i + n + 1 + 1)
                        for hh in range(4):
                            f = j * P + (half * 4 + hh) * DA
                            mm = pe.matmul(o[:, c, f:f + DA], am[u][:, n % 2, hh, :], vx[u][:, c, f:f + DA],
                                           start=(c == 0), stop=True, skip_group_check=True)
                        mm.then_inc(av_d[u], 1)

                    def t_att(u):
                        pe.wait_ge(att_r[u], i + 1 + 1)
                        pe.wait_ge(T_cp[u], TU * i + T_ATT + 1)
                        turn(bank(4 * u, KC, S), xn[u], T_full[u])

                    def p_out(u):
                        pe.wait_ge(T_cp[u], TU * i + T_ATT + 1 + 1)
                        pe.wait_ge(P_cp[u], PU * i + P_OUT + 1)
                        for c in range(2):
                            for k in range(KC):
                                mm = pe.matmul(bank(4 * u + 1, 2, D)[:, c, :], xnT[u][:, k, c * P:(c + 1) * P],
                                               woT[:, k, :], start=(k == 0), stop=(k == KC - 1))
                        mm.then_inc(P_full[u], 1)

                    def t_q(u):
                        pe.wait_ge(q_r[u], i + 1)
                        pe.wait_ge(T_cp[u], TU * i + T_Q + 1)
                        turn(bank(4 * u, KC, S), xn[u], T_full[u])

                    def t_cx(u):
                        pe.wait_ge(cx_r[u], 16 * i + 16)
                        pe.wait_ge(T_cp[u], TU * i + T_CX + 1)
                        turn(bank(4 * u, KC, S), cx[u], T_full[u])

                    def gates(u):
                        pe.wait_ge(T_cp[u], TU * i + T_CX + 1 + 1)
                        pe.wait_ge(P_cp[u], PU * i + P_GATE + 1)
                        o = bank(4 * u + 1, 2, 2 * HX)
                        for c in range(2):
                            for k in range(4):
                                src = qT[u] if k < 2 else kT[u]
                                mm = pe.matmul(o[:, c, :], src[:, k % 2, c * P:(c + 1) * P], wg6[:, k, :],
                                               start=(k == 0), stop=(k == 3))
                        mm.then_inc(P_full[u], 1)

                    def both(f, *a):
                        for u in range(2):
                            f(u, *a)

                    both(t_xn)
                    both(p_feat, wqT, P_QT)
                    both(p_feat, wkT, P_KT)
                    both(p_tok, wvx, D + 2 * HA, 0, P_V0)
                    both(p_tok, wvx, D + 2 * HA, 1, P_V1)
                    both(p_tok, wkT, D, 0, P_KTOK)
                    both(score, 0)
                    both(cum)
                    both(state)
                    for n in range(1, SU):
                        both(score, n)
                        both(values, n - 1)
                    both(values, SU - 1)
                    both(t_att)
                    both(p_out)
                    both(t_q)
                    both(t_cx)
                    both(gates)

            @block.scalar
            def _(act):
                CHAIN = 4
                with act.Fori(0, B // 2) as i:
                    link = Chain(act, ch_a, i * CHAIN)

                    def rs(u, ready, done):
                        act.wait_ge(ready[u], i + 1)
                        link(nc.scalar.activation(rstd[u], mv[u][:, :, 1], ACT.Ln, bias=eps_ap[:, :]))
                        nc.scalar.activation(rstd[u], rstd[u], ACT.Exp, scale=-0.5).then_inc(done[u], 1)

                    def t_copy(u, dsts, use):
                        act.wait_ge(T_full[u], TU * i + use + 1)
                        for dst in dsts:
                            ins = nc.scalar.activation(dst, bank(4 * u, KC, S), ACT.Copy)
                        ins.then_inc(T_cp[u], 1)

                    def p_copy(u, dst, shape, use):
                        act.wait_ge(P_full[u], PU * i + use + 1)
                        nc.scalar.activation(dst, bank(4 * u + 1, *shape), ACT.Copy).then_inc(P_cp[u], 1)

                    for u in range(2):
                        rs(u, mv_r, rstd_r)
                    for u in range(2):
                        t_copy(u, [xnT[u]], T_XN)
                    for u in range(2):
                        p_copy(u, qT[u], (KC, S), P_QT)
                    for u in range(2):
                        p_copy(u, kT[u], (KC, S), P_KT)
                    for c in range(2):
                        for u in range(2):
                            p_copy(u, vx[u][:, c, :], (D + 2 * HA,), P_V0 + c)
                    for u in range(2):
                        act.wait_ge(P_cp[u], PU * i + P_V1 + 1 + 1)
                        nc.scalar.activation(eg[u], vx[u][:, :, D:D + 2 * HA], ACT.Exp, scale=-1.0).then_inc(eg_r[u], 1)
                    for u in range(2):
                        p_copy(u, ktok[u], (D,), P_KTOK)
                    for u in range(2):
                        act.wait_ge(g_r[u], i + 1)
                        nc.scalar.activation(lgg[u], coef[u], ACT.Ln).then_inc(lg_r[u], 1)
                    for u in range(2):
                        act.wait_ge(P_cp[u], PU * i + P_CUM + 1 + 1)
                        nc.scalar.activation(gc[u], gc[u], ACT.Exp).then_inc(gc_r[u], 1)
                    for u in range(2):
                        t_copy(u, [xnT[u]], T_ATT)
                    for u in range(2):
                        rs(u, mv2_r, rstd2_r)
                    for u in range(2):
                        t_copy(u, [QT[:, :, ds(2 * i + u, 1), :].squeeze(2), qT[u]], T_Q)
                    for u in range(2):
                        t_copy(u, [kT[u]], T_CX)
                    assert link.n == CHAIN

            @block.vector
            def _(dve):
                dve.wait_ge(ld_cst, 16)
                dve.wait_ge(ld_w, 16 * 9)
                nc.vector.memset(eps_ap[:, :], LN_EPS)
                nc.vector.memset(wvx[:, :, D:D + 2 * HA], 0.0).then_inc(ch_v, 1)
                nc.vector.tensor_scalar(swb, hm16, swc, None, ALU.mult).then_inc(w_ready, 1)
                nc.vector.tensor_tensor(wg6[:, 2:4, :], wg6[:, 2:4, :], wg6[:, 4:6, :], ALU.add)
                dve.wait_ge(ch_v, 1)
                for k in range(KC):
                    nc.vector.tensor_scalar(wvx[:, k, D + k * HC:D + (k + 1) * HC], hm16, gwc, None, ALU.mult)
                dve.wait_ge(w_full, 1)
                nc.vector.tensor_copy(wvx[:, :, D + HA:D + 2 * HA], bank(0, KC, HA)).then_inc(w_ready, 1)

                def spacer():
                    nc.vector.memset(pad_v[:, pads[0] % 8:pads[0] % 8 + 1], 0.0)
                    pads[0] += 1

                pads = [0]
                CHAIN = 16
                with dve.Fori(0, B // 2) as i:
                    link = Chain(dve, ch_v, 1 + i * CHAIN)

                    def stats(u, done):
                        t0 = 4 * i + 2 * u
                        spacer()
                        for c in range(2):
                            ins = nc.vector.bn_stats(st[u][:, c, :], X[:, ds(t0 + c, 1)].rearrange("p o d -> p (o d)"))
                        link(ins)
                        spacer()
                        for c in range(2):
                            ins = nc.vector.bn_aggr(mv[u][:, c, :], st[u][:, c, :])
                        ins.then_inc(done[u], 1)

                    def norm(u, ready, done):
                        dve.wait_ge(ready[u], i + 1)
                        t0 = 4 * i + 2 * u
                        for c in range(2):
                            ins = nc.vector.tensor_scalar(xn[u][:, c, :],
                                                          X[:, ds(t0 + c, 1)].rearrange("p o d -> p (o d)"),
                                                          mv[u][:, c, 0:1], rstd[u][:, c:c + 1],
                                                          ALU.subtract, ALU.mult)
                        ins.then_inc(done[u], 1)

                    dve.wait_ge(ld_x, 32)
                    for u in range(2):
                        stats(u, mv_r)
                    for u in range(2):
                        norm(u, rstd_r, xn_r)

                    def blocks(u, m):
                        c, j = m // 2, m % 2
                        if m == 0:
                            dve.wait_ge(P_cp[u], PU * i + P_QT + 1 + 1)
                        if m >= 2:
                            dve.wait_ge(S_full[u], SU * i + 2 * (m - 2) + 2)
                        q = qT[u][:, j, c * P:(c + 1) * P].unsqueeze(1).to_broadcast([P, HC, P])
                        nc.vector.tensor_tensor(qblk[u][:, m % 2], q, hm16.unsqueeze(2).to_broadcast([P, HC, P]),
                                                ALU.mult).then_inc(qb_r[u], 1)

                    for m in range(2):
                        for u in range(2):
                            blocks(u, m)
                    for u in range(2):
                        dve.wait_ge(eg_r[u], i + 1)
                        link(nc.vector.tensor_scalar(eg[u], eg[u], 1.0, None, ALU.add))
                        link(nc.vector.reciprocal(eg[u], eg[u]))
                        nc.vector.tensor_scalar(coef[u], eg[u][:, :, 0:HA], 1e-6, None, ALU.max).then_inc(g_r[u], 1)

                    def masked(u, n):
                        dve.wait_ge(S_full[u], SU * i + n + 1)
                        if n >= 2:
                            dve.wait_ge(av_d[u], SU * i + n - 1)
                        nc.vector.tensor_tensor(am[u][:, n % 2], bank(4 * u + 2, 4, P),
                                                tri.unsqueeze(1).to_broadcast([P, 4, P]), ALU.mult) \
                            .then_inc(S_cp[u], 1)

                    for u in range(2):
                        masked(u, 0)
                    for u in range(2):
                        dve.wait_ge(P_full[u], PU * i + P_CUM + 1)
                        ins = nc.vector.tensor_scalar(gc[u], bank(4 * u + 1, 2, HA), -30.0, 30.0, ALU.max, ALU.min)
                        ins.then_inc(P_cp[u], 1)
                        dve.wait_ge(lg_r[u], i + 1)
                        link(nc.vector.tensor_tensor(coef[u], vx[u][:, :, D + HA:D + 2 * HA], eg[u][:, :, HA:2 * HA],
                                                     ALU.mult))
                    for u in range(2):
                        dve.wait_ge(gc_r[u], i + 1)
                        link(nc.vector.tensor_scalar(gc[u], gc[u], 1e-6, None, ALU.add))
                        link(nc.vector.reciprocal(eg[u][:, :, 0:HA], gc[u]))
                        link(nc.vector.tensor_tensor(coef[u], coef[u], eg[u][:, :, 0:HA], ALU.mult))
                        for c in range(2):
                            v = vx[u][:, c, 0:D].rearrange("p (h e) -> p h e", h=HA)
                            ins = nc.vector.tensor_tensor(v, v, coef[u][:, c, :].unsqueeze(2).to_broadcast([P, HA, DA]),
                                                          ALU.mult)
                        ins.then_inc(vp_r[u], 1)
                    for n in range(1, SU):
                        if n in (2, 4):
                            for u in range(2):
                                blocks(u, n // 2 + 1)
                        for u in range(2):
                            masked(u, n)
                        if n == 1:
                            for u in range(2):
                                dve.wait_ge(P_full[u], PU * i + P_STATE + 1)
                                ins = nc.vector.tensor_tensor(sm[u], bank(4 * u + 1, KC, P),
                                                              blkm.unsqueeze(1).to_broadcast([P, KC, P]), ALU.mult)
                                ins.then_inc(P_cp[u], 1)
                    for u in range(2):
                        dve.wait_ge(av_d[u], SU * i + SU)
                        for c in range(2):
                            ins = nc.vector.tensor_tensor(xn[u][:, c, :].rearrange("p (h e) -> p h e", h=HA),
                                                          bank(4 * u + 3, 2, HA, DA)[:, c],
                                                          gc[u][:, c, :].unsqueeze(2).to_broadcast([P, HA, DA]),
                                                          ALU.mult)
                        ins.then_inc(att_r[u], 1)
                    for u in range(2):
                        dve.wait_ge(P_full[u], PU * i + P_OUT + 1)
                        xt = X[:, ds(4 * i + 2 * u, 2), :]
                        nc.vector.tensor_tensor(xt, bank(4 * u + 1, 2, D), xt, ALU.add).then_inc(P_cp[u], 1)
                        dve.wait_ge(P_cp[u], PU * i + P_OUT + 1 + 1)
                    for u in range(2):
                        stats(u, mv2_r)
                    for u in range(2):
                        norm(u, rstd2_r, q_r)
                    for u in range(2):
                        dve.wait_ge(P_full[u], PU * i + P_GATE + 1)
                        for c in range(2):
                            o = GT[:, c, :, :, ds(2 * i + u, 1)].rearrange("p g h o -> p (g h) o")
                            ins = nc.vector.tensor_tensor(o, bank(4 * u + 1, 2, 2 * HX)[:, c, :].unsqueeze(2),
                                                          gbias.unsqueeze(2), ALU.add)
                        ins.then_inc(P_cp[u], 1)
                    assert link.n == CHAIN, link.n

        next_phase()

        QBLK = U[:, 0:KC * XC * B * S].rearrange("p (j h b s) -> p j h b s", j=KC, h=XC, b=B)
        KHv = KH[:, :].rearrange("p (s h b) -> p s h b", h=HX, b=B)
        qblk_v, qblk_a = sem("qblk_v"), sem("qblk_a")
        turned, prod = sem("turned"), sem("prod")
        pet_r, kh_cp = sems("pet_r"), sems("kh_cp")
        NPAIR = (NBLK + 1) // 2
        NGRP = (NBLK + GRP - 1) // GRP

        def tiles(q):
            return range(2 * q, min(2 * q + 2, NBLK))

        def gathered(n):
            g = n // GRP
            return sum(16 * (min(NBLK, (k + 1) * GRP) - k * GRP) for k in range(g % NGS, g + 1, NGS))

        def turn_copy(copy, wait, q):
            wait(turned, q + 1)
            if q >= 3:
                wait(prod, q - 2)
            w = len(tiles(q)) * KC * P
            copy(PET[:, q % 3, 0:w], bank(q % 4, 512)[:, 0:w]).then_inc(pet_r[q % 2], 1)

        def group_copy(copy, wait, g):
            n = min(NBLK, (g + 1) * GRP)
            wait(prod, (n + 1) // 2)
            w = (n - g * GRP) * HX * B
            copy(KH[:, g * 512:g * 512 + w], bank(4 + g % 2, 512)[:, 0:w]).then_inc(kh_cp[g % 2], 1)

        def copies(copy, wait, e):
            for q in range(NPAIR + 4):
                if q < NPAIR and q % 2 == e:
                    turn_copy(copy, wait, q)
                if q >= 6 and q % 4 == 2 and (q - 6) // 4 % 2 == e and (q - 6) // 4 < NGRP - 1:
                    group_copy(copy, wait, (q - 6) // 4)
            if (NGRP - 1) % 2 == e:
                group_copy(copy, wait, NGRP - 1)

        with nc.Block() as block:
            @block.gpsimd
            def _(pool):
                for n in range(NPRE + NRING, NBLK):
                    pool.wait_ge(turned, (n - NRING) // 2 + 1)
                    gather(pool, n)

            @block.tensor
            def _(pe):
                def turn(q):
                    n0 = 2 * q
                    if n0 % GRP == 0:
                        pe.wait_ge(gat[n0 // GRP % NGS], gathered(n0))
                    if q >= 4:
                        pe.wait_ge(pet_r[q % 2], (q - 4) // 2 + 1)
                    o = bank(q % 4, 2, KC, P)
                    for n in tiles(q):
                        src = KH[:, n * D:(n + 1) * D] if n < NPRE else RING[:, (n - NPRE) % NRING * D:((n - NPRE) % NRING + 1) * D]
                        for j in range(KC):
                            mm = pe.transpose(o[:, n % 2, j, :], src[:, j * P:(j + 1) * P], ident)
                    mm.then_inc(turned, 1)

                def products(q):
                    pe.wait_ge(pet_r[q % 2], q // 2 + 1)
                    g = 2 * q // GRP
                    if 2 * q % GRP == 0 and g >= 2:
                        pe.wait_ge(kh_cp[g % 2], g // 2)
                    pet = PET[:, q % 3, :].rearrange("p (n j m) -> p n j m", n=2, j=KC)
                    o = bank(4 + g % 2, GRP, KC, XC, B)
                    for n in tiles(q):
                        for j in range(KC):
                            if n < P:
                                mm = pe.matmul(o[:, n % GRP, j], pet[:, n % 2, j, :], QBLK[:, j, :, :, S - 1 - n],
                                               start=True, stop=True, skip_group_check=True)
                            if n >= 1:
                                m = min(n, P)
                                mm = pe.matmul(o[0:m, n % GRP, j], pet[:, n % 2, j, 0:m], QBLK[:, j, :, :, n - 1],
                                               start=True, stop=True, skip_group_check=True)
                    mm.then_inc(prod, 1)

                for q in range(NPAIR + 2):
                    if q < NPAIR:
                        turn(q)
                    if q == 2:
                        pe.wait_ge(qblk_v, 1)
                        pe.wait_ge(qblk_a, 1)
                    if q >= 2:
                        products(q - 2)

            @block.scalar
            def _(act):
                for h in range(XC):
                    ins = nc.scalar.activation(QBLK[:, 1, h], QT[:, 1], ACT.Copy, scale=hm32[:, h:h + 1])
                ins.then_inc(qblk_a, 1)
                copies(lambda o, a: nc.scalar.activation(o, a, ACT.Copy), act.wait_ge, 0)

            @block.vector
            def _(dve):
                for h in range(XC):
                    ins = nc.vector.tensor_scalar(QBLK[:, 0, h], QT[:, 0], hm32[:, h:h + 1], None, ALU.mult)
                ins.then_inc(qblk_v, 1)
                copies(nc.vector.tensor_copy, dve.wait_ge, 1)

        next_phase()

        R = HX * B
        cr = Carve(RING, NRING * D)
        r_t, r_l, r_F, r_a, r_M, r_ml, r_rev, r_one = [cr(S)[0:R] for _ in range(8)]
        r_full, r_ch, r_ab, r_ln, r_nm, r_am = sem("r_full"), sem("r_ch"), sem("r_ab"), sem("r_ln"), sem("r_nm"), sem("r_am")
        r_tt, r_dma, r_ach = sem("r_tt"), sem("r_dma"), sem("r_ach")
        with nc.Block() as block:
            @block.tensor
            def _(pe):
                for g in range(2):
                    for c in range(2):
                        mm = pe.transpose(bank(0, 2, 2, P)[0:R, g, c, :], GT[:, c, g].rearrange("p h b -> p (h b)"), ident)
                mm.then_inc(r_full, 1)
                pe.wait_ge(r_am, 1)
                pe.transpose(bank(1, 2, R)[:, 0], r_a[:, 0:P], ident[0:R, 0:R])
                pe.transpose(bank(1, 2, R)[:, 1], r_rev[:, 0:P], ident[0:R, 0:R]).then_inc(r_tt, 1)
                pe.transpose(bank(2, 2, R)[:, 0], r_ml[:, 0:P], ident[0:R, 0:R])
                pe.transpose(bank(2, 2, R)[:, 1], r_ml[:, P:S], ident[0:R, 0:R]).then_inc(r_tt, 1)

            @block.scalar
            def _(act):
                act.wait_ge(r_full, 1)
                nc.scalar.activation(r_t, bank(0, 2, S)[0:R, 1, :], ACT.Abs).then_inc(r_ab, 1)
                act.wait_ge(r_ab, 1)
                nc.scalar.activation(r_l, r_t, ACT.Exp, scale=-1.0).then_inc(r_ach, 1)
                act.wait_ge(r_ach, 1)
                nc.scalar.activation(r_l, r_l, ACT.Ln, bias=ones[0:R, 0:1]).then_inc(r_ln, 1)
                act.wait_ge(r_tt, 2)
                nc.scalar.activation(EX[:, :, :], bank(2, 2, R), ACT.Exp, scale=-1.0)

            @block.vector
            def _(dve):
                link = Chain(dve, r_ch)
                ig, fg = bank(0, 2, S)[0:R, 0, :], bank(0, 2, S)[0:R, 1, :]
                nc.vector.memset(r_one, 1.0)
                dve.wait_ge(r_full, 1)
                dve.wait_ge(r_ln, 1)
                link(nc.vector.scalar_tensor_tensor(r_t, fg, 0.0, r_l, ALU.min, ALU.subtract))
                link(nc.vector.tensor_tensor_scan(r_F, r_one, r_t, 0.0, ALU.mult, ALU.add))
                link(nc.vector.tensor_tensor(r_a, ig, r_F, ALU.subtract))
                link(nc.vector.tensor_tensor_scan(r_M, r_a, r_a, -3.0e38, ALU.max, ALU.max))
                nc.vector.tensor_scalar(r_l, r_M, -1.0, None, ALU.mult).then_inc(r_nm, 1)
                nc.vector.tensor_tensor(r_ml, r_F, r_M, ALU.add)
                nc.vector.tensor_copy(r_rev[:, 0:P], r_a[:, S - 1:P - 1:-1]).then_inc(r_am, 1)
                dve.wait_ge(r_tt, 1)
                nc.vector.tensor_copy(AT[:, :, :], bank(1, 2, R))

            @block.sync
            def _(sp):
                sp.wait_ge(r_nm, 1)
                sp.dma_start(negm_dram, r_l).then_inc(r_dma, 16)
                sp.wait_ge(r_dma, 16)

        co = Carve(RING, NRING * D)
        cq = Carve(QT[:, :, :, :].rearrange("p j b s -> p (j b s)"), KC * B * S)
        cp = Carve(PET[:, :, :].rearrange("p a b -> p (a b)"), 3 * 512)
        NVX = DX + 1
        mx = [co(2, HX, DX) for _ in range(2)]
        mk = [co(KC, S) for _ in range(2)]
        nm = [co(XC, S) for _ in range(2)]
        Dm = [cq(XC, S + P) for _ in range(2)]
        tmp = [co(2, 512) for _ in range(2)]
        v1 = [cp(2, HX, NVX) for _ in range(2)]
        pst = [cq(2, HX) for _ in range(2)]
        hmu = [cq(2, HX) for _ in range(2)]
        lnwb = cp(D)
        lnbb = cq(D)
        m_ld, m_cst = sem("m_ld"), sem("m_cst")
        mx_r, nm_r, v1_r, mk_r = sems("mx_r"), sems("nm_r"), sems("v1_r"), sems("mk_r")
        A_full, B_full, A_cp, B_cp = sems("A_full"), sems("B_full"), sems("A_cp"), sems("B_cp")
        arg_r, ex_r, dec_r, c_r, pv_r = sems("arg_r"), sems("ex_r"), sems("dec_r"), sems("c_r"), sems("pv_r")
        h_cp, var_r, mrs_r, hn_r, x2_r = sems("h_cp"), sems("var_r"), sems("mrs_r"), sems("hn_r"), sems("x2_r")
        m_ch, m_ach = sem("m_ch"), sem("m_ach")
        AU, BU = 4, 3
        with nc.Block() as block:
            @block.sync
            def _(sp):
                prime(sp, A_full, v1_r, arg_r, h_cp, A_cp, B_cp, x2_r)
                sp.dma_start(lnwb, lnw_d.partition_broadcast(P)).then_inc(m_ld, 16)
                sp.dma_start(lnbb, lnb_d.partition_broadcast(P)).then_inc(m_ld, 16)
                negm_v = negm_dram.rearrange("(h b) s -> b h s", b=B)
                with sp.Fori(0, B // 2) as i:
                    for u in range(2):
                        sp.wait_ge(A_full[u], AU * i + 1)
                        sp.sem_inc(sp_on, 1)
                        sp.wait_ge(v1_r[u], i + 1)
                        sp.sem_inc(sp_on, 1)
                        sp.dma_start(mx[u][:, 0].rearrange("p h d -> p (h d)"),
                                     ctx_d[ds(2 * i + u, 1), 0:P].rearrange("o p d -> p (o d)")).then_inc(mx_r[u], 16)
                        sp.dma_start(mx[u][:, 1].rearrange("p h d -> p (h d)"),
                                     ctxr_d[ds(2 * i + u, 1)].rearrange("o p d -> p (o d)")).then_inc(mx_r[u], 16)
                    for j in range(KC):
                        for u in range(2):
                            sp.wait_ge(arg_r[u], 2 * i + j + 1)
                            sp.sem_inc(sp_on, 1)
                            sp.dma_start(nm[u], negm_v[ds(2 * i + u, 1), j * XC:(j + 1) * XC].rearrange("o h s -> (o h) s")
                                         .partition_broadcast(P)).then_inc(nm_r[u], 16)

            @block.gpsimd
            def _(pool):
                pool.wait_ge(m_ld, 32)
                nc.gpsimd.tensor_scalar(lnwb, lnwb, 1.0, None, ALU.add)
                for u in range(2):
                    ins = nc.gpsimd.memset(v1[u][:, :, :, DX:NVX], 1.0)
                ins.then_inc(m_cst, 1)
                pool.wait_ge(m_cst, 1)
                with pool.Fori(0, B // 2) as i:
                    for j in range(KC):
                        for u in range(2):
                            pool.wait_ge(ex_r[u], 2 * i + j + 1)
                            nc.gpsimd.tensor_tensor(Dm[u][:, :, 0:P], Dm[u][:, :, 0:P],
                                                    tri.unsqueeze(1).to_broadcast([P, XC, P]), ALU.mult)
                            nc.gpsimd.tensor_tensor(Dm[u][:, :, S:S + P], Dm[u][:, :, S:S + P],
                                                    trirev.unsqueeze(1).to_broadcast([P, XC, P]), ALU.mult) \
                                .then_inc(dec_r[u], 1)
                    for u in range(2):
                        pool.wait_ge(hn_r[u], i + 1)
                        h = tmp[u].rearrange("p a b -> p (a b)")[:, 0:2 * D].rearrange("p (c d) -> p c d", c=2)
                        nc.gpsimd.tensor_tensor(h, h, lnwb.unsqueeze(1).to_broadcast([P, 2, D]), ALU.mult).then_inc(x2_r[u], 1)
                        pool.wait_ge(x2_r[u], 3 * i + 1 + 1)
                        nc.gpsimd.tensor_tensor(h, h, lnbb.unsqueeze(1).to_broadcast([P, 2, D]), ALU.add).then_inc(x2_r[u], 1)
                        pool.wait_ge(x2_r[u], 3 * i + 2 + 1)
                        xt = X[:, ds(4 * i + 2 * u, 2), :]
                        nc.gpsimd.tensor_tensor(xt, xt, h, ALU.add).then_inc(x2_r[u], 1)

            @block.tensor
            def _(pe):
                with pe.Fori(0, B // 2) as i:
                    def keys(u):
                        pe.wait_ge(mx_r[u], 32 * i + 32)
                        pe.wait_ge(A_cp[u], AU * i + 1)
                        for k in range(KC):
                            for c in range(2):
                                mm = pe.transpose(bank(4 * u, KC, 2, P)[:, k, c, :],
                                                  mx[u][:, c].rearrange("p h d -> p (h d)")[:, k * P:(k + 1) * P], ident)
                        mm.then_inc(A_full[u], 1)

                    def score(u, m):
                        j, q, b = m // 3, m % 3, ds(2 * i + u, 1)
                        if m % 2 == 0:
                            pe.wait_ge(A_cp[u], AU * i + m // 2 + 1 + 1)
                        else:
                            pe.wait_ge(A_cp[u], AU * i + 1 + 1)
                            pe.wait_ge(B_cp[u], BU * i + m // 2 + 1)
                        o = bank(4 * u + m % 2, 512)
                        if q < 2:
                            rhs = QBLK[:, j, 2 * q:2 * q + 2, b, :].rearrange("p h o s -> p h (o s)")
                            lhs = mk[u][:, j, 0:P]
                        else:
                            rhs = QBLK[:, j, :, b, P:S].rearrange("p h o s -> p h (o s)")
                            lhs = mk[u][:, j, P:S]
                        pe.matmul(o, lhs, rhs, start=True, stop=True).then_inc((B_full if m % 2 else A_full)[u], 1)

                    def values(u, j):
                        pe.wait_ge(c_r[u], 6 * i + 3 * j + 3)
                        pe.wait_ge(v1_r[u], i + 1 + 1)
                        if j == 0:
                            pe.wait_ge(h_cp[u], i + 1)
                        for hh in range(XC):
                            h = j * XC + hh
                            for c in range(2):
                                o = bank(4 * u + 2 + c, HX, NVX)[:, h, :]
                                mm = pe.matmul(o, Dm[u][:, hh, c * P:(c + 1) * P], v1[u][:, 0, h, :],
                                               start=True, stop=(c == 0), skip_group_check=True)
                            mm = pe.matmul(o, Dm[u][:, hh, S:S + P], v1[u][:, 1, h, :],
                                           start=False, stop=True, skip_group_check=True)
                        mm.then_inc(pv_r[u], 1)

                    for u in range(2):
                        keys(u)
                    for m in range(6):
                        for u in range(2):
                            score(u, m)
                        if m == 3:
                            for u in range(2):
                                values(u, 0)
                    for u in range(2):
                        values(u, 1)

            @block.scalar
            def _(act):
                ACHAIN = 2
                with act.Fori(0, B // 2) as i:
                    link = Chain(act, m_ach, i * ACHAIN)
                    for u in range(2):
                        act.wait_ge(A_full[u], AU * i + 1 + 1)
                        nc.scalar.activation(mk[u], bank(4 * u, KC, S), ACT.Copy, scale=float(DX) ** -0.5) \
                            .then_inc(A_cp[u], 1)
                    for u in range(2):
                        act.wait_ge(h_cp[u], i + 1)
                        nc.scalar.activation(v1[u][:, :, :, 0:DX], mx[u], ACT.Copy).then_inc(v1_r[u], 1)
                    for j in range(KC):
                        for u in range(2):
                            act.wait_ge(arg_r[u], 2 * i + j + 1 + 1)
                            nc.scalar.activation(Dm[u], Dm[u], ACT.Exp).then_inc(ex_r[u], 1)
                    for u in range(2):
                        act.wait_ge(var_r[u], i + 1)
                        link(nc.scalar.activation(hmu[u], hmu[u], ACT.Ln, bias=eps_ap[:, :], scale=1.0 / DX))
                        nc.scalar.activation(hmu[u], hmu[u], ACT.Exp, scale=-0.5).then_inc(mrs_r[u], 1)

            @block.vector
            def _(dve):
                MCHAIN = 18
                with dve.Fori(0, B // 2) as i:
                    link = Chain(dve, m_ch, i * MCHAIN)

                    def args(u, j):
                        dve.wait_ge(nm_r[u], 32 * i + 16 * j + 16)
                        if j == 1:
                            dve.wait_ge(pv_r[u], 2 * i + 1)
                        for hh in range(XC):
                            hb = (j * XC + hh) * B
                            nc.vector.tensor_scalar(Dm[u][:, hh, 0:S], nm[u][:, hh, :], AT[:, 0, ds(hb + 2 * i + u, 1)],
                                                    0.0, ALU.add, ALU.min)
                            ins = nc.vector.tensor_scalar(Dm[u][:, hh, S:S + P], nm[u][:, hh, P:S],
                                                          AT[:, 1, ds(hb + 2 * i + u, 1)], 0.0, ALU.add, ALU.min)
                        ins.then_inc(arg_r[u], 1)

                    def weights(u, m):
                        j, q = m // 3, m % 3
                        b = ds(2 * i + u, 1)
                        cpd = (B_cp if m % 2 else A_cp)[u]
                        dve.wait_ge((B_full if m % 2 else A_full)[u], (BU if m % 2 else AU) * i + m // 2 + 3 - 2 * (m % 2))
                        if q < 2:
                            kh = KHv[:, 1:S + 1, j * XC + 2 * q:j * XC + 2 * q + 2, b].rearrange("p s h o -> p h (s o)")
                            n, w, d = 2, S, Dm[u][:, 2 * q:2 * q + 2, 0:S]
                        else:
                            kh = KHv[:, 0:P, j * XC:(j + 1) * XC, b].rearrange("p s h o -> p h (s o)")
                            n, w, d = XC, P, Dm[u][:, :, S:S + P]
                        if m == 0:
                            dve.wait_ge(x2_r[u], 3 * i + 1)
                        tt = tmp[u][:, m % 2, :].rearrange("p (h s) -> p h s", h=n)
                        sc = bank(4 * u + m % 2, n, w)
                        if q == 2:
                            nc.vector.tensor_tensor(tt[:, :, ::-1], sc[:, :, ::-1], kh, ALU.add).then_inc(cpd, 1)
                        else:
                            nc.vector.tensor_tensor(tt, sc, kh, ALU.add).then_inc(cpd, 1)
                        dve.wait_ge(cpd, (BU if m % 2 else AU) * i + m // 2 + 3 - m % 2)
                        if q == 0:
                            dve.wait_ge(dec_r[u], 2 * i + j + 1)
                        nc.vector.tensor_tensor(d, tt, d, ALU.mult).then_inc(c_r[u], 1)

                    def finish(u):
                        dve.wait_ge(pv_r[u], 2 * i + 2)
                        h = tmp[u].rearrange("p a b -> p (a b)")[:, 0:2 * D].rearrange("p (c h d) -> p c h d", c=2, h=HX)
                        exv = EX[:, :, :].rearrange("p c (h b) -> p c h b", b=B)[:, :, :, ds(2 * i + u, 1)].rearrange("p c h o -> p c (h o)")
                        for c in range(2):
                            ins = nc.vector.tensor_scalar(pst[u][:, c], bank(4 * u + 2 + c, HX, NVX)[:, :, DX], -1.0, None, ALU.mult)
                        link(ins)
                        for c in range(2):
                            ins = nc.vector.tensor_tensor(pst[u][:, c], bank(4 * u + 2 + c, HX, NVX)[:, :, DX], pst[u][:, c], ALU.max)
                        link(ins)
                        link(nc.vector.tensor_tensor(pst[u], pst[u], exv, ALU.max))
                        link(nc.vector.tensor_scalar(pst[u], pst[u], MLSTM_EPS, None, ALU.add))
                        link(nc.vector.reciprocal(pst[u], pst[u]))
                        for c in range(2):
                            ins = nc.vector.tensor_tensor(h[:, c], bank(4 * u + 2 + c, HX, NVX)[:, :, 0:DX],
                                                          pst[u][:, c].unsqueeze(2).to_broadcast([P, HX, DX]), ALU.mult)
                        ins.then_inc(h_cp[u], 1)
                        dve.wait_ge(h_cp[u], i + 1 + 1)
                        hf = h.rearrange("p c h d -> p (c h) d")
                        hmf, psf = hmu[u].rearrange("p c h -> p (c h)"), pst[u].rearrange("p c h -> p (c h)")
                        link(nc.vector.tensor_reduce(out=hmf, in_=hf, op=ALU.add, axis=AX))
                        link(nc.vector.tensor_scalar(hmf, hmf, 1.0 / DX, None, ALU.mult))
                        link(nc.vector.tensor_tensor(hf, hf, hmf.unsqueeze(2).to_broadcast([P, 2 * HX, DX]), ALU.subtract))
                        sq = tmp[u].rearrange("p a b -> p (a b)")[:, 2 * D:4 * D].rearrange("p (h d) -> p h d", d=DX)
                        link(nc.vector.tensor_tensor(sq, hf, hf, ALU.mult))
                        nc.vector.tensor_reduce(out=hmf, in_=sq, op=ALU.add, axis=AX).then_inc(var_r[u], 1)
                        dve.wait_ge(mrs_r[u], i + 1)
                        nc.vector.tensor_tensor(hf, hf, hmf.unsqueeze(2).to_broadcast([P, 2 * HX, DX]), ALU.mult) \
                            .then_inc(hn_r[u], 1)

                    for u in range(2):
                        args(u, 0)
                    for m in range(3):
                        for u in range(2):
                            weights(u, m)
                    for u in range(2):
                        args(u, 1)
                    for m in range(3, 6):
                        for u in range(2):
                            weights(u, m)
                    for u in range(2):
                        finish(u)
                    assert link.n == MCHAIN, link.n

        next_phase()

        cf = Carve(U, U_W)
        ZT = QT[:, :, :, :].rearrange("p j b s -> p j (b s)")
        hid = [cf(2, D) for _ in range(2)]
        zt = [cf(2, D) for _ in range(2)]
        zs = [cf(KC, S) for _ in range(2)]
        fst = [cf(2, 6) for _ in range(2)]
        fmv = [cf(2, 2) for _ in range(2)]
        frs = [cf(2) for _ in range(2)]
        rwT, rwp, rnbb = cf(KC, E), cf(KC, E), cf(KC, P)
        rngc, rnbc, rbb = cf(KC), cf(KC), cf(E)
        LG, LG2, EQ = cf(T, E), cf(T, E), cf(T, E)
        OH = [cf(T, E) for _ in range(2)]
        M1, M2, IX, PR = cf(T), cf(T), cf(T), cf(T)
        comb = KH[:, NBLK * HX * B - T * E:NBLK * HX * B].rearrange("p (t e) -> p t e", e=E)
        combT = cf(T * P)
        b2s = cf(D)
        f_ld, f_w, f_rb = sem("f_ld"), sem("f_w"), sem("f_rb")
        fmv_r, frs_r, hid_r, zt_r = sems("fmv_r"), sems("frs_r"), sems("hid_r"), sems("zt_r")
        FT_full, FT_cp, FL_full, FL_cp = sems("FT_full"), sems("FT_cp"), sems("FL_full"), sems("FL_cp")
        f_ch, f_ach, f_df, f_ex, f_cb = sem("f_ch"), sem("f_ach"), sem("f_df"), sem("f_ex"), sem("f_cb")
        f_ct, f_cc, f_bb = sem("f_ct"), sem("f_cc"), sem("f_bb")
        with nc.Block() as block:
            @block.sync
            def _(sp):
                prime(sp, FT_cp, FL_cp)
                sp.dma_start(rwT, rw_d.rearrange("(k p) n -> p k n", p=P)).then_inc(f_ld, 16)
                sp.dma_start(rngc, rng_d).then_inc(f_ld, 16)
                sp.dma_start(rnbc, rnb_d).then_inc(f_ld, 16)
                sp.dma_start(rbb, rb_d.partition_broadcast(P)).then_inc(f_ld, 16)
                sp.dma_start(b2s[0:E], b2_d).then_inc(f_ld, 16)

            @block.tensor
            def _(pe):
                pe.wait_ge(f_w, 1)
                for k in range(KC):
                    mm = pe.matmul(bank(7, E), rnbb[:, k, :], rwT[:, k, :], start=(k == 0), stop=(k == KC - 1))
                mm.then_inc(f_rb, 1)
                with pe.Fori(0, B // 2) as i:
                    for u in range(2):
                        pe.wait_ge(zt_r[u], i + 1)
                        pe.wait_ge(FT_cp[u], i + 1)
                        for k in range(KC):
                            for c in range(2):
                                mm = pe.transpose(bank(u, KC, 2, P)[:, k, c], zt[u][:, c, k * P:(k + 1) * P], ident)
                        mm.then_inc(FT_full[u], 1)
                    for u in range(2):
                        pe.wait_ge(FT_cp[u], i + 1 + 1)
                        pe.wait_ge(FL_cp[u], i + 1)
                        for c in range(2):
                            for k in range(KC):
                                mm = pe.matmul(bank(2 + u, 2, E)[:, c], zs[u][:, k, c * P:(c + 1) * P], rwp[:, k, :],
                                               start=(k == 0), stop=(k == KC - 1))
                        mm.then_inc(FL_full[u], 1)
                pe.wait_ge(f_cb, 1)
                for t in range(T):
                    mm = pe.transpose(bank(4 + t // 4, 4, P)[0:E, t % 4], comb[:, t, :], ident)
                mm.then_inc(f_ct, 1)
                pe.wait_ge(f_cc, 1)
                for t in range(T):
                    mm = pe.matmul(bank(t // 2, 2, D)[:, t % 2], combT[0:E, t * P:(t + 1) * P], b2s[0:E],
                                   start=True, stop=True)
                mm.then_inc(f_bb, 1)

            @block.scalar
            def _(act):
                with act.Fori(0, B // 2) as i:
                    link = Chain(act, f_ach, 4 * i)
                    for r in range(2):
                        for u in range(2):
                            act.wait_ge(fmv_r[u], 2 * i + r + 1)
                            link(nc.scalar.activation(frs[u], fmv[u][:, :, 1], ACT.Ln, bias=eps_ap[:, :]))
                            nc.scalar.activation(frs[u], frs[u], ACT.Exp, scale=-0.5).then_inc(frs_r[u], 1)
                    for u in range(2):
                        act.wait_ge(FT_full[u], i + 1)
                        nc.scalar.activation(ZT[:, :, ds((2 * i + u) * S, S)], bank(u, KC, S), ACT.Copy)
                        nc.scalar.activation(zs[u], bank(u, KC, S), ACT.Copy).then_inc(FT_cp[u], 1)
                act.wait_ge(f_df, 1)
                nc.scalar.activation(M2, M2, ACT.Exp).then_inc(f_ex, 1)
                act.wait_ge(f_ct, 1)
                for k in range(4):
                    ins = nc.scalar.activation(combT[0:E, k * 512:(k + 1) * 512], bank(4 + k, 512)[0:E], ACT.Copy)
                ins.then_inc(f_cc, 1)

            @block.vector
            def _(dve):
                pads = [0]

                def spacer():
                    nc.vector.memset(pad_v[:, pads[0] % 8:pads[0] % 8 + 1], 0.0)
                    pads[0] += 1

                dve.wait_ge(f_ld, 16 * 5)
                for k in range(KC):
                    nc.vector.tensor_scalar(rnbb[:, k, :], ones, rnbc[:, k:k + 1], None, ALU.mult)
                    ins = nc.vector.tensor_scalar(rwp[:, k, :], rwT[:, k, :], rngc[:, k:k + 1], None, ALU.mult)
                ins.then_inc(f_w, 1)
                dve.wait_ge(f_rb, 1)
                nc.vector.tensor_tensor(rbb, bank(7, E), rbb, ALU.add)
                FCHAIN = 4
                with dve.Fori(0, B // 2) as i:
                    link = Chain(dve, f_ch, FCHAIN * i)
                    for r in range(2):
                        for u in range(2):
                            if r == 1:
                                dve.wait_ge(hid_r[u], i + 1)
                            spacer()
                            for c in range(2):
                                src = hid[u][:, c, :] if r else X[:, ds(4 * i + 2 * u + c, 1)].rearrange("p o d -> p (o d)")
                                ins = nc.vector.bn_stats(fst[u][:, c, :], src)
                            link(ins)
                            spacer()
                            for c in range(2):
                                ins = nc.vector.bn_aggr(fmv[u][:, c, :], fst[u][:, c, :])
                            ins.then_inc(fmv_r[u], 1)
                        for u in range(2):
                            dve.wait_ge(frs_r[u], 2 * i + r + 1)
                            for c in range(2):
                                src = hid[u][:, c, :] if r else X[:, ds(4 * i + 2 * u + c, 1)].rearrange("p o d -> p (o d)")
                                ins = nc.vector.tensor_scalar((zt if r else hid)[u][:, c, :], src, fmv[u][:, c, 0:1],
                                                              frs[u][:, c:c + 1], ALU.subtract, ALU.mult)
                            ins.then_inc((zt_r if r else hid_r)[u], 1)
                    for u in range(2):
                        dve.wait_ge(FL_full[u], i + 1)
                        nc.vector.tensor_tensor(LG[:, ds(4 * i + 2 * u, 2), :], bank(2 + u, 2, E),
                                                rbb.unsqueeze(1).to_broadcast([P, 2, E]), ALU.add).then_inc(FL_cp[u], 1)
                    assert link.n == FCHAIN, link.n
                dve.wait_ge(FL_cp[1], B // 2 + 1)
                link = Chain(dve, f_ch, FCHAIN * (B // 2))
                iota = cst[:, C_IOTA:C_IOTA + E].unsqueeze(1).to_broadcast([P, T, E])

                def wide(a):
                    return a.unsqueeze(2).to_broadcast([P, T, E])

                src = LG
                for k, m in enumerate((M1, M2)):
                    link(nc.vector.tensor_reduce(out=m, in_=src, op=ALU.max, axis=AX))
                    link(nc.vector.tensor_tensor(EQ, src, wide(m), ALU.is_ge))
                    link(nc.vector.tensor_tensor(EQ, EQ, iota, ALU.mult))
                    link(nc.vector.tensor_reduce(out=IX, in_=EQ, op=ALU.min, axis=AX))
                    link(nc.vector.tensor_tensor(OH[k], iota, wide(IX), ALU.is_equal))
                    if k == 0:
                        link(nc.vector.tensor_scalar(LG2, OH[0], -3.0e38, None, ALU.mult))
                        link(nc.vector.tensor_tensor(LG2, LG2, LG, ALU.add))
                        src = LG2
                nc.vector.tensor_tensor(M2, M2, M1, ALU.subtract).then_inc(f_df, 1)
                dve.wait_ge(f_ex, 1)
                link(nc.vector.tensor_scalar(PR, M2, 1.0, None, ALU.add))
                link(nc.vector.reciprocal(PR, PR))
                link(nc.vector.tensor_tensor(M2, M2, PR, ALU.mult))
                link(nc.vector.tensor_tensor(OH[0], OH[0], wide(PR), ALU.mult))
                link(nc.vector.tensor_tensor(OH[1], OH[1], wide(M2), ALU.mult))
                nc.vector.tensor_tensor(comb, OH[0], OH[1], ALU.add).then_inc(f_cb, 1)
                dve.wait_ge(f_bb, 1)
                for t in range(0, T, 2):
                    nc.vector.tensor_tensor(X[:, t:t + 2, :], bank(t // 2, 2, D), X[:, t:t + 2, :], ALU.add)

        next_phase()

        TG = 512
        NTG = B * S // TG
        NI = I // P
        cg = Carve(U, U_W)
        ck = Carve(KH, (NBLK - 2) * HX * B)
        w1s = [cg(KC, I) for _ in range(2)]
        w2s = [cg(NI, D) for _ in range(2)]
        hT = [cg(KC, TG) for _ in range(2)]
        b1s = [cg(NI) for _ in range(2)]
        gs = [cg(KC) for _ in range(2)]
        bs = [cg(KC) for _ in range(2)]
        gel = [ck(NI, TG) for _ in range(2)]
        w_r, w_use = sems("w_r"), sems("w_use")
        hT_r, g1_d, g2_d = sems("hT_r"), sems("g1_d"), sems("g2_d")
        I_full, I_cp, Y_full, Y_cp = sems("I_full", 4), sems("I_cp", 4), sems("Y_full", 4), sems("Y_cp", 4)
        with nc.Block() as block:
            @block.sync
            def _(sp):
                prime(sp, w_use, g1_d, g2_d, I_cp, Y_cp)
                with sp.Fori(0, E // 2) as i:
                    for u in range(2):
                        sp.wait_ge(w_use[u], i + 1)
                        sp.sem_inc(sp_on, 1)
                        e = ds(2 * i + u, 1)
                        for dst, src in ((w1s[u], w1_d[e].rearrange("o (k p) n -> p (o k) n", p=P)),
                                         (w2s[u], w2_d[e].rearrange("o (k p) n -> p (o k) n", p=P)),
                                         (b1s[u], b1_d[e].rearrange("o p n -> p (o n)")),
                                         (gs[u], lg_d[e].rearrange("o p n -> p (o n)")),
                                         (bs[u], lb_d[e].rearrange("o p n -> p (o n)"))):
                            sp.dma_start(dst, src).then_inc(w_r[u], 16)

            @block.vector
            def _(dve):
                with dve.Fori(0, E // 2) as i:
                    def hidden(u, g):
                        s, n = g % 2, 4 * i + 2 * u + g // 2
                        if g == 0:
                            dve.wait_ge(w_r[u], 80 * i + 80)
                        dve.wait_ge(g1_d[s], n + 1)
                        for k in range(KC):
                            ins = nc.vector.tensor_scalar(hT[s][:, k, :], ZT[:, k, g * TG:(g + 1) * TG],
                                                          gs[u][:, k:k + 1], bs[u][:, k:k + 1], ALU.mult, ALU.add)
                        ins.then_inc(hT_r[s], 1)

                    def add(u, g):
                        for t in range(4):
                            dve.wait_ge(Y_full[t], 8 * i + 4 * u + g + 1)
                            xt = X[:, 4 * g + t, :]
                            nc.vector.scalar_tensor_tensor(xt, bank(4 + t, D), comb[:, 4 * g + t, ds(2 * i + u, 1)], xt,
                                                           ALU.mult, ALU.add).then_inc(Y_cp[t], 1)

                    for u in range(2):
                        hidden(u, 0)
                        hidden(u, 1)
                        for g in range(NTG):
                            add(u, g)
                            if g + 2 < NTG:
                                hidden(u, g + 2)

            @block.scalar
            def _(act):
                with act.Fori(0, E // 2) as i:
                    for u in range(2):
                        for g in range(NTG):
                            act.wait_ge(g2_d[g % 2], 4 * i + 2 * u + g // 2 + 1)
                            for n in range(NI):
                                act.wait_ge(I_full[n % 4], 16 * i + 8 * u + 2 * g + n // 4 + 1)
                                nc.scalar.activation(gel[g % 2][:, n, :], bank(n % 4, TG), ACT.Gelu,
                                                     bias=b1s[u][:, n:n + 1]).then_inc(I_cp[n % 4], 1)

            @block.tensor
            def _(pe):
                with pe.Fori(0, E // 2) as i:
                    def up(u, g):
                        pe.wait_ge(hT_r[g % 2], 4 * i + 2 * u + g // 2 + 1)
                        for n in range(NI):
                            pe.wait_ge(I_cp[n % 4], 16 * i + 8 * u + 2 * g + n // 4 + 1)
                            for k in range(KC):
                                mm = pe.matmul(bank(n % 4, TG), w1s[u][:, k, n * P:(n + 1) * P], hT[g % 2][:, k, :],
                                               start=(k == 0), stop=(k == KC - 1))
                            mm.then_inc(I_full[n % 4], 1)
                        pe.wait_ge(I_full[3], 16 * i + 8 * u + 2 * g + 2)
                        pe.sem_inc(g1_d[g % 2], 1)

                    def down(u, g):
                        for k in range(4):
                            pe.wait_ge(I_cp[k], 16 * i + 8 * u + 2 * g + 2 + 1)
                        for t in range(4):
                            pe.wait_ge(Y_cp[t], 8 * i + 4 * u + g + 1)
                            for n in range(NI):
                                mm = pe.matmul(bank(4 + t, D), gel[g % 2][:, n, t * P:(t + 1) * P], w2s[u][:, n, :],
                                               start=(n == 0), stop=(n == NI - 1))
                            mm.then_inc(Y_full[t], 1)
                        pe.wait_ge(Y_full[3], 8 * i + 4 * u + g + 1)
                        pe.sem_inc(g2_d[g % 2], 1)
                        if g == NTG - 1:
                            pe.sem_inc(w_use[u], 1)

                    for u in range(2):
                        up(u, 0)
                        for g in range(1, NTG):
                            up(u, g)
                            down(u, g - 1)
                        down(u, NTG - 1)

        ld_out = sem("ld_out")
        with nc.Block() as block:
            @block.sync
            def _(sp):
                sp.dma_start(out_d.rearrange("b (c p) d -> p (b c) d", p=P), X[:, :, :]).then_inc(ld_out, 16)
                sp.wait_ge(ld_out, 16)


def kernel(**inputs):
    import concourse.bacc as bacc
    from concourse.bass_utils import run_bass_kernel_spmd

    v = {k: np.asarray(a) for k, a in inputs.items()}
    wg = np.concatenate([v["L0_xattn_igate_w"], v["L0_xattn_fgate_w"]], 0).T
    arrays = {
        "x": v["x"], "ctx": v["ctx_1024"], "ctxr": v["ctx_1024"][:, :P - 1:-1],
        "idx": hop_layout(v["itok_SxS2_0_2016"]), "cst": constants(),
        "wqT": v["L0_attn_Wq"].T, "wkT": v["L0_attn_Wk"].T, "wvT": v["L0_attn_Wv"].T, "woT": v["L0_attn_Wo"].T,
        "wk": v["L0_attn_Wk"], "gw": np.tile(v["L0_attn_gw"].reshape(DA, 1), (HC, 1)),
        "sw": np.tile(v["L0_attn_sw"].reshape(DA, 1), (HC, 1)), "wg": wg,
        "gb": np.concatenate([v["L0_xattn_igate_b"], v["L0_xattn_fgate_b"]]), "rpe": v["L0_xattn_rpe"],
        "lnw": v["L0_xattn_ln_w"], "lnb": v["L0_xattn_ln_b"],
        "rng": v["L0_ffn_rn_g"].reshape(KC, P).T, "rnb": v["L0_ffn_rn_b"].reshape(KC, P).T,
        "rw": v["L0_ffn_router_w"].T, "rb": v["L0_ffn_router_b"],
        "lg": v["L0_ffn_ln_g"].reshape(E, KC, P).transpose(0, 2, 1),
        "lb": v["L0_ffn_ln_b"].reshape(E, KC, P).transpose(0, 2, 1),
        "w1": v["L0_ffn_w1"], "b1": v["L0_ffn_b1"].reshape(E, I // P, P).transpose(0, 2, 1),
        "w2": v["L0_ffn_w2"], "b2": v["L0_ffn_b2"],
    }
    arrays = {f"in_{k}": np.ascontiguousarray(a) for k, a in arrays.items()}
    nc = bacc.Bacc("TRN2", target_bir_lowering=False, num_devices=1)
    args = [nc.dram_tensor(k, a.shape, mybir.dt.from_np(a.dtype), kind="ExternalInput").ap() for k, a in arrays.items()]
    out = nc.dram_tensor("out", (B, S, D), F32, kind="ExternalOutput").ap()
    build(nc, *args, out)
    return run_bass_kernel_spmd(nc, [arrays], core_ids=[0]).results[0]["out"]
```

```python
from contextlib import ExitStack

import numpy as np

import concourse.bass as bass
from concourse import mybir
from concourse.bass import ds

F32 = mybir.dt.float32
I32 = mybir.dt.int32
ALU = mybir.AluOpType
ACT = mybir.ActivationFunctionType
AX = mybir.AxisListType.X

P = 128
B, S, D = 8, 256, 256
T = B * S // P
HA, DA = 16, 16
HX, DX = 8, 32
E, I = 8, 1024
KC = D // P
HC = HA // KC
XC = HX // KC
LN_EPS = 1e-5
MLSTM_EPS = 1e-6

C_ID, C_TRI, C_TRIREV, C_ONE, C_BLK = 0, 128, 256, 384, 512
C_HM16, C_HM32, C_IOTA = 640, 648, 652
C_TOK, C_CNT, C_TILE, C_RESET, C_PAD, C_W = 660, 676, 692, 732, 860, 869

NT = 2 * B * S // P + E * (P - 1) // P
ROW = D + 1 + E

NBLK = 257
GRP = 8
NPRE = 64
NRING = 24
NFIRST = 6
NMIX = P // GRP
U_W = 17400
NGS = (NPRE + NRING) // GRP


def constants():
    c = np.zeros((P, C_W), np.float32)
    p = np.arange(P)
    c[:, C_ID:C_ID + P] = np.eye(P)
    c[:, C_TRI:C_TRI + P] = p[:, None] <= p[None, :]
    c[:, C_TRIREV:C_TRIREV + P] = p[:, None] >= P - 1 - p[None, :]
    c[:, C_ONE:C_ONE + P] = 1.0
    c[:, C_BLK:C_BLK + P] = p[:, None] // DA == p[None, :] // DA
    c[:, C_HM16:C_HM16 + HC] = p[:, None] // DA == np.arange(HC)[None, :]
    c[:, C_HM32:C_HM32 + XC] = p[:, None] // DX == np.arange(XC)[None, :]
    c[:, C_IOTA:C_IOTA + E] = np.arange(E)[None, :] - E
    c[:, C_TOK:C_TOK + T] = p[:, None] + P * np.arange(T)[None, :]
    c[:, C_CNT:C_CNT + T] = P * np.arange(T)[None, :]
    c[:, C_TILE:C_TILE + NT] = np.arange(NT)[None, :]
    c[:, C_RESET:C_RESET + E * T] = np.arange(E * T)[None, :] % T != 0
    c[:, C_PAD] = B * S + p
    return c


def hop_layout(hops):
    h = np.asarray(hops)
    idx = np.empty((P, NBLK), np.int32)
    idx[:, 0] = h[S - 1, S - 1:P - 1:-1]
    for n in range(1, P):
        idx[:n, n] = h[n - 1, :n]
        idx[n:, n] = h[S - 1 - n, S - 1 - np.arange(n, P)]
    idx[:, P] = h[P - 1, :P]
    idx[:, P + 1:] = h[P:, :P].T
    return idx


class Chain:

    def __init__(self, eng, sem, base=0):
        self.eng, self.sem, self.n, self.base = eng, sem, 0, base

    def __call__(self, ins):
        self.n += 1
        ins.then_inc(self.sem, 1)
        self.eng.wait_ge(self.sem, self.base + self.n)


def build(nc, x_d, ctx_d, ctxr_d, idx_d, cst_d, wqT_d, wkT_d, wvT_d, woT_d, wk_d, gw_d, sw_d, wg_d, gb_d,
          rpe_d, lnw_d, lnb_d, rng_d, rnb_d, rw_d, rb_d, lg_d, lb_d, w1_d, b1_d, w2_d, b2_d, out_d):
    ctx = ExitStack()
    with ctx:
        phase = ExitStack()
        held = []

        def sem(name):
            h = phase.enter_context(nc.semaphore(name))
            held.append(h)
            return h

        def prime(sp, *groups):
            for g in groups:
                for h in g:
                    sp.sem_inc(h, 1)

        def next_phase():
            with nc.Block() as block:
                @block.sync
                def _(sp):
                    for h in held:
                        sp.sem_clear(h)
            held.clear()
            phase.close()

        def sems(name, n=2):
            return [sem(f"{name}{k}") for k in range(n)]

        def sb(name, shape, dt=F32):
            return ctx.enter_context(nc.sbuf_tensor(name, shape, dt))

        cst = sb("cst", [P, C_W])
        ident = cst[:, C_ID:C_ID + P]
        tri = cst[:, C_TRI:C_TRI + P]
        trirev = cst[:, C_TRIREV:C_TRIREV + P]
        ones = cst[:, C_ONE:C_ONE + P]
        blkm = cst[:, C_BLK:C_BLK + P]
        hm16 = cst[:, C_HM16:C_HM16 + HC]
        hm32 = cst[:, C_HM32:C_HM32 + XC]
        X = sb("X", [P, T, D])
        QT = sb("QT", [P, KC, B, S])
        KH = sb("KH", [P, (NBLK + 1) * HX * B])
        RING = sb("RING", [P, NRING * D])
        U = sb("U", [P, U_W])
        eps_ap = sb("eps", [P, 1])
        pad_v = sb("pad_v", [P, 8])
        PET = sb("PET", [P, 3, 512])
        GT = sb("GT", [P, 2, 2, HX, B])
        hopi = sb("hopi", [P, NBLK], I32)
        EX = sb("EX", [P, 2, HX * B])
        AT = sb("AT", [P, 2, HX * B])

        psum = [ctx.enter_context(nc.psum_tensor(f"ps{k}", [P, 512], F32)) for k in range(8)]
        slots = sb("slots", [P, 2 * T], I32)
        tile_e = sb("tile_e", [P, NT], I32)
        negm_dram = nc.dram_tensor("negm", [HX * B, S], F32).ap()
        rows_dram = nc.dram_tensor("slot_rows", [NT * P, ROW], F32).ap()

        class Carve:
            def __init__(self, t, size):
                self.t, self.at, self.size = t, 0, size

            def __call__(self, *shape):
                n = int(np.prod(shape))
                a = self.t[:, self.at:self.at + n]
                self.at += n
                assert self.at <= self.size, (self.at, self.size)
                names = [f"d{k}" for k in range(len(shape))]
                if len(shape) == 1:
                    return a
                kw = {k: s for k, s in zip(names, shape)}
                return a.rearrange(f"p ({' '.join(names)}) -> p {' '.join(names)}", **kw)

        def bank(k, *shape):
            n = int(np.prod(shape))
            a = psum[k][:, 0:n]
            if len(shape) == 1:
                return a
            names = [f"d{j}" for j in range(len(shape))]
            return a.rearrange(f"p ({' '.join(names)}) -> p {' '.join(names)}", **dict(zip(names, shape)))

        cu = Carve(U, U_W)
        wqT, wkT, woT = cu(KC, D), cu(KC, D), cu(KC, D)
        wvx = cu(KC, D + 2 * HA)
        wg6 = cu(6, 2 * HX)
        gbias = cu(2 * HX)
        gwc, swc, swb = cu(1), cu(1), cu(HC)
        xn = [cu(2, D) for _ in range(2)]
        xnT = [cu(KC, S) for _ in range(2)]
        qT = [cu(KC, S) for _ in range(2)]
        kT = [cu(KC, S) for _ in range(2)]
        ktok = [cu(D) for _ in range(2)]
        vx = [cu(2, D + 2 * HA) for _ in range(2)]
        am = [cu(2, 4, P) for _ in range(2)]
        sm = [cu(KC, P) for _ in range(2)]
        qblk = [cu(2, HC, P) for _ in range(2)]
        cx = [cu(2, D) for _ in range(2)]
        st = [cu(2, 6) for _ in range(2)]
        mv = [cu(2, 2) for _ in range(2)]
        rstd = [cu(2) for _ in range(2)]
        eg = [cu(2, 2 * HA) for _ in range(2)]
        lgg = [cu(2, HA) for _ in range(2)]
        gc = [cu(2, HA) for _ in range(2)]
        coef = [cu(2, HA) for _ in range(2)]
        wkN = qblk[0][:, 0, 0:4, :].rearrange("p a (b c) -> p (a b c)", b=1).rearrange("p (k n) -> p k n", k=KC)

        sp_on = ctx.enter_context(nc.semaphore("sp_on"))
        gat = [ctx.enter_context(nc.semaphore(f"gathered{k}")) for k in range(NGS)]
        ld_idx, ld_cst, ld_x, ld_w = sem("ld_idx"), sem("ld_cst"), sem("ld_x"), sem("ld_w")
        w_ready, w_full = sem("w_ready"), sem("w_full")
        ch_v, ch_a = sem("ch_v"), sem("ch_a")
        mv_r, rstd_r, xn_r = sems("mv_r"), sems("rstd_r"), sems("xn_r")
        mv2_r, rstd2_r, q_r = sems("mv2_r"), sems("rstd2_r"), sems("q_r")
        eg_r, g_r, lg_r, gc_r, vp_r = sems("eg_r"), sems("g_r"), sems("lg_r"), sems("gc_r"), sems("vp_r")
        qb_r, av_d, att_r, cx_r = sems("qb_r"), sems("av_d"), sems("att_r"), sems("cx_r")
        T_full, T_cp, P_full, P_cp = sems("T_full"), sems("T_cp"), sems("P_full"), sems("P_cp")
        S_full, S_cp = sems("S_full"), sems("S_cp")
        TU, PU, SU = 4, 9, 8
        T_XN, T_ATT, T_Q, T_CX = range(TU)
        P_QT, P_KT, P_V0, P_V1, P_KTOK, P_CUM, P_STATE, P_OUT, P_GATE = range(PU)

        def rows_of(n):
            if n < NFIRST or NFIRST + NRING <= n < NPRE + NRING:
                k = n if n < NFIRST else n - NRING
                return KH[:, k * D:(k + 1) * D]
            k = (n - NFIRST if n < NPRE else n - NPRE - NRING) % NRING
            return RING[:, k * D:(k + 1) * D]

        def gather(pool, n):
            dst = rows_of(n)
            pool.indirect_dma_start(out=dst, out_offset=None, in_=rpe_d,
                                    in_offset=bass.IndirectOffsetOnAxis(ap=hopi[:, n:n + 1], axis=0)) \
                .then_inc(gat[n // GRP % NGS], 16)

        with nc.Block() as block:
            @block.sync
            def _(sp):
                sp.dma_start(hopi[:, :], idx_d).then_inc(ld_idx, 16)
                prime(sp, T_cp, P_cp, S_cp, att_r)
                sp.dma_start(X[:, 0:2], x_d[0].rearrange("(c p) d -> p c d", p=P)).then_inc(ld_x, 16)
                sp.dma_start(cst[:, :], cst_d).then_inc(ld_cst, 16)
                for dst, src in ((wqT, wqT_d), (wkT, wkT_d), (wvx[:, :, 0:D], wvT_d), (woT, woT_d), (wkN, wk_d)):
                    sp.dma_start(dst, src.rearrange("(k p) n -> p k n", p=P)).then_inc(ld_w, 16)
                sp.dma_start(wg6, wg_d.rearrange("(k p) n -> p k n", p=P)).then_inc(ld_w, 16)
                sp.dma_start(gbias, gb_d.partition_broadcast(P)).then_inc(ld_w, 16)
                sp.dma_start(gwc, gw_d).then_inc(ld_w, 16)
                sp.dma_start(swc, sw_d).then_inc(ld_w, 16)
                sp.dma_start(X[:, 2:T], x_d[1:B].rearrange("b (c p) d -> p (b c) d", p=P)).then_inc(ld_x, 16)
                with sp.Fori(0, B // 2) as i:
                    for u in range(2):
                        sp.wait_ge(T_cp[u], TU * i + 1)
                        sp.sem_inc(sp_on, 1)
                        sp.dma_start(cx[u], ctx_d[ds(2 * i + u, 1)].rearrange("o (c p) d -> p (o c) d", p=P)) \
                            .then_inc(cx_r[u], 16)

            @block.gpsimd
            def _(pool):
                pool.wait_ge(ld_idx, 16)
                for n in range(NPRE + NRING):
                    gather(pool, n)

            @block.tensor
            def _(pe):
                pe.wait_ge(ld_w, 16 * 9)
                pe.wait_ge(ld_cst, 16)
                pe.wait_ge(w_ready, 1)
                for k in range(KC):
                    for o in range(KC):
                        mm = pe.matmul(bank(0, 512)[:, k * HA + o * HC:k * HA + (o + 1) * HC],
                                       wkN[:, o, k * P:(k + 1) * P], swb, start=True, stop=True)
                mm.then_inc(w_full, 1)
                pe.wait_ge(w_ready, 2)

                def turn(dst, src, last_sem):
                    for k in range(KC):
                        for c in range(2):
                            mm = pe.transpose(dst[:, k, c * P:(c + 1) * P], src[:, c, k * P:(k + 1) * P], ident)
                    mm.then_inc(last_sem, 1)

                with pe.Fori(0, B // 2) as i:
                    def t_xn(u):
                        pe.wait_ge(xn_r[u], i + 1)
                        pe.wait_ge(T_cp[u], TU * i + T_XN + 1)
                        turn(bank(4 * u, KC, S), xn[u], T_full[u])

                    def p_feat(u, w, use):
                        pe.wait_ge(T_cp[u], TU * i + T_XN + 1 + 1)
                        pe.wait_ge(P_cp[u], PU * i + use + 1)
                        o = bank(4 * u + 1, KC, S)
                        for j in range(KC):
                            for k in range(KC):
                                mm = pe.matmul(o[:, j, :], w[:, k, j * P:(j + 1) * P], xnT[u][:, k, :],
                                               start=(k == 0), stop=(k == KC - 1))
                        mm.then_inc(P_full[u], 1)

                    def p_tok(u, w, n, c, use):
                        pe.wait_ge(P_cp[u], PU * i + use + 1)
                        for k in range(KC):
                            mm = pe.matmul(bank(4 * u + 1, n), xnT[u][:, k, c * P:(c + 1) * P], w[:, k, 0:n],
                                           start=(k == 0), stop=(k == KC - 1))
                        mm.then_inc(P_full[u], 1)

                    def cum(u):
                        pe.wait_ge(lg_r[u], i + 1)
                        pe.wait_ge(P_cp[u], PU * i + P_CUM + 1)
                        o = bank(4 * u + 1, 2, HA)
                        pe.matmul(o[:, 0, :], tri, lgg[u][:, 0, :], start=True, stop=True)
                        pe.matmul(o[:, 1, :], ones, lgg[u][:, 0, :], start=True, stop=False)
                        pe.matmul(o[:, 1, :], tri, lgg[u][:, 1, :], start=False, stop=True).then_inc(P_full[u], 1)

                    def state(u):
                        pe.wait_ge(vp_r[u], i + 1)
                        pe.wait_ge(P_cp[u], PU * i + P_STATE + 1)
                        o = bank(4 * u + 1, KC, P)
                        for j in range(KC):
                            mm = pe.matmul(o[:, j, :], ktok[u][:, j * P:(j + 1) * P], vx[u][:, 0, j * P:(j + 1) * P],
                                           start=True, stop=True)
                        mm.then_inc(P_full[u], 1)

                    def score(u, n):
                        c, j, half = n // 4, n // 2 % 2, n % 2
                        pe.wait_ge(qb_r[u], 4 * i + n // 2 + 1)
                        if n == 0:
                            pe.wait_ge(P_cp[u], PU * i + P_KT + 1 + 1)
                        pe.wait_ge(S_cp[u], SU * i + n + 1)
                        pe.matmul(bank(4 * u + 2, 512), kT[u][:, j, c * P:(c + 1) * P],
                                  qblk[u][:, n // 2 % 2, half * 4:half * 4 + 4, :],
                                  start=True, stop=True).then_inc(S_full[u], 1)

                    def values(u, n):
                        c, j, half = n // 4, n // 2 % 2, n % 2
                        if n == 0:
                            pe.wait_ge(att_r[u], i + 1)
                        o = bank(4 * u + 3, 2, D)
                        if c == 1 and half == 0:
                            if j == 0:
                                pe.wait_ge(P_cp[u], PU * i + P_STATE + 1 + 1)
                            pe.matmul(o[:, 1, j * P:(j + 1) * P], qT[u][:, j, P:S], sm[u][:, j, :],
                                      start=True, stop=False, skip_group_check=True)
                        pe.wait_ge(S_cp[u], SU * i + n + 1 + 1)
                        for hh in range(4):
                            f = j * P + (half * 4 + hh) * DA
                            mm = pe.matmul(o[:, c, f:f + DA], am[u][:, n % 2, hh, :], vx[u][:, c, f:f + DA],
                                           start=(c == 0), stop=True, skip_group_check=True)
                        mm.then_inc(av_d[u], 1)

                    def t_att(u):
                        pe.wait_ge(att_r[u], i + 1 + 1)
                        pe.wait_ge(T_cp[u], TU * i + T_ATT + 1)
                        turn(bank(4 * u, KC, S), xn[u], T_full[u])

                    def p_out(u):
                        pe.wait_ge(T_cp[u], TU * i + T_ATT + 1 + 1)
                        pe.wait_ge(P_cp[u], PU * i + P_OUT + 1)
                        for c in range(2):
                            for k in range(KC):
                                mm = pe.matmul(bank(4 * u + 1, 2, D)[:, c, :], xnT[u][:, k, c * P:(c + 1) * P],
                                               woT[:, k, :], start=(k == 0), stop=(k == KC - 1))
                        mm.then_inc(P_full[u], 1)

                    def t_q(u):
                        pe.wait_ge(q_r[u], i + 1)
                        pe.wait_ge(T_cp[u], TU * i + T_Q + 1)
                        turn(bank(4 * u, KC, S), xn[u], T_full[u])

                    def t_cx(u):
                        pe.wait_ge(cx_r[u], 16 * i + 16)
                        pe.wait_ge(T_cp[u], TU * i + T_CX + 1)
                        turn(bank(4 * u, KC, S), cx[u], T_full[u])

                    def gates(u):
                        pe.wait_ge(T_cp[u], TU * i + T_CX + 1 + 1)
                        pe.wait_ge(P_cp[u], PU * i + P_GATE + 1)
                        o = bank(4 * u + 1, 2, 2 * HX)
                        for c in range(2):
                            for k in range(4):
                                src = qT[u] if k < 2 else kT[u]
                                mm = pe.matmul(o[:, c, :], src[:, k % 2, c * P:(c + 1) * P], wg6[:, k, :],
                                               start=(k == 0), stop=(k == 3))
                        mm.then_inc(P_full[u], 1)

                    def both(f, *a):
                        for u in range(2):
                            f(u, *a)

                    both(t_xn)
                    both(p_feat, wqT, P_QT)
                    both(p_feat, wkT, P_KT)
                    both(p_tok, wvx, D + 2 * HA, 0, P_V0)
                    both(p_tok, wvx, D + 2 * HA, 1, P_V1)
                    both(p_tok, wkT, D, 0, P_KTOK)
                    both(score, 0)
                    both(cum)
                    both(state)
                    for n in range(1, SU):
                        both(score, n)
                        both(values, n - 1)
                    both(values, SU - 1)
                    both(t_att)
                    both(p_out)
                    both(t_q)
                    both(t_cx)
                    both(gates)

            @block.scalar
            def _(act):
                act.preload_act_table_set("natural_log_exp_and_others")
                CHAIN = 4
                with act.Fori(0, B // 2) as i:
                    link = Chain(act, ch_a, i * CHAIN)

                    def rs(u, ready, done):
                        act.wait_ge(ready[u], i + 1)
                        link(nc.scalar.activation(rstd[u], mv[u][:, :, 1], ACT.Ln, bias=eps_ap[:, :]))
                        nc.scalar.activation(rstd[u], rstd[u], ACT.Exp, scale=-0.5).then_inc(done[u], 1)

                    def t_copy(u, dsts, use):
                        act.wait_ge(T_full[u], TU * i + use + 1)
                        for dst in dsts:
                            ins = nc.scalar.activation(dst, bank(4 * u, KC, S), ACT.Copy)
                        ins.then_inc(T_cp[u], 1)

                    def p_copy(u, dst, shape, use):
                        act.wait_ge(P_full[u], PU * i + use + 1)
                        nc.scalar.activation(dst, bank(4 * u + 1, *shape), ACT.Copy).then_inc(P_cp[u], 1)

                    for u in range(2):
                        rs(u, mv_r, rstd_r)
                    for u in range(2):
                        t_copy(u, [xnT[u]], T_XN)
                    for u in range(2):
                        p_copy(u, qT[u], (KC, S), P_QT)
                    for u in range(2):
                        p_copy(u, kT[u], (KC, S), P_KT)
                    for c in range(2):
                        for u in range(2):
                            p_copy(u, vx[u][:, c, :], (D + 2 * HA,), P_V0 + c)
                    for u in range(2):
                        act.wait_ge(P_cp[u], PU * i + P_V1 + 1 + 1)
                        nc.scalar.activation(eg[u], vx[u][:, :, D:D + 2 * HA], ACT.Exp, scale=-1.0).then_inc(eg_r[u], 1)
                    for u in range(2):
                        p_copy(u, ktok[u], (D,), P_KTOK)
                    for u in range(2):
                        act.wait_ge(g_r[u], i + 1)
                        nc.scalar.activation(lgg[u], coef[u], ACT.Ln).then_inc(lg_r[u], 1)
                    for u in range(2):
                        act.wait_ge(P_cp[u], PU * i + P_CUM + 1 + 1)
                        nc.scalar.activation(gc[u], gc[u], ACT.Exp).then_inc(gc_r[u], 1)
                    for u in range(2):
                        t_copy(u, [xnT[u]], T_ATT)
                    for u in range(2):
                        rs(u, mv2_r, rstd2_r)
                    for u in range(2):
                        t_copy(u, [QT[:, :, ds(2 * i + u, 1), :].squeeze(2), qT[u]], T_Q)
                    for u in range(2):
                        t_copy(u, [kT[u]], T_CX)
                    assert link.n == CHAIN

            @block.vector
            def _(dve):
                dve.wait_ge(ld_cst, 16)
                dve.wait_ge(ld_w, 16 * 9)
                nc.vector.memset(eps_ap[:, :], LN_EPS)
                nc.vector.memset(wvx[:, :, D:D + 2 * HA], 0.0).then_inc(ch_v, 1)
                nc.vector.tensor_scalar(swb, hm16, swc, None, ALU.mult).then_inc(w_ready, 1)
                nc.vector.tensor_tensor(wg6[:, 2:4, :], wg6[:, 2:4, :], wg6[:, 4:6, :], ALU.add)
                dve.wait_ge(ch_v, 1)
                for k in range(KC):
                    nc.vector.tensor_scalar(wvx[:, k, D + k * HC:D + (k + 1) * HC], hm16, gwc, None, ALU.mult)
                dve.wait_ge(w_full, 1)
                nc.vector.tensor_copy(wvx[:, :, D + HA:D + 2 * HA], bank(0, KC, HA)).then_inc(w_ready, 1)

                def spacer():
                    nc.vector.memset(pad_v[:, pads[0] % 8:pads[0] % 8 + 1], 0.0)
                    pads[0] += 1

                pads = [0]
                CHAIN = 16
                with dve.Fori(0, B // 2) as i:
                    link = Chain(dve, ch_v, 1 + i * CHAIN)

                    def stats(u, done):
                        t0 = 4 * i + 2 * u
                        spacer()
                        for c in range(2):
                            ins = nc.vector.bn_stats(st[u][:, c, :], X[:, ds(t0 + c, 1)].rearrange("p o d -> p (o d)"))
                        link(ins)
                        spacer()
                        for c in range(2):
                            ins = nc.vector.bn_aggr(mv[u][:, c, :], st[u][:, c, :])
                        ins.then_inc(done[u], 1)

                    def norm(u, ready, done):
                        dve.wait_ge(ready[u], i + 1)
                        t0 = 4 * i + 2 * u
                        for c in range(2):
                            ins = nc.vector.tensor_scalar(xn[u][:, c, :],
                                                          X[:, ds(t0 + c, 1)].rearrange("p o d -> p (o d)"),
                                                          mv[u][:, c, 0:1], rstd[u][:, c:c + 1],
                                                          ALU.subtract, ALU.mult)
                        ins.then_inc(done[u], 1)

                    dve.wait_ge(ld_x, 32)
                    for u in range(2):
                        stats(u, mv_r)
                    for u in range(2):
                        norm(u, rstd_r, xn_r)

                    def blocks(u, m):
                        c, j = m // 2, m % 2
                        if m == 0:
                            dve.wait_ge(P_cp[u], PU * i + P_QT + 1 + 1)
                        if m >= 2:
                            dve.wait_ge(S_full[u], SU * i + 2 * (m - 2) + 2)
                        q = qT[u][:, j, c * P:(c + 1) * P].unsqueeze(1).to_broadcast([P, HC, P])
                        nc.vector.tensor_tensor(qblk[u][:, m % 2], q, hm16.unsqueeze(2).to_broadcast([P, HC, P]),
                                                ALU.mult).then_inc(qb_r[u], 1)

                    for m in range(2):
                        for u in range(2):
                            blocks(u, m)
                    for u in range(2):
                        dve.wait_ge(eg_r[u], i + 1)
                        link(nc.vector.tensor_scalar(eg[u], eg[u], 1.0, None, ALU.add))
                        link(nc.vector.reciprocal(eg[u], eg[u]))
                        nc.vector.tensor_scalar(coef[u], eg[u][:, :, 0:HA], 1e-6, None, ALU.max).then_inc(g_r[u], 1)

                    def masked(u, n):
                        dve.wait_ge(S_full[u], SU * i + n + 1)
                        if n >= 2:
                            dve.wait_ge(av_d[u], SU * i + n - 1)
                        nc.vector.tensor_tensor(am[u][:, n % 2], bank(4 * u + 2, 4, P),
                                                tri.unsqueeze(1).to_broadcast([P, 4, P]), ALU.mult) \
                            .then_inc(S_cp[u], 1)

                    for u in range(2):
                        masked(u, 0)
                    for u in range(2):
                        dve.wait_ge(P_full[u], PU * i + P_CUM + 1)
                        ins = nc.vector.tensor_scalar(gc[u], bank(4 * u + 1, 2, HA), -30.0, 30.0, ALU.max, ALU.min)
                        ins.then_inc(P_cp[u], 1)
                        dve.wait_ge(lg_r[u], i + 1)
                        link(nc.vector.tensor_tensor(coef[u], vx[u][:, :, D + HA:D + 2 * HA], eg[u][:, :, HA:2 * HA],
                                                     ALU.mult))
                    for u in range(2):
                        dve.wait_ge(gc_r[u], i + 1)
                        link(nc.vector.tensor_scalar(gc[u], gc[u], 1e-6, None, ALU.add))
                        link(nc.vector.reciprocal(eg[u][:, :, 0:HA], gc[u]))
                        link(nc.vector.tensor_tensor(coef[u], coef[u], eg[u][:, :, 0:HA], ALU.mult))
                        for c in range(2):
                            v = vx[u][:, c, 0:D].rearrange("p (h e) -> p h e", h=HA)
                            ins = nc.vector.tensor_tensor(v, v, coef[u][:, c, :].unsqueeze(2).to_broadcast([P, HA, DA]),
                                                          ALU.mult)
                        ins.then_inc(vp_r[u], 1)
                    for n in range(1, SU):
                        if n in (2, 4):
                            for u in range(2):
                                blocks(u, n // 2 + 1)
                        for u in range(2):
                            masked(u, n)
                        if n == 1:
                            for u in range(2):
                                dve.wait_ge(P_full[u], PU * i + P_STATE + 1)
                                ins = nc.vector.tensor_tensor(sm[u], bank(4 * u + 1, KC, P),
                                                              blkm.unsqueeze(1).to_broadcast([P, KC, P]), ALU.mult)
                                ins.then_inc(P_cp[u], 1)
                    for u in range(2):
                        dve.wait_ge(av_d[u], SU * i + SU)
                        for c in range(2):
                            ins = nc.vector.tensor_tensor(xn[u][:, c, :].rearrange("p (h e) -> p h e", h=HA),
                                                          bank(4 * u + 3, 2, HA, DA)[:, c],
                                                          gc[u][:, c, :].unsqueeze(2).to_broadcast([P, HA, DA]),
                                                          ALU.mult)
                        ins.then_inc(att_r[u], 1)
                    for u in range(2):
                        dve.wait_ge(P_full[u], PU * i + P_OUT + 1)
                        xt = X[:, ds(4 * i + 2 * u, 2), :]
                        nc.vector.tensor_tensor(xt, bank(4 * u + 1, 2, D), xt, ALU.add).then_inc(P_cp[u], 1)
                        dve.wait_ge(P_cp[u], PU * i + P_OUT + 1 + 1)
                    for u in range(2):
                        stats(u, mv2_r)
                    for u in range(2):
                        norm(u, rstd2_r, q_r)
                    for u in range(2):
                        dve.wait_ge(P_full[u], PU * i + P_GATE + 1)
                        for c in range(2):
                            o = GT[:, c, :, :, ds(2 * i + u, 1)].rearrange("p g h o -> p (g h) o")
                            ins = nc.vector.tensor_tensor(o, bank(4 * u + 1, 2, 2 * HX)[:, c, :].unsqueeze(2),
                                                          gbias.unsqueeze(2), ALU.add)
                        ins.then_inc(P_cp[u], 1)
                    assert link.n == CHAIN, link.n

        next_phase()

        QBLK = U[:, 0:KC * XC * B * S].rearrange("p (j h b s) -> p j h b s", j=KC, h=XC, b=B)
        KHv = KH[:, :].rearrange("p (s h b) -> p s h b", h=HX, b=B)
        qblk_v, qblk_a, late_cp = sem("qblk_v"), sem("qblk_a"), sem("late_cp")
        turned, prod = sem("turned"), sem("prod")
        pet_r, kh_cp = sems("pet_r"), sems("kh_cp")
        NPAIR = (NBLK + 1) // 2
        NGRP = (NBLK + GRP - 1) // GRP

        def tiles(q):
            return range(2 * q, min(2 * q + 2, NBLK))

        def gathered(n):
            g = n // GRP
            return sum(16 * (min(NBLK, (k + 1) * GRP) - k * GRP) for k in range(g % NGS, g + 1, NGS))

        def turn_copy(copy, wait, q):
            wait(turned, q + 1)
            if q >= 3:
                wait(prod, q - 2)
            w = len(tiles(q)) * KC * P
            copy(PET[:, q % 3, 0:w], bank(q % 4, 512)[:, 0:w]).then_inc(pet_r[q % 2], 1)

        def mixed(g):
            return [bank(4 + 2 * (g % 2) + k, GRP // 2, HX * B, 2) for k in range(2)]

        def group_copy(copy, wait, g):
            n = min(NBLK, (g + 1) * GRP)
            wait(prod, (n + 1) // 2)
            w = (n - g * GRP) * HX * B
            if g >= NMIX:
                copy(KH[:, g * 512:g * 512 + w], bank(4 + 2 * (g % 2), 512)[:, 0:w]).then_inc(kh_cp[g % 2], 1)
                return
            out = KH[:, g * 512:(g + 1) * 512].rearrange("p (n x) -> p n x", n=GRP)
            for k in range(2):
                ins = copy(out[:, k * 4:k * 4 + 4], mixed(g)[k][:, :, :, 1])
            ins.then_inc(late_cp, 1)
            wait(late_cp, g + 1)
            for k in range(2):
                n0, n1 = max(1, g * GRP + 4 * k), g * GRP + 4 * k + 4
                w = n1 - n0
                ins = nc.vector.copy_predicated(out[:, 4 * k + 4 - w:4 * k + 4],
                                                tri.bitcast(I32)[:, n0 - 1:n1 - 1].unsqueeze(2).to_broadcast([P, w, HX * B]),
                                                mixed(g)[k][:, 4 - w:4, :, 0])
            ins.then_inc(kh_cp[g % 2], 1)

        def copies(copy, wait, e):
            for q in range(NPAIR + 4):
                if q < NPAIR and q % 2 == e:
                    turn_copy(copy, wait, q)
                g = (q - 6) // 4
                if q >= 6 and q % 4 == 2 and g < NGRP - 1 and (1 if g < NMIX else g % 2) == e:
                    group_copy(copy, wait, g)
            if (NGRP - 1) % 2 == e:
                group_copy(copy, wait, NGRP - 1)

        with nc.Block() as block:
            @block.gpsimd
            def _(pool):
                for n in range(NPRE + NRING, NBLK):
                    last = n - NRING if n >= NPRE + 2 * NRING else n - NPRE - NRING + NFIRST
                    pool.wait_ge(turned, last // 2 + 1)
                    gather(pool, n)

            @block.tensor
            def _(pe):
                def turn(q):
                    n0 = 2 * q
                    if n0 % GRP == 0:
                        pe.wait_ge(gat[n0 // GRP % NGS], gathered(n0))
                    if q >= 4:
                        pe.wait_ge(pet_r[q % 2], (q - 4) // 2 + 1)
                    o = bank(q % 4, 2, KC, P)
                    for n in tiles(q):
                        src = rows_of(n)
                        for j in range(KC):
                            mm = pe.transpose(o[:, n % 2, j, :], src[:, j * P:(j + 1) * P], ident)
                    mm.then_inc(turned, 1)

                def products(q):
                    pe.wait_ge(pet_r[q % 2], q // 2 + 1)
                    g = 2 * q // GRP
                    if 2 * q % GRP == 0 and g >= 2:
                        pe.wait_ge(kh_cp[g % 2], g // 2)
                    pet = PET[:, q % 3, :].rearrange("p (n j m) -> p n j m", n=2, j=KC)
                    for n in tiles(q):
                        for j in range(KC):
                            if g < NMIX:
                                o = mixed(g)[n % GRP // 4].rearrange("p n (j h b) s -> p n j h b s", j=KC, h=XC)[:, n % 4, j]
                                if n == 0:
                                    rhs = QBLK[:, j, :, :, S - 1:S].to_broadcast([P, XC, B, 2])
                                else:
                                    rhs = QBLK[:, j, :, :, n - 1:S - n + 1:S - 2 * n]
                            else:
                                o = bank(4 + 2 * (g % 2), GRP, KC, XC, B)[:, n % GRP, j]
                                rhs = QBLK[:, j, :, :, n - 1]
                            mm = pe.matmul(o, pet[:, n % 2, j, :], rhs, start=True, stop=True, skip_group_check=True)
                    mm.then_inc(prod, 1)

                for q in range(NPAIR + 2):
                    if q < NPAIR:
                        turn(q)
                    if q == 2:
                        pe.wait_ge(qblk_v, 1)
                        pe.wait_ge(qblk_a, 1)
                    if q >= 2:
                        products(q - 2)

            @block.scalar
            def _(act):
                for h in range(XC):
                    ins = nc.scalar.activation(QBLK[:, 1, h], QT[:, 1], ACT.Copy, scale=hm32[:, h:h + 1])
                ins.then_inc(qblk_a, 1)
                copies(lambda o, a: nc.scalar.activation(o, a, ACT.Copy), act.wait_ge, 0)

            @block.vector
            def _(dve):
                for h in range(XC):
                    ins = nc.vector.tensor_scalar(QBLK[:, 0, h], QT[:, 0], hm32[:, h:h + 1], None, ALU.mult)
                ins.then_inc(qblk_v, 1)
                copies(nc.vector.tensor_copy, dve.wait_ge, 1)

        next_phase()

        R = HX * B
        cr = Carve(RING, NRING * D)
        r_t, r_l, r_F, r_a, r_M, r_ml, r_rev, r_one = [cr(S)[0:R] for _ in range(8)]
        r_full, r_ch, r_ab, r_ln, r_nm, r_am = sem("r_full"), sem("r_ch"), sem("r_ab"), sem("r_ln"), sem("r_nm"), sem("r_am")
        r_tt, r_dma, r_ach = sem("r_tt"), sem("r_dma"), sem("r_ach")
        with nc.Block() as block:
            @block.tensor
            def _(pe):
                for g in range(2):
                    for c in range(2):
                        mm = pe.transpose(bank(0, 2, 2, P)[0:R, g, c, :], GT[:, c, g].rearrange("p h b -> p (h b)"), ident)
                mm.then_inc(r_full, 1)
                pe.wait_ge(r_am, 1)
                pe.transpose(bank(1, 2, R)[:, 0], r_a[:, 0:P], ident[0:R, 0:R])
                pe.transpose(bank(1, 2, R)[:, 1], r_rev[:, 0:P], ident[0:R, 0:R]).then_inc(r_tt, 1)
                pe.transpose(bank(2, 2, R)[:, 0], r_ml[:, 0:P], ident[0:R, 0:R])
                pe.transpose(bank(2, 2, R)[:, 1], r_ml[:, P:S], ident[0:R, 0:R]).then_inc(r_tt, 1)

            @block.scalar
            def _(act):
                act.wait_ge(r_full, 1)
                nc.scalar.activation(r_t, bank(0, 2, S)[0:R, 1, :], ACT.Abs).then_inc(r_ab, 1)
                act.wait_ge(r_ab, 1)
                nc.scalar.activation(r_l, r_t, ACT.Exp, scale=-1.0).then_inc(r_ach, 1)
                act.wait_ge(r_ach, 1)
                nc.scalar.activation(r_l, r_l, ACT.Ln, bias=ones[0:R, 0:1]).then_inc(r_ln, 1)
                act.wait_ge(r_tt, 2)
                nc.scalar.activation(EX[:, :, :], bank(2, 2, R), ACT.Exp, scale=-1.0)

            @block.vector
            def _(dve):
                link = Chain(dve, r_ch)
                ig, fg = bank(0, 2, S)[0:R, 0, :], bank(0, 2, S)[0:R, 1, :]
                nc.vector.memset(r_one, 1.0)
                dve.wait_ge(r_full, 1)
                dve.wait_ge(r_ln, 1)
                link(nc.vector.scalar_tensor_tensor(r_t, fg, 0.0, r_l, ALU.min, ALU.subtract))
                link(nc.vector.tensor_tensor_scan(r_F, r_one, r_t, 0.0, ALU.mult, ALU.add))
                link(nc.vector.tensor_tensor(r_a, ig, r_F, ALU.subtract))
                link(nc.vector.tensor_tensor_scan(r_M, r_a, r_a, -3.0e38, ALU.max, ALU.max))
                nc.vector.tensor_scalar(r_l, r_M, -1.0, None, ALU.mult).then_inc(r_nm, 1)
                nc.vector.tensor_tensor(r_ml, r_F, r_M, ALU.add)
                nc.vector.tensor_copy(r_rev[:, 0:P], r_a[:, S - 1:P - 1:-1]).then_inc(r_am, 1)
                dve.wait_ge(r_tt, 1)
                nc.vector.tensor_copy(AT[:, :, :], bank(1, 2, R))

            @block.sync
            def _(sp):
                sp.wait_ge(r_nm, 1)
                sp.dma_start(negm_dram, r_l).then_inc(r_dma, 16)
                sp.wait_ge(r_dma, 16)

        co = Carve(RING, NRING * D)
        cq = Carve(QT[:, :, :, :].rearrange("p j b s -> p (j b s)"), KC * B * S)
        cp = Carve(PET[:, :, :].rearrange("p a b -> p (a b)"), 3 * 512)
        NVX = DX + 1
        mx = [co(2, HX, DX) for _ in range(2)]
        mk = [co(KC, S) for _ in range(2)]
        nm = [co(XC, S) for _ in range(2)]
        Dm = [cq(XC, S + P) for _ in range(2)]
        tmp = [co(2, 512) for _ in range(2)]
        v1 = [cp(2, HX, NVX) for _ in range(2)]
        pst = [cq(2, HX) for _ in range(2)]
        hmu = [cq(2, HX) for _ in range(2)]
        lnwb = cp(D)
        lnbb = cq(D)
        m_ld, m_cst, m_fill = sem("m_ld"), sem("m_cst"), sem("m_fill")
        mx_r, nm_r, v1_r, mk_r = sems("mx_r"), sems("nm_r"), sems("v1_r"), sems("mk_r")
        A_full, B_full, A_cp, B_cp = sems("A_full"), sems("B_full"), sems("A_cp"), sems("B_cp")
        arg_r, ex_r, dec_r, c_r, pv_r = sems("arg_r"), sems("ex_r"), sems("dec_r"), sems("c_r"), sems("pv_r")
        h_cp, var_r, mrs_r, hn_r, x2_r = sems("h_cp"), sems("var_r"), sems("mrs_r"), sems("hn_r"), sems("x2_r")
        m_ch, m_ach = sem("m_ch"), sem("m_ach")
        AU, BU = 4, 3
        with nc.Block() as block:
            @block.sync
            def _(sp):
                prime(sp, A_full, v1_r, arg_r, h_cp, A_cp, B_cp, x2_r)
                sp.dma_start(rows_dram.rearrange("(n p) d -> p n d", p=P),
                             cst[:, C_W - ROW:C_W].unsqueeze(1).to_broadcast([P, NT, ROW])).then_inc(m_fill, 16)
                sp.dma_start(lnwb, lnw_d.partition_broadcast(P)).then_inc(m_ld, 16)
                sp.dma_start(lnbb, lnb_d.partition_broadcast(P)).then_inc(m_ld, 16)
                negm_v = negm_dram.rearrange("(h b) s -> b h s", b=B)
                with sp.Fori(0, B // 2) as i:
                    for u in range(2):
                        sp.wait_ge(A_full[u], AU * i + 1)
                        sp.sem_inc(sp_on, 1)
                        sp.wait_ge(v1_r[u], i + 1)
                        sp.sem_inc(sp_on, 1)
                        sp.dma_start(mx[u][:, 0].rearrange("p h d -> p (h d)"),
                                     ctx_d[ds(2 * i + u, 1), 0:P].rearrange("o p d -> p (o d)")).then_inc(mx_r[u], 16)
                        sp.dma_start(mx[u][:, 1].rearrange("p h d -> p (h d)"),
                                     ctxr_d[ds(2 * i + u, 1)].rearrange("o p d -> p (o d)")).then_inc(mx_r[u], 16)
                    for j in range(KC):
                        for u in range(2):
                            sp.wait_ge(arg_r[u], 2 * i + j + 1)
                            sp.sem_inc(sp_on, 1)
                            sp.dma_start(nm[u], negm_v[ds(2 * i + u, 1), j * XC:(j + 1) * XC].rearrange("o h s -> (o h) s")
                                         .partition_broadcast(P)).then_inc(nm_r[u], 16)
                sp.wait_ge(m_fill, 16)

            @block.gpsimd
            def _(pool):
                pool.wait_ge(m_ld, 32)
                nc.gpsimd.tensor_scalar(lnwb, lnwb, 1.0, None, ALU.add)
                for u in range(2):
                    ins = nc.gpsimd.memset(v1[u][:, :, :, DX:NVX], 1.0)
                ins.then_inc(m_cst, 1)
                pool.wait_ge(m_cst, 1)
                with pool.Fori(0, B // 2) as i:
                    for j in range(KC):
                        for u in range(2):
                            pool.wait_ge(ex_r[u], 2 * i + j + 1)
                            nc.gpsimd.tensor_tensor(Dm[u][:, :, 0:P], Dm[u][:, :, 0:P],
                                                    tri.unsqueeze(1).to_broadcast([P, XC, P]), ALU.mult)
                            nc.gpsimd.tensor_tensor(Dm[u][:, :, S:S + P], Dm[u][:, :, S:S + P],
                                                    trirev.unsqueeze(1).to_broadcast([P, XC, P]), ALU.mult) \
                                .then_inc(dec_r[u], 1)
                    for u in range(2):
                        pool.wait_ge(hn_r[u], i + 1)
                        h = tmp[u].rearrange("p a b -> p (a b)")[:, 0:2 * D].rearrange("p (c d) -> p c d", c=2)
                        nc.gpsimd.tensor_tensor(h, h, lnwb.unsqueeze(1).to_broadcast([P, 2, D]), ALU.mult).then_inc(x2_r[u], 1)
                        pool.wait_ge(x2_r[u], 3 * i + 1 + 1)
                        nc.gpsimd.tensor_tensor(h, h, lnbb.unsqueeze(1).to_broadcast([P, 2, D]), ALU.add).then_inc(x2_r[u], 1)
                        pool.wait_ge(x2_r[u], 3 * i + 2 + 1)
                        xt = X[:, ds(4 * i + 2 * u, 2), :]
                        nc.gpsimd.tensor_tensor(xt, xt, h, ALU.add).then_inc(x2_r[u], 1)

            @block.tensor
            def _(pe):
                with pe.Fori(0, B // 2) as i:
                    def keys(u):
                        pe.wait_ge(mx_r[u], 32 * i + 32)
                        pe.wait_ge(A_cp[u], AU * i + 1)
                        for k in range(KC):
                            for c in range(2):
                                mm = pe.transpose(bank(4 * u, KC, 2, P)[:, k, c, :],
                                                  mx[u][:, c].rearrange("p h d -> p (h d)")[:, k * P:(k + 1) * P], ident)
                        mm.then_inc(A_full[u], 1)

                    def score(u, m):
                        j, q, b = m // 3, m % 3, ds(2 * i + u, 1)
                        if m % 2 == 0:
                            pe.wait_ge(A_cp[u], AU * i + m // 2 + 1 + 1)
                        else:
                            pe.wait_ge(A_cp[u], AU * i + 1 + 1)
                            pe.wait_ge(B_cp[u], BU * i + m // 2 + 1)
                        o = bank(4 * u + m % 2, 512)
                        if q < 2:
                            rhs = QBLK[:, j, 2 * q:2 * q + 2, b, :].rearrange("p h o s -> p h (o s)")
                            lhs = mk[u][:, j, 0:P]
                        else:
                            rhs = QBLK[:, j, :, b, P:S].rearrange("p h o s -> p h (o s)")
                            lhs = mk[u][:, j, P:S]
                        pe.matmul(o, lhs, rhs, start=True, stop=True).then_inc((B_full if m % 2 else A_full)[u], 1)

                    def values(u, j):
                        pe.wait_ge(c_r[u], 6 * i + 3 * j + 3)
                        pe.wait_ge(v1_r[u], i + 1 + 1)
                        if j == 0:
                            pe.wait_ge(h_cp[u], i + 1)
                        for hh in range(XC):
                            h = j * XC + hh
                            for c in range(2):
                                o = bank(4 * u + 2 + c, HX, NVX)[:, h, :]
                                mm = pe.matmul(o, Dm[u][:, hh, c * P:(c + 1) * P], v1[u][:, 0, h, :],
                                               start=True, stop=(c == 0), skip_group_check=True)
                            mm = pe.matmul(o, Dm[u][:, hh, S:S + P], v1[u][:, 1, h, :],
                                           start=False, stop=True, skip_group_check=True)
                        mm.then_inc(pv_r[u], 1)

                    for u in range(2):
                        keys(u)
                    for m in range(6):
                        for u in range(2):
                            score(u, m)
                        if m == 3:
                            for u in range(2):
                                values(u, 0)
                    for u in range(2):
                        values(u, 1)

            @block.scalar
            def _(act):
                ACHAIN = 2
                with act.Fori(0, B // 2) as i:
                    link = Chain(act, m_ach, i * ACHAIN)
                    for u in range(2):
                        act.wait_ge(A_full[u], AU * i + 1 + 1)
                        nc.scalar.activation(mk[u], bank(4 * u, KC, S), ACT.Copy, scale=float(DX) ** -0.5) \
                            .then_inc(A_cp[u], 1)
                    for u in range(2):
                        act.wait_ge(h_cp[u], i + 1)
                        nc.scalar.activation(v1[u][:, :, :, 0:DX], mx[u], ACT.Copy).then_inc(v1_r[u], 1)
                    for j in range(KC):
                        for u in range(2):
                            act.wait_ge(arg_r[u], 2 * i + j + 1 + 1)
                            nc.scalar.activation(Dm[u], Dm[u], ACT.Exp).then_inc(ex_r[u], 1)
                    for u in range(2):
                        act.wait_ge(var_r[u], i + 1)
                        link(nc.scalar.activation(hmu[u], hmu[u], ACT.Ln, bias=eps_ap[:, :], scale=1.0 / DX))
                        nc.scalar.activation(hmu[u], hmu[u], ACT.Exp, scale=-0.5).then_inc(mrs_r[u], 1)

            @block.vector
            def _(dve):
                MCHAIN = 18
                with dve.Fori(0, B // 2) as i:
                    link = Chain(dve, m_ch, i * MCHAIN)

                    def args(u, j):
                        dve.wait_ge(nm_r[u], 32 * i + 16 * j + 16)
                        if j == 1:
                            dve.wait_ge(pv_r[u], 2 * i + 1)
                        for hh in range(XC):
                            hb = (j * XC + hh) * B
                            nc.vector.tensor_scalar(Dm[u][:, hh, 0:S], nm[u][:, hh, :], AT[:, 0, ds(hb + 2 * i + u, 1)],
                                                    0.0, ALU.add, ALU.min)
                            ins = nc.vector.tensor_scalar(Dm[u][:, hh, S:S + P], nm[u][:, hh, P:S],
                                                          AT[:, 1, ds(hb + 2 * i + u, 1)], 0.0, ALU.add, ALU.min)
                        ins.then_inc(arg_r[u], 1)

                    def weights(u, m):
                        j, q = m // 3, m % 3
                        b = ds(2 * i + u, 1)
                        cpd = (B_cp if m % 2 else A_cp)[u]
                        dve.wait_ge((B_full if m % 2 else A_full)[u], (BU if m % 2 else AU) * i + m // 2 + 3 - 2 * (m % 2))
                        if q < 2:
                            kh = KHv[:, 1:S + 1, j * XC + 2 * q:j * XC + 2 * q + 2, b].rearrange("p s h o -> p h (s o)")
                            n, w, d = 2, S, Dm[u][:, 2 * q:2 * q + 2, 0:S]
                        else:
                            kh = KHv[:, 0:P, j * XC:(j + 1) * XC, b].rearrange("p s h o -> p h (s o)")
                            n, w, d = XC, P, Dm[u][:, :, S:S + P]
                        if m == 0:
                            dve.wait_ge(x2_r[u], 3 * i + 1)
                        tt = tmp[u][:, m % 2, :].rearrange("p (h s) -> p h s", h=n)
                        sc = bank(4 * u + m % 2, n, w)
                        if q == 2:
                            nc.vector.tensor_tensor(tt[:, :, ::-1], sc[:, :, ::-1], kh, ALU.add).then_inc(cpd, 1)
                        else:
                            nc.vector.tensor_tensor(tt, sc, kh, ALU.add).then_inc(cpd, 1)
                        dve.wait_ge(cpd, (BU if m % 2 else AU) * i + m // 2 + 3 - m % 2)
                        if q == 0:
                            dve.wait_ge(dec_r[u], 2 * i + j + 1)
                        nc.vector.tensor_tensor(d, tt, d, ALU.mult).then_inc(c_r[u], 1)

                    def finish(u):
                        dve.wait_ge(pv_r[u], 2 * i + 2)
                        h = tmp[u].rearrange("p a b -> p (a b)")[:, 0:2 * D].rearrange("p (c h d) -> p c h d", c=2, h=HX)
                        exv = EX[:, :, :].rearrange("p c (h b) -> p c h b", b=B)[:, :, :, ds(2 * i + u, 1)].rearrange("p c h o -> p c (h o)")
                        for c in range(2):
                            ins = nc.vector.tensor_scalar(pst[u][:, c], bank(4 * u + 2 + c, HX, NVX)[:, :, DX], -1.0, None, ALU.mult)
                        link(ins)
                        for c in range(2):
                            ins = nc.vector.tensor_tensor(pst[u][:, c], bank(4 * u + 2 + c, HX, NVX)[:, :, DX], pst[u][:, c], ALU.max)
                        link(ins)
                        link(nc.vector.tensor_tensor(pst[u], pst[u], exv, ALU.max))
                        link(nc.vector.tensor_scalar(pst[u], pst[u], MLSTM_EPS, None, ALU.add))
                        link(nc.vector.reciprocal(pst[u], pst[u]))
                        for c in range(2):
                            ins = nc.vector.tensor_tensor(h[:, c], bank(4 * u + 2 + c, HX, NVX)[:, :, 0:DX],
                                                          pst[u][:, c].unsqueeze(2).to_broadcast([P, HX, DX]), ALU.mult)
                        ins.then_inc(h_cp[u], 1)
                        dve.wait_ge(h_cp[u], i + 1 + 1)
                        hf = h.rearrange("p c h d -> p (c h) d")
                        hmf, psf = hmu[u].rearrange("p c h -> p (c h)"), pst[u].rearrange("p c h -> p (c h)")
                        link(nc.vector.tensor_reduce(out=hmf, in_=hf, op=ALU.add, axis=AX))
                        link(nc.vector.tensor_scalar(hmf, hmf, 1.0 / DX, None, ALU.mult))
                        link(nc.vector.tensor_tensor(hf, hf, hmf.unsqueeze(2).to_broadcast([P, 2 * HX, DX]), ALU.subtract))
                        sq = tmp[u].rearrange("p a b -> p (a b)")[:, 2 * D:4 * D].rearrange("p (h d) -> p h d", d=DX)
                        link(nc.vector.tensor_tensor(sq, hf, hf, ALU.mult))
                        nc.vector.tensor_reduce(out=hmf, in_=sq, op=ALU.add, axis=AX).then_inc(var_r[u], 1)
                        dve.wait_ge(mrs_r[u], i + 1)
                        nc.vector.tensor_tensor(hf, hf, hmf.unsqueeze(2).to_broadcast([P, 2 * HX, DX]), ALU.mult) \
                            .then_inc(hn_r[u], 1)

                    for u in range(2):
                        args(u, 0)
                    for m in range(3):
                        for u in range(2):
                            weights(u, m)
                    for u in range(2):
                        args(u, 1)
                    for m in range(3, 6):
                        for u in range(2):
                            weights(u, m)
                    for u in range(2):
                        finish(u)
                    assert link.n == MCHAIN, link.n

        next_phase()

        cf = Carve(QT[:, :, :, :].rearrange("p j b s -> p (j b s)"), KC * B * S)
        cl = Carve(PET[:, :, :].rearrange("p a b -> p (a b)"), 3 * 512)
        cw = Carve(U, U_W)
        w1s = cw(E, KC, I)
        b1s, lgs, lbs = cw(E, I // P), cw(E, KC), cw(E, KC)
        w2s = KH[:, 0:E * (I // P) * D].rearrange("p (e n d) -> p e n d", e=E, n=I // P)
        ZR = RING[:, 0:T * ROW].rearrange("p (t w) -> p t w", w=ROW)
        combT = QT[:, 0, :, :].rearrange("p b s -> p (b s)")
        hid = [cf(2, D) for _ in range(2)]
        zt = [cf(2, D) for _ in range(2)]
        zs = [cf(KC, S) for _ in range(2)]
        fst = [cf(2, 6) for _ in range(2)]
        fmv = [cf(2, 2) for _ in range(2)]
        frs = [cf(2) for _ in range(2)]
        rwT, rwp, rnbb = cf(KC, E), cf(KC, E), cf(KC, P)
        rngc, rnbc, rbb = cf(KC), cf(KC), cf(E)
        over, open_, base = cf(E, T), cf(NT, E), cf(E)
        ntile, tile_end, tile_f, slot_f = cf(E), cf(E), cf(NT), cf(2 * T)
        LG, LG2, EQ = cl(T, E), cl(T, E), cl(T, E)
        OH = [cl(T, E) for _ in range(2)]
        picked, count, upto, slot_of = cl(T, E), cl(E, T), cl(E, T), cl(T, E)
        M1, M2, IX, PR = cl(T), cl(T), cl(T), cl(T)
        b2s = cl(D)
        comb = ZR[:, :, D + 1:ROW]
        f_ld, f_w, f_rb = sem("f_ld"), sem("f_w"), sem("f_rb")
        fmv_r, frs_r, hid_r, zt_r = sems("fmv_r"), sems("frs_r"), sems("hid_r"), sems("zt_r")
        FT_full, FT_cp, FL_full, FL_cp = sems("FT_full"), sems("FT_cp"), sems("FL_full"), sems("FL_cp")
        f_ch, f_ach, f_df, f_ex, f_cb = sem("f_ch"), sem("f_ach"), sem("f_df"), sem("f_ex"), sem("f_cb")
        f_ct, f_cc, f_bb, f_pk, f_ps, f_sl = sem("f_ct"), sem("f_cc"), sem("f_bb"), sem("f_pk"), sem("f_ps"), sem("f_sl")
        f_wt, f_sc, f_x, f_st = sem("f_wt"), sem("f_sc"), sem("f_x"), sem("f_st")
        with nc.Block() as block:
            @block.sync
            def _(sp):
                prime(sp, FT_cp, FL_cp)
                sp.dma_start(rwT, rw_d.rearrange("(k p) n -> p k n", p=P)).then_inc(f_ld, 16)
                sp.dma_start(rngc, rng_d).then_inc(f_ld, 16)
                sp.dma_start(rnbc, rnb_d).then_inc(f_ld, 16)
                sp.dma_start(rbb, rb_d.partition_broadcast(P)).then_inc(f_ld, 16)
                sp.dma_start(b2s[0:E], b2_d).then_inc(f_ld, 16)
                sp.dma_start(b1s, b1_d.rearrange("e p n -> p e n")).then_inc(f_wt, 16)
                sp.dma_start(lgs, lg_d.rearrange("e p n -> p e n")).then_inc(f_wt, 16)
                sp.dma_start(lbs, lb_d.rearrange("e p n -> p e n")).then_inc(f_wt, 16)
                for e in range(E):
                    sp.dma_start(w1s[:, e], w1_d[e].rearrange("(k p) n -> p k n", p=P)).then_inc(f_wt, 16)
                    sp.dma_start(w2s[:, e], w2_d[e].rearrange("(k p) n -> p k n", p=P)).then_inc(f_wt, 16)
                sp.wait_ge(f_x, 1)
                sp.dma_start(out_d[0:B * S].rearrange("(t p) d -> p t d", p=P), X[:, :, :]).then_inc(f_st, 16)
                sp.dma_start(out_d[B * S:B * S + P], X[:, 0]).then_inc(f_st, 16)
                sp.wait_ge(f_st, 32)
                sp.wait_ge(f_wt, 16 * (3 + 2 * E))

            @block.gpsimd
            def _(pool):
                pool.wait_ge(f_sl, 1)
                pool.wait_ge(f_cb, 1)
                pool.wait_ge(FT_cp[1], B // 2 + 1)
                for k in range(2 * T):
                    pool.indirect_dma_start(out=rows_dram, out_offset=bass.IndirectOffsetOnAxis(ap=slots[:, k:k + 1], axis=0),
                                            in_=ZR[:, k % T, :], in_offset=None).then_inc(f_sc, 16)
                pool.wait_ge(f_sc, 16 * 2 * T)

            @block.tensor
            def _(pe):
                pe.wait_ge(f_w, 1)
                for k in range(KC):
                    mm = pe.matmul(bank(7, E), rnbb[:, k, :], rwT[:, k, :], start=(k == 0), stop=(k == KC - 1))
                mm.then_inc(f_rb, 1)
                with pe.Fori(0, B // 2) as i:
                    for u in range(2):
                        pe.wait_ge(zt_r[u], i + 1)
                        pe.wait_ge(FT_cp[u], i + 1)
                        for k in range(KC):
                            for c in range(2):
                                mm = pe.transpose(bank(u, KC, 2, P)[:, k, c], zt[u][:, c, k * P:(k + 1) * P], ident)
                        mm.then_inc(FT_full[u], 1)
                    for u in range(2):
                        pe.wait_ge(FT_cp[u], i + 1 + 1)
                        pe.wait_ge(FL_cp[u], i + 1)
                        for c in range(2):
                            for k in range(KC):
                                mm = pe.matmul(bank(2 + u, 2, E)[:, c], zs[u][:, k, c * P:(c + 1) * P], rwp[:, k, :],
                                               start=(k == 0), stop=(k == KC - 1))
                        mm.then_inc(FL_full[u], 1)
                pe.wait_ge(f_pk, 1)
                pe.matmul(bank(0, T * E), tri, picked.rearrange("p t e -> p (t e)"), start=True, stop=True)
                pe.matmul(bank(1, T * E), ones, picked.rearrange("p t e -> p (t e)"), start=True, stop=True).then_inc(f_ps, 1)
                pe.wait_ge(f_cb, 1)
                for t in range(T):
                    mm = pe.transpose(bank(4 + t // 4, 4, P)[0:E, t % 4], comb[:, t, :], ident)
                mm.then_inc(f_ct, 1)
                pe.wait_ge(f_cc, 1)
                pe.wait_ge(f_sl, 1)
                for t in range(T):
                    mm = pe.matmul(bank(t // 2, 2, D)[:, t % 2], combT[0:E, t * P:(t + 1) * P], b2s[0:E],
                                   start=True, stop=True)
                mm.then_inc(f_bb, 1)

            @block.scalar
            def _(act):
                with act.Fori(0, B // 2) as i:
                    link = Chain(act, f_ach, 4 * i)
                    for r in range(2):
                        for u in range(2):
                            act.wait_ge(fmv_r[u], 2 * i + r + 1)
                            link(nc.scalar.activation(frs[u], fmv[u][:, :, 1], ACT.Ln, bias=eps_ap[:, :]))
                            nc.scalar.activation(frs[u], frs[u], ACT.Exp, scale=-0.5).then_inc(frs_r[u], 1)
                    for u in range(2):
                        act.wait_ge(FT_full[u], i + 1)
                        nc.scalar.activation(ZR[:, ds(4 * i + 2 * u, 2), 0:D], zt[u], ACT.Copy)
                        nc.scalar.activation(zs[u], bank(u, KC, S), ACT.Copy).then_inc(FT_cp[u], 1)
                act.wait_ge(f_df, 1)
                nc.scalar.activation(M2, M2, ACT.Exp).then_inc(f_ex, 1)
                act.wait_ge(f_ct, 1)
                for k in range(4):
                    ins = nc.scalar.activation(combT[0:E, k * 512:(k + 1) * 512], bank(4 + k, 512)[0:E], ACT.Copy)
                ins.then_inc(f_cc, 1)

            @block.vector
            def _(dve):
                pads = [0]

                def spacer():
                    nc.vector.memset(pad_v[:, pads[0] % 8:pads[0] % 8 + 1], 0.0)
                    pads[0] += 1

                nc.vector.tensor_copy(ZR[:, :, D], cst[:, C_TOK:C_TOK + T])
                dve.wait_ge(f_ld, 16 * 5)
                for k in range(KC):
                    nc.vector.tensor_scalar(rnbb[:, k, :], ones, rnbc[:, k:k + 1], None, ALU.mult)
                    ins = nc.vector.tensor_scalar(rwp[:, k, :], rwT[:, k, :], rngc[:, k:k + 1], None, ALU.mult)
                ins.then_inc(f_w, 1)
                dve.wait_ge(f_rb, 1)
                nc.vector.tensor_tensor(rbb, bank(7, E), rbb, ALU.add)
                FCHAIN = 4
                with dve.Fori(0, B // 2) as i:
                    link = Chain(dve, f_ch, FCHAIN * i)
                    for r in range(2):
                        for u in range(2):
                            if r == 1:
                                dve.wait_ge(hid_r[u], i + 1)
                            spacer()
                            for c in range(2):
                                src = hid[u][:, c, :] if r else X[:, ds(4 * i + 2 * u + c, 1)].rearrange("p o d -> p (o d)")
                                ins = nc.vector.bn_stats(fst[u][:, c, :], src)
                            link(ins)
                            spacer()
                            for c in range(2):
                                ins = nc.vector.bn_aggr(fmv[u][:, c, :], fst[u][:, c, :])
                            ins.then_inc(fmv_r[u], 1)
                        for u in range(2):
                            dve.wait_ge(frs_r[u], 2 * i + r + 1)
                            for c in range(2):
                                src = hid[u][:, c, :] if r else X[:, ds(4 * i + 2 * u + c, 1)].rearrange("p o d -> p (o d)")
                                ins = nc.vector.tensor_scalar((zt if r else hid)[u][:, c, :], src, fmv[u][:, c, 0:1],
                                                              frs[u][:, c:c + 1], ALU.subtract, ALU.mult)
                            ins.then_inc((zt_r if r else hid_r)[u], 1)
                    for u in range(2):
                        dve.wait_ge(FL_full[u], i + 1)
                        nc.vector.tensor_tensor(LG[:, ds(4 * i + 2 * u, 2), :], bank(2 + u, 2, E),
                                                rbb.unsqueeze(1).to_broadcast([P, 2, E]), ALU.add).then_inc(FL_cp[u], 1)
                    assert link.n == FCHAIN, link.n
                dve.wait_ge(FL_cp[1], B // 2 + 1)
                link = Chain(dve, f_ch, FCHAIN * (B // 2))
                iota = cst[:, C_IOTA:C_IOTA + E].unsqueeze(1).to_broadcast([P, T, E])

                def wide(a):
                    return a.unsqueeze(2).to_broadcast([P, T, E])

                src = LG
                for k, m in enumerate((M1, M2)):
                    link(nc.vector.tensor_reduce(out=m, in_=src, op=ALU.max, axis=AX))
                    link(nc.vector.tensor_tensor(EQ, src, wide(m), ALU.is_ge))
                    link(nc.vector.tensor_tensor(EQ, EQ, iota, ALU.mult))
                    link(nc.vector.tensor_reduce(out=IX, in_=EQ, op=ALU.min, axis=AX))
                    link(nc.vector.tensor_tensor(OH[k], iota, wide(IX), ALU.is_equal))
                    if k == 0:
                        link(nc.vector.tensor_scalar(LG2, OH[0], -3.0e38, None, ALU.mult))
                        link(nc.vector.tensor_tensor(LG2, LG2, LG, ALU.add))
                        src = LG2
                nc.vector.tensor_tensor(picked, OH[0], OH[1], ALU.add).then_inc(f_pk, 1)
                nc.vector.tensor_tensor(M2, M2, M1, ALU.subtract).then_inc(f_df, 1)
                dve.wait_ge(f_ps, 1)
                link(nc.vector.tensor_copy(count, bank(1, T, E).rearrange("p t e -> p e t")))
                link(nc.vector.tensor_tensor_scan(upto.rearrange("p e t -> p (e t)"), cst[:, C_RESET:C_RESET + E * T],
                                                  count.rearrange("p e t -> p (e t)"), 0.0, ALU.mult, ALU.add))
                link(nc.vector.tensor_tensor(over, upto[:, :, T - 1:T].to_broadcast([P, E, T]),
                                             cst[:, C_CNT:C_CNT + T].unsqueeze(1).to_broadcast([P, E, T]), ALU.is_gt))
                link(nc.vector.tensor_reduce(out=ntile, in_=over, op=ALU.add, axis=AX))
                link(nc.vector.tensor_tensor_scan(tile_end, ones[:, 0:E], ntile, 0.0, ALU.mult, ALU.add))
                link(nc.vector.tensor_tensor(open_, tile_end.unsqueeze(1).to_broadcast([P, NT, E]),
                                             cst[:, C_TILE:C_TILE + NT].unsqueeze(2).to_broadcast([P, NT, E]), ALU.is_le))
                link(nc.vector.tensor_reduce(out=tile_f, in_=open_, op=ALU.add, axis=AX))
                nc.vector.tensor_scalar(tile_e[:, :], tile_f, float(E - 1), None, ALU.min)
                link(nc.vector.tensor_tensor(base, tile_end, ntile, ALU.subtract))
                link(nc.vector.tensor_scalar(base, base, float(P), -1.0, ALU.mult, ALU.add))
                link(nc.vector.tensor_tensor(upto, upto, count, ALU.subtract))
                link(nc.vector.tensor_tensor(slot_of, upto.rearrange("p e t -> p t e"),
                                             base.unsqueeze(1).to_broadcast([P, T, E]), ALU.add))
                link(nc.vector.tensor_tensor(slot_of, bank(0, T, E), slot_of, ALU.add))
                for k in range(2):
                    link(nc.vector.tensor_tensor(EQ, OH[k], slot_of, ALU.mult))
                    link(nc.vector.tensor_reduce(out=slot_f[:, k * T:(k + 1) * T], in_=EQ, op=ALU.add, axis=AX))
                nc.vector.tensor_copy(slots[:, :], slot_f).then_inc(f_sl, 1)
                dve.wait_ge(f_ex, 1)
                link(nc.vector.tensor_scalar(PR, M2, 1.0, None, ALU.add))
                link(nc.vector.reciprocal(PR, PR))
                link(nc.vector.tensor_tensor(M2, M2, PR, ALU.mult))
                link(nc.vector.tensor_tensor(OH[0], OH[0], wide(PR), ALU.mult))
                link(nc.vector.tensor_tensor(OH[1], OH[1], wide(M2), ALU.mult))
                nc.vector.tensor_tensor(comb, OH[0], OH[1], ALU.add).then_inc(f_cb, 1)
                dve.wait_ge(f_bb, 1)
                for t in range(0, T, 2):
                    ins = nc.vector.tensor_tensor(X[:, t:t + 2, :], bank(t // 2, 2, D), X[:, t:t + 2, :], ALU.add)
                ins.then_inc(f_x, 1)

        next_phase()

        NI = I // P
        cg = Carve(RING, NRING * D)
        z_in = [cg(D) for _ in range(2)]
        meta = [cg(1 + E) for _ in range(2)]
        hT = [cg(KC, P) for _ in range(2)]
        w1c = [QT[:, u].rearrange("p b s -> p (b s)").rearrange("p (k n) -> p k n", k=KC) for u in range(2)]
        gel = [cg(NI, P) for _ in range(2)]
        ysb = [cg(D) for _ in range(2)]
        b1c = [cg(NI) for _ in range(2)]
        tok_f = cg(2)
        tok = slots[:, 0:2]
        Z_full, h_r, w1_v, w1_a, U_full, gel_r, Y_full, y_r, put = counters = [
            sem(n) for n in ("Z_full", "h_r", "w1_v", "w1_a", "U_full", "gel_r", "Y_full", "y_r", "put")]
        z_ld, meta_ld, scat = sems("z_ld"), sems("meta_ld"), sem("scat")
        pool_pad = cg(8)

        def done(m):
            return m + 3

        def each_tile(eng, step, ahead=0):
            pairs = (NT - 3) // 2
            with eng.Fori(0, pairs) as i:
                for u in range(2):
                    step(2 * i + u, u, i)
            for n in range(2 * pairs, NT):
                step(n, n % 2, n // 2)

        def live(n):
            return not isinstance(n, int) or n < NT

        def one(n):
            return ds(n, 1)

        with nc.Block() as block:
            @block.sync
            def _(sp):
                prime(sp, counters, counters)

                def load_z(n, u):
                    sp.dma_start(z_in[u], rows_dram[ds(n * P, P), 0:D]).then_inc(z_ld[u], 16)

                def load_meta(n, u):
                    sp.dma_start(meta[u], rows_dram[ds(n * P, P), D:ROW]).then_inc(meta_ld[u], 16)

                load_z(0, 0)
                load_z(1, 1)

                def step(n, u, i):
                    sp.wait_ge(y_r, done(n - 2))
                    sp.sem_inc(sp_on, 1)
                    load_meta(n, u)
                    if live(n + 2):
                        sp.wait_ge(Z_full, done(n))
                        sp.sem_inc(sp_on, 1)
                        load_z(n + 2, u)

                each_tile(sp, step)
                sp.wait_ge(scat, 16 * NT)

            @block.gpsimd
            def _(pool):
                def step(n, u, i):
                    pool.wait_ge(y_r, done(n))
                    nc.gpsimd.tensor_tensor(pool_pad[:, 2 * u:2 * u + 1], ones[:, 0:1], ones[:, 1:2], ALU.mult)
                    pool.indirect_dma_start(out=out_d, out_offset=bass.IndirectOffsetOnAxis(ap=tok[:, u:u + 1], axis=0),
                                            in_=ysb[u], in_offset=None, bounds_check=B * S + P - 1, oob_is_err=True,
                                            compute_op=ALU.add).then_inc(scat, 16)
                    pool.wait_ge(scat, 16 * (n + 1))
                    nc.gpsimd.tensor_tensor(pool_pad[:, 2 * u + 1:2 * u + 2], ones[:, 0:1], ones[:, 1:2], ALU.mult) \
                        .then_inc(put, 1)

                each_tile(pool, step)

            @block.tensor
            def _(pe):
                def turn_z(n, u, i):
                    pe.wait_ge(z_ld[u], 16 * (i + 1))
                    pe.wait_ge(h_r, done(n - 1))
                    for k in range(KC):
                        mm = pe.transpose(bank(0, 2, KC, P)[:, u, k], z_in[u][:, k * P:(k + 1) * P], ident)
                    mm.then_inc(Z_full, 1)

                def up(n, u, i):
                    pe.wait_ge(w1_v, done(n))
                    pe.wait_ge(w1_a, done(n))
                    pe.wait_ge(h_r, done(n))
                    pe.wait_ge(gel_r, done(n - 2))
                    for c in range(NI):
                        for k in range(KC):
                            mm = pe.matmul(bank(1 + 2 * u + c // 4, 4, P)[:, c % 4], w1c[u][:, k, c * P:(c + 1) * P],
                                           hT[u][:, k, :], start=(k == 0), stop=(k == KC - 1))
                    mm.then_inc(U_full, 1)

                def down(n, u, i):
                    e = pe.value_load(tile_e[0:1, one(n)], min_val=0, max_val=E - 1)
                    pe.wait_ge(gel_r, done(n))
                    pe.wait_ge(y_r, done(n - 1))
                    for c in range(NI):
                        mm = pe.matmul(bank(7, 2, D)[:, u], gel[u][:, c, :],
                                       w2s[:, one(e), c, :].rearrange("p o n -> p (o n)"),
                                       start=(c == 0), stop=(c == NI - 1))
                    mm.then_inc(Y_full, 1)

                turn_z(0, 0, 0)
                turn_z(1, 1, 0)
                up(0, 0, 0)

                def step(n, u, i):
                    if live(n + 1):
                        up(n + 1, 1 - u, i + u)
                    if live(n + 2):
                        turn_z(n + 2, u, i + 1)
                    down(n, u, i)

                each_tile(pe, step)

            @block.scalar
            def _(act):
                def weights(n, u, i):
                    e = act.value_load(tile_e[0:1, one(n)], min_val=0, max_val=E - 1)
                    act.wait_ge(U_full, done(n - 2))
                    nc.scalar.activation(w1c[u][:, 1], w1s[:, one(e), 1].rearrange("p o n -> p (o n)"), ACT.Copy) \
                        .then_inc(w1_a, 1)

                act.preload_act_table(ACT.Gelu)
                weights(0, 0, 0)
                weights(1, 1, 0)

                def step(n, u, i):
                    act.wait_ge(U_full, done(n))
                    act.wait_ge(Y_full, done(n - 2))
                    for c in range(NI):
                        ins = nc.scalar.activation(gel[u][:, c, :], bank(1 + 2 * u + c // 4, 4, P)[:, c % 4], ACT.Gelu,
                                                   bias=b1c[u][:, c:c + 1])
                    ins.then_inc(gel_r, 1)
                    if live(n + 2):
                        weights(n + 2, u, i + 1)

                each_tile(act, step)

            @block.vector
            def _(dve):
                def weights(n, u, i):
                    e = dve.value_load(tile_e[0:1, one(n)], min_val=0, max_val=E - 1)
                    dve.wait_ge(U_full, done(n - 2))
                    nc.vector.tensor_scalar(w1c[u][:, 0], w1s[:, one(e), 0].rearrange("p o n -> p (o n)"), 1.0, None,
                                            ALU.mult)
                    dve.wait_ge(gel_r, done(n - 2))
                    nc.vector.tensor_scalar(b1c[u], b1s[:, one(e), :].rearrange("p o n -> p (o n)"), 1.0, None,
                                            ALU.mult).then_inc(w1_v, 1)

                def hidden(n, u, i):
                    e = dve.value_load(tile_e[0:1, one(n)], min_val=0, max_val=E - 1)
                    dve.wait_ge(Z_full, done(n))
                    dve.wait_ge(U_full, done(n - 2))
                    for k in range(KC):
                        ins = nc.vector.tensor_scalar(hT[u][:, k, :], bank(0, 2, KC, P)[:, u, k],
                                                      lgs[:, one(e), k], lbs[:, one(e), k], ALU.mult, ALU.add)
                    ins.then_inc(h_r, 1)

                for n in range(2):
                    hidden(n, n, 0)
                    weights(n, n, 0)

                def step(n, u, i):
                    if live(n + 2):
                        weights(n + 2, u, i + 1)
                        hidden(n + 2, u, i + 1)
                    e = dve.value_load(tile_e[0:1, one(n)], min_val=0, max_val=E - 1)
                    dve.wait_ge(meta_ld[u], 16 * (i + 1))
                    dve.wait_ge(put, done(n - 1))
                    nc.vector.tensor_scalar(tok[:, u:u + 1], meta[u][:, 0:1], 0.0, None, ALU.add)
                    dve.wait_ge(Y_full, done(n))
                    nc.vector.tensor_scalar(ysb[u], bank(7, 2, D)[:, u], meta[u][:, ds(e + 1, 1)], None,
                                            ALU.mult).then_inc(y_r, 1)

                each_tile(dve, step)


def kernel(**inputs):
    import concourse.bacc as bacc
    from concourse.bass_utils import run_bass_kernel_spmd

    v = {k: np.asarray(a) for k, a in inputs.items()}
    wg = np.concatenate([v["L0_xattn_igate_w"], v["L0_xattn_fgate_w"]], 0).T
    arrays = {
        "x": v["x"], "ctx": v["ctx_1024"], "ctxr": v["ctx_1024"][:, :P - 1:-1],
        "idx": hop_layout(v["itok_SxS2_0_2016"]), "cst": constants(),
        "wqT": v["L0_attn_Wq"].T, "wkT": v["L0_attn_Wk"].T, "wvT": v["L0_attn_Wv"].T, "woT": v["L0_attn_Wo"].T,
        "wk": v["L0_attn_Wk"], "gw": np.tile(v["L0_attn_gw"].reshape(DA, 1), (HC, 1)),
        "sw": np.tile(v["L0_attn_sw"].reshape(DA, 1), (HC, 1)), "wg": wg,
        "gb": np.concatenate([v["L0_xattn_igate_b"], v["L0_xattn_fgate_b"]]), "rpe": v["L0_xattn_rpe"],
        "lnw": v["L0_xattn_ln_w"], "lnb": v["L0_xattn_ln_b"],
        "rng": v["L0_ffn_rn_g"].reshape(KC, P).T, "rnb": v["L0_ffn_rn_b"].reshape(KC, P).T,
        "rw": v["L0_ffn_router_w"].T, "rb": v["L0_ffn_router_b"],
        "lg": v["L0_ffn_ln_g"].reshape(E, KC, P).transpose(0, 2, 1),
        "lb": v["L0_ffn_ln_b"].reshape(E, KC, P).transpose(0, 2, 1),
        "w1": v["L0_ffn_w1"], "b1": v["L0_ffn_b1"].reshape(E, I // P, P).transpose(0, 2, 1),
        "w2": v["L0_ffn_w2"], "b2": v["L0_ffn_b2"],
    }
    arrays = {f"in_{k}": np.ascontiguousarray(a) for k, a in arrays.items()}
    nc = bacc.Bacc("TRN2", target_bir_lowering=False, num_devices=1)
    args = [nc.dram_tensor(k, a.shape, mybir.dt.from_np(a.dtype), kind="ExternalInput").ap() for k, a in arrays.items()]
    out = nc.dram_tensor("out", (B * S + P, D), F32, kind="ExternalOutput").ap()
    build(nc, *args, out)
    return run_bass_kernel_spmd(nc, [arrays], core_ids=[0]).results[0]["out"][0:B * S].reshape(B, S, D)
```

```python
from contextlib import ExitStack

import numpy as np

import concourse.bass as bass
from concourse import mybir
from concourse.bass import ds

F32 = mybir.dt.float32
I32 = mybir.dt.int32
ALU = mybir.AluOpType
ACT = mybir.ActivationFunctionType
AX = mybir.AxisListType.X

P = 128
B, S, D = 8, 256, 256
T = B * S // P
HA, DA = 16, 16
HX, DX = 8, 32
E, I = 8, 1024
KC = D // P
HC = HA // KC
XC = HX // KC
LN_EPS = 1e-5
MLSTM_EPS = 1e-6

C_ID, C_TRI, C_TRIREV, C_ONE, C_BLK = 0, 128, 256, 384, 512
C_HM16, C_HM32, C_IOTA = 640, 648, 652
C_TOK, C_CNT, C_TILE, C_RESET, C_PAD, C_W = 660, 676, 692, 732, 860, 869

NT = 2 * B * S // P + E * (P - 1) // P
ROW = D + 1 + E

NBLK = 257
GRP = 8
NPRE = 64
NRING = 24
NFIRST = 6
AGAIN = NPRE + 2 * NRING
NAGAIN = 34
NMIX = P // GRP
U_W = 17400
NGS = (NPRE + NRING) // GRP


def constants():
    c = np.zeros((P, C_W), np.float32)
    p = np.arange(P)
    c[:, C_ID:C_ID + P] = np.eye(P)
    c[:, C_TRI:C_TRI + P] = p[:, None] <= p[None, :]
    c[:, C_TRIREV:C_TRIREV + P] = p[:, None] >= P - 1 - p[None, :]
    c[:, C_ONE:C_ONE + P] = 1.0
    c[:, C_BLK:C_BLK + P] = p[:, None] // DA == p[None, :] // DA
    c[:, C_HM16:C_HM16 + HC] = p[:, None] // DA == np.arange(HC)[None, :]
    c[:, C_HM32:C_HM32 + XC] = p[:, None] // DX == np.arange(XC)[None, :]
    c[:, C_IOTA:C_IOTA + E] = np.arange(E)[None, :] - E
    c[:, C_TOK:C_TOK + T] = p[:, None] + P * np.arange(T)[None, :]
    c[:, C_CNT:C_CNT + T] = P * np.arange(T)[None, :]
    c[:, C_TILE:C_TILE + NT] = np.arange(NT)[None, :]
    c[:, C_RESET:C_RESET + E * T] = np.arange(E * T)[None, :] % T != 0
    c[:, C_PAD] = B * S + p
    return c


def hop_layout(hops):
    h = np.asarray(hops)
    idx = np.empty((P, NBLK), np.int32)
    idx[:, 0] = h[S - 1, S - 1:P - 1:-1]
    for n in range(1, P):
        idx[:n, n] = h[n - 1, :n]
        idx[n:, n] = h[S - 1 - n, S - 1 - np.arange(n, P)]
    idx[:, P] = h[P - 1, :P]
    idx[:, P + 1:] = h[P:, :P].T
    return idx


class Chain:

    def __init__(self, eng, sem, base=0):
        self.eng, self.sem, self.n, self.base = eng, sem, 0, base

    def __call__(self, ins):
        self.n += 1
        ins.then_inc(self.sem, 1)
        self.eng.wait_ge(self.sem, self.base + self.n)


def build(nc, x_d, ctx_d, ctxr_d, idx_d, cst_d, wqT_d, wkT_d, wvT_d, woT_d, wk_d, gw_d, sw_d, wg_d, gb_d,
          rpe_d, lnw_d, lnb_d, rng_d, rnb_d, rw_d, rb_d, lg_d, lb_d, w1_d, b1_d, w2_d, b2_d, out_d):
    ctx = ExitStack()
    with ctx:
        early, late = ExitStack(), ExitStack()
        done_with = []
        stage = [early]

        def sem(name):
            h = stage[0].enter_context(nc.semaphore(name))
            if stage[0] is early:
                done_with.append(h)
            return h

        def prime(sp, *groups):
            for g in groups:
                for h in g:
                    sp.sem_inc(h, 1)

        def retire(sp):
            for h in done_with:
                sp.sem_clear(h)

        def sems(name, n=2):
            return [sem(f"{name}{k}") for k in range(n)]

        def sb(name, shape, dt=F32):
            return ctx.enter_context(nc.sbuf_tensor(name, shape, dt))

        cst = sb("cst", [P, C_W])
        ident = cst[:, C_ID:C_ID + P]
        tri = cst[:, C_TRI:C_TRI + P]
        trirev = cst[:, C_TRIREV:C_TRIREV + P]
        ones = cst[:, C_ONE:C_ONE + P]
        blkm = cst[:, C_BLK:C_BLK + P]
        hm16 = cst[:, C_HM16:C_HM16 + HC]
        hm32 = cst[:, C_HM32:C_HM32 + XC]
        X = sb("X", [P, T, D])
        QT = sb("QT", [P, KC, B, S])
        KH = sb("KH", [P, (NBLK + 1) * HX * B])
        RING = sb("RING", [P, NRING * D])
        U = sb("U", [P, U_W])
        eps_ap = sb("eps", [P, 2])
        pad_v = sb("pad_v", [P, 8])
        PET = sb("PET", [P, 3, 512])
        GT = sb("GT", [P, 2, 2, HX, B])
        hopi = sb("hopi", [P, NBLK], I32)
        EX = sb("EX", [P, 2, HX * B])
        AT = sb("AT", [P, 2, HX * B])

        psum = [ctx.enter_context(nc.psum_tensor(f"ps{k}", [P, 512], F32)) for k in range(8)]
        slots = sb("slots", [P, 2 * T], I32)
        tile_e = sb("tile_e", [P, NT], I32)
        m_dram = nc.dram_tensor("run_max", [HX * B, S], F32).ap()
        rows_dram = nc.dram_tensor("slot_rows", [NT * P, ROW], F32).ap()

        class Carve:
            def __init__(self, t, size):
                self.t, self.at, self.size = t, 0, size

            def __call__(self, *shape):
                n = int(np.prod(shape))
                a = self.t[:, self.at:self.at + n]
                self.at += n
                assert self.at <= self.size, (self.at, self.size)
                names = [f"d{k}" for k in range(len(shape))]
                if len(shape) == 1:
                    return a
                kw = {k: s for k, s in zip(names, shape)}
                return a.rearrange(f"p ({' '.join(names)}) -> p {' '.join(names)}", **kw)

        def bank(k, *shape):
            n = int(np.prod(shape))
            a = psum[k][:, 0:n]
            if len(shape) == 1:
                return a
            names = [f"d{j}" for j in range(len(shape))]
            return a.rearrange(f"p ({' '.join(names)}) -> p {' '.join(names)}", **dict(zip(names, shape)))


        def passes(eng, step):
            with eng.Fori(0, B // 2 - 1) as i:
                step(i, False)
            step(B // 2 - 1, True)

        cu = Carve(U, U_W)
        ce = Carve(PET[:, :, :].rearrange("p a b -> p (a b)"), 3 * 512)
        wqT, wkT, woT = cu(KC, D), cu(KC, D), cu(KC, D)
        wvx = cu(KC, D + 2 * HA)
        wg6 = cu(6, 2 * HX)
        gbias = cu(2 * HX)
        gwc, swc, swb = cu(1), cu(1), cu(HC)
        lnbb = cu(D)
        xna = [ce(2, D) for _ in range(2)]
        xn = [cu(2, D) for _ in range(2)]
        xnT = [cu(KC, S) for _ in range(2)]
        qT = [cu(KC, S) for _ in range(2)]
        kT = [cu(KC, S) for _ in range(2)]
        ktok = [xn[u][:, 0, :] for u in range(2)]
        v2 = [[cu(HA, 2 * DA), cu(HA, 2 * DA)], [cu(HA, 2 * DA), ce(HA, 2 * DA)]]
        vx = [cu(2, D + 2 * HA) for _ in range(2)]
        am = [cu(2, 4, P) for _ in range(2)]
        sm = [cu(KC, P) for _ in range(2)]
        qblk = [cu(2, HC, P) for _ in range(2)]
        gcT = [qblk[u][:, 0, 0:4, :].rearrange("p a b -> p (a b)").rearrange("p (k s) -> p k s", k=KC)
               for u in range(2)]
        lgx = [qblk[u][:, 0, 4:8, :].rearrange("p a b -> p (a b)").rearrange("p (c h e) -> p c h e", c=2, e=DA)
               for u in range(2)]
        cx = [cu(2, D) for _ in range(2)]
        st = [cu(2, 6) for _ in range(2)]
        mv = [cu(2, 2) for _ in range(2)]
        rstd = [cu(2) for _ in range(2)]
        eg = [cu(2, 2 * HA) for _ in range(2)]
        lgg = [cu(2, HA) for _ in range(2)]
        gc = [cu(2, HA) for _ in range(2)]
        coef = [cu(2, HA) for _ in range(2)]
        wkN = qblk[0][:, 0, 0:4, :].rearrange("p a (b c) -> p (a b c)", b=1).rearrange("p (k n) -> p k n", k=KC)

        sp_on = ctx.enter_context(nc.semaphore("sp_on"))
        gat = [ctx.enter_context(nc.semaphore(f"gathered{k}")) for k in range(NGS)]
        ld_lnb = sem("ld_lnb")
        ld_idx, ld_cst, ld_x, ld_xr, ld_w = sem("ld_idx"), sem("ld_cst"), sem("ld_x"), sem("ld_xr"), sem("ld_w")
        w_ready, w_full = sem("w_ready"), sem("w_full")
        ch_v, ch_a = sem("ch_v"), sem("ch_a")
        mv_r, rstd_r, xn_r = sems("mv_r"), sems("rstd_r"), sems("xn_r")
        mv2_r, rstd2_r, q_r = sems("mv2_r"), sems("rstd2_r"), sems("q_r")
        eg_r, g_r, lg_r, gc_r, vp_r = sems("eg_r"), sems("g_r"), sems("lg_r"), sems("gc_r"), sems("vp_r")
        qb_r, av_d, att_r, cx_r, gct_r, lgx_r = sems("qb_r"), sems("av_d"), sems("att_r"), sems("cx_r"), sems("gct_r"), sems("lgx_r")
        T_full, T_cp, P_full, P_cp = sems("T_full"), sems("T_cp"), sems("P_full"), sems("P_cp")
        S_full, S_cp = sems("S_full"), sems("S_cp")
        TU, PU, SU = 3, 10, 8
        T_XN, T_CX, T_Q = range(TU)
        P_QT, P_KT, P_V0, P_V1, P_KTOK, P_CUM, P_STATE, P_GCT, P_OUT, P_GATE = range(PU)

        def rows_of(n):
            if n < NFIRST or NFIRST + NRING <= n < NPRE + NRING or AGAIN <= n < AGAIN + NAGAIN:
                k = n if n < NFIRST else n - NRING if n < AGAIN else n - AGAIN + NPRE - NAGAIN
                return KH[:, k * D:(k + 1) * D]
            k = (n - NFIRST if n < NPRE else n - NPRE - NRING if n < AGAIN else n - AGAIN - NAGAIN) % NRING
            return RING[:, k * D:(k + 1) * D]

        def rows_before(n):
            if n < AGAIN:
                return n - NPRE - NRING + NFIRST
            return n - NAGAIN - NRING if n < AGAIN + NAGAIN + NRING else n - NRING

        def packed(v):
            return v.rearrange("p (a s) e -> p a (s e)", s=2).rearrange("p a (s e) -> p a s e", e=DA)[:, :, 0:4:3, :]

        def gather(pool, n):
            dst = rows_of(n)
            pool.indirect_dma_start(out=dst, out_offset=None, in_=rpe_d,
                                    in_offset=bass.IndirectOffsetOnAxis(ap=hopi[:, n:n + 1], axis=0)) \
                .then_inc(gat[n // GRP % NGS], 16)

        with nc.Block() as block:
            @block.sync
            def _(sp):
                sp.dma_start(hopi[:, :], idx_d).then_inc(ld_idx, 16)
                prime(sp, T_cp, P_cp, S_cp, att_r)
                sp.dma_start(X[:, 0:4], x_d[0:2].rearrange("b (c p) d -> p (b c) d", p=P)).then_inc(ld_x, 16)
                sp.dma_start(cst[:, :], cst_d).then_inc(ld_cst, 16)
                for dst, src in ((wqT, wqT_d), (wkT, wkT_d), (wvx[:, :, 0:D], wvT_d), (woT, woT_d), (wkN, wk_d)):
                    sp.dma_start(dst, src.rearrange("(k p) n -> p k n", p=P)).then_inc(ld_w, 16)
                sp.dma_start(wg6, wg_d.rearrange("(k p) n -> p k n", p=P)).then_inc(ld_w, 16)
                sp.dma_start(gbias, gb_d.partition_broadcast(P)).then_inc(ld_w, 16)
                sp.dma_start(gwc, gw_d).then_inc(ld_w, 16)
                sp.dma_start(swc, sw_d).then_inc(ld_w, 16)
                sp.dma_start(lnbb, lnb_d.partition_broadcast(P)).then_inc(ld_lnb, 16)
                sp.dma_start(X[:, 4:T], x_d[2:B].rearrange("b (c p) d -> p (b c) d", p=P)).then_inc(ld_xr, 16)
                with sp.Fori(0, B // 2) as i:
                    for u in range(2):
                        sp.wait_ge(T_cp[u], TU * i + 1)
                        sp.sem_inc(sp_on, 1)
                        sp.dma_start(cx[u], ctx_d[ds(2 * i + u, 1)].rearrange("o (c p) d -> p (o c) d", p=P)) \
                            .then_inc(cx_r[u], 16)

            @block.gpsimd
            def _(pool):
                pool.wait_ge(ld_idx, 16)
                for n in range(NPRE + NRING):
                    gather(pool, n)
                pool.wait_ge(ld_lnb, 16)
                with pool.Fori(0, B // 2) as i:
                    for u in range(2):
                        pool.wait_ge(q_r[u], i + 1)
                        xt = X[:, ds(4 * i + 2 * u, 2), :]
                        nc.gpsimd.tensor_tensor(xt, xt, lnbb.unsqueeze(1).to_broadcast([P, 2, D]), ALU.add)

            @block.tensor
            def _(pe):
                pe.wait_ge(ld_w, 16 * 9)
                pe.wait_ge(ld_cst, 16)
                pe.wait_ge(w_ready, 1)
                for k in range(KC):
                    for o in range(KC):
                        mm = pe.matmul(bank(0, 512)[:, k * HA + o * HC:k * HA + (o + 1) * HC],
                                       wkN[:, o, k * P:(k + 1) * P], swb, start=True, stop=True)
                mm.then_inc(w_full, 1)
                pe.wait_ge(w_ready, 2)

                def turn(dst, src, last_sem):
                    for k in range(KC):
                        for c in range(2):
                            mm = pe.transpose(dst[:, k, c * P:(c + 1) * P], src[:, c, k * P:(k + 1) * P], ident)
                    mm.then_inc(last_sem, 1)

                with pe.Fori(0, B // 2) as i:
                    def t_xn(u):
                        pe.wait_ge(xn_r[u], i + 1)
                        pe.wait_ge(T_cp[u], TU * i + T_XN + 1)
                        turn(bank(4 * u, KC, S), xna[u], T_full[u])

                    def p_feat(u, w, use):
                        pe.wait_ge(T_cp[u], TU * i + T_XN + 1 + 1)
                        pe.wait_ge(P_cp[u], PU * i + use + 1)
                        o = bank(4 * u + 1, KC, S)
                        for j in range(KC):
                            for k in range(KC):
                                mm = pe.matmul(o[:, j, :], w[:, k, j * P:(j + 1) * P], xnT[u][:, k, :],
                                               start=(k == 0), stop=(k == KC - 1))
                        mm.then_inc(P_full[u], 1)

                    def p_tok(u, w, n, c, use):
                        pe.wait_ge(P_cp[u], PU * i + use + 1)
                        for k in range(KC):
                            mm = pe.matmul(bank(4 * u + 1, n), xnT[u][:, k, c * P:(c + 1) * P], w[:, k, 0:n],
                                           start=(k == 0), stop=(k == KC - 1))
                        mm.then_inc(P_full[u], 1)

                    def cum(u):
                        pe.wait_ge(lg_r[u], i + 1)
                        pe.wait_ge(P_cp[u], PU * i + P_CUM + 1)
                        o = bank(4 * u + 1, 2, HA)
                        pe.matmul(o[:, 0, :], tri, lgg[u][:, 0, :], start=True, stop=True)
                        pe.matmul(o[:, 1, :], ones, lgg[u][:, 0, :], start=True, stop=False)
                        pe.matmul(o[:, 1, :], tri, lgg[u][:, 1, :], start=False, stop=True).then_inc(P_full[u], 1)

                    def state(u):
                        pe.wait_ge(vp_r[u], i + 1)
                        pe.wait_ge(P_cp[u], PU * i + P_STATE + 1)
                        o = bank(4 * u + 1, KC, P)
                        for j in range(KC):
                            mm = pe.matmul(o[:, j, :], ktok[u][:, j * P:(j + 1) * P],
                                           packed(v2[u][0])[:, j * XC:(j + 1) * XC],
                                           start=True, stop=True)
                        mm.then_inc(P_full[u], 1)

                    def score(u, n):
                        c, j, half = n // 4, n // 2 % 2, n % 2
                        pe.wait_ge(qb_r[u], 4 * i + n // 2 + 1)
                        if n == 0:
                            pe.wait_ge(P_cp[u], PU * i + P_KT + 1 + 1)
                        pe.wait_ge(S_cp[u], SU * i + n + 1)
                        pe.matmul(bank(4 * u + 2, 512), kT[u][:, j, c * P:(c + 1) * P],
                                  qblk[u][:, n // 2 % 2, half:HC:2, :],
                                  start=True, stop=True).then_inc(S_full[u], 1)

                    def values(u, n):
                        c, j, half = n // 4, n // 2 % 2, n % 2
                        if n == 0:
                            pe.wait_ge(att_r[u], i + 1)
                        o = bank(4 * u + 3, KC, S)[:, j, c * P:(c + 1) * P]
                        if c == 1 and half == 0:
                            if j == 0:
                                pe.wait_ge(P_cp[u], PU * i + P_STATE + 1 + 1)
                            pe.matmul(o, sm[u][:, j, :], qT[u][:, j, P:S], start=True, stop=False, skip_group_check=True)
                        pe.wait_ge(S_cp[u], SU * i + n + 1 + 1)
                        for hh in range(4):
                            mm = pe.matmul(o[32 * hh:32 * hh + 32], v2[u][c][:, j * HC + 2 * hh + half, :],
                                           am[u][:, n % 2, hh, :], start=(c == 0 and half == 0), stop=(half == 1),
                                           skip_group_check=True)
                        mm.then_inc(av_d[u], 1)

                    def gates_feat(u):
                        pe.wait_ge(P_cp[u], PU * i + P_GCT + 1)
                        pe.wait_ge(lgx_r[u], i + 1)
                        o = bank(4 * u + 1, KC, S)
                        for j in range(KC):
                            lx = [lgx[u][:, c, j * HC:(j + 1) * HC].rearrange("p h e -> p (h e)") for c in range(2)]
                            pe.matmul(o[:, j, 0:P], lx[0], tri, start=True, stop=True)
                            pe.matmul(o[:, j, P:S], lx[0], ones, start=True, stop=False)
                            mm = pe.matmul(o[:, j, P:S], lx[1], tri, start=False, stop=True)
                        mm.then_inc(P_full[u], 1)

                    def p_out(u):
                        pe.wait_ge(att_r[u], i + 1 + 1)
                        pe.wait_ge(P_cp[u], PU * i + P_OUT + 1)
                        for c in range(2):
                            for k in range(KC):
                                mm = pe.matmul(bank(4 * u + 1, 2, D)[:, c, :], xnT[u][:, k, c * P:(c + 1) * P],
                                               woT[:, k, :], start=(k == 0), stop=(k == KC - 1))
                        mm.then_inc(P_full[u], 1)

                    def t_q(u):
                        pe.wait_ge(q_r[u], i + 1)
                        pe.wait_ge(T_cp[u], TU * i + T_Q + 1)
                        turn(bank(4 * u, KC, S), xn[u], T_full[u])

                    def t_cx(u):
                        pe.wait_ge(cx_r[u], 16 * i + 16)
                        pe.wait_ge(T_cp[u], TU * i + T_CX + 1)
                        turn(bank(4 * u, KC, S), cx[u], T_full[u])

                    def gates(u, part):
                        src = (kT, qT)[part][u]
                        if part == 0:
                            pe.wait_ge(T_cp[u], TU * i + T_CX + 1 + 1)
                            pe.wait_ge(P_cp[u], PU * i + P_GATE + 1)
                        else:
                            pe.wait_ge(T_cp[u], TU * i + T_Q + 1 + 1)
                        o = bank(4 * u + 1, 2, 2 * HX)
                        for c in range(2):
                            for k in range(KC):
                                mm = pe.matmul(o[:, c, :], src[:, k, c * P:(c + 1) * P], wg6[:, 2 * (1 - part) + k, :],
                                               start=(part == 0 and c == 0 and k == 0), stop=(part == 1 and k == KC - 1),
                                               skip_group_check=True)
                        if part == 1:
                            mm.then_inc(P_full[u], 1)

                    def both(f, *a):
                        for u in range(2):
                            f(u, *a)

                    both(t_xn)
                    both(p_feat, wqT, P_QT)
                    both(p_feat, wkT, P_KT)
                    both(p_tok, wvx, D + 2 * HA, 0, P_V0)
                    both(p_tok, wvx, D + 2 * HA, 1, P_V1)
                    both(p_tok, wkT, D, 0, P_KTOK)
                    both(score, 0)
                    both(cum)
                    both(state)
                    for n in range(1, SU):
                        both(score, n)
                        both(values, n - 1)
                    both(gates_feat)
                    both(values, SU - 1)
                    both(p_out)
                    both(t_cx)
                    both(gates, 0)
                    both(t_q)
                    both(gates, 1)

            @block.scalar
            def _(act):
                act.preload_act_table_set("natural_log_exp_and_others")
                def rs(i, u, ready, done, link):
                    act.wait_ge(ready[u], i + 1)
                    link(nc.scalar.activation(rstd[u], mv[u][:, :, 1], ACT.Ln, bias=eps_ap[:, 0:1]))
                    nc.scalar.activation(rstd[u], rstd[u], ACT.Exp, scale=-0.5).then_inc(done[u], 1)

                HEAD, CHAIN = 2, 4
                link = Chain(act, ch_a)
                for u in range(2):
                    rs(0, u, mv_r, rstd_r, link)

                def step(i, last):
                    link = Chain(act, ch_a, HEAD + i * CHAIN)

                    def t_copy(u, dsts, use):
                        act.wait_ge(T_full[u], TU * i + use + 1)
                        for dst in dsts:
                            ins = nc.scalar.activation(dst, bank(4 * u, KC, S), ACT.Copy)
                        ins.then_inc(T_cp[u], 1)

                    def p_copy(u, dst, shape, use):
                        act.wait_ge(P_full[u], PU * i + use + 1)
                        nc.scalar.activation(dst, bank(4 * u + 1, *shape), ACT.Copy).then_inc(P_cp[u], 1)

                    for u in range(2):
                        t_copy(u, [xnT[u]], T_XN)
                    for u in range(2):
                        p_copy(u, qT[u], (KC, S), P_QT)
                    for u in range(2):
                        p_copy(u, kT[u], (KC, S), P_KT)
                    for c in range(2):
                        for u in range(2):
                            p_copy(u, vx[u][:, c, :], (D + 2 * HA,), P_V0 + c)
                    for u in range(2):
                        act.wait_ge(P_cp[u], PU * i + P_V1 + 1 + 1)
                        nc.scalar.activation(eg[u], vx[u][:, :, D:D + 2 * HA], ACT.Exp, scale=-1.0).then_inc(eg_r[u], 1)
                    for u in range(2):
                        p_copy(u, ktok[u], (D,), P_KTOK)
                    for u in range(2):
                        act.wait_ge(g_r[u], i + 1)
                        nc.scalar.activation(lgg[u], coef[u], ACT.Ln).then_inc(lg_r[u], 1)
                    for u in range(2):
                        act.wait_ge(P_cp[u], PU * i + P_CUM + 1 + 1)
                        nc.scalar.activation(gc[u], gc[u], ACT.Exp).then_inc(gc_r[u], 1)
                    if not last:
                        for u in range(2):
                            rs(i + 1, u, mv_r, rstd_r, link)
                    for u in range(2):
                        act.wait_ge(S_full[u], SU * i + 6)
                        nc.scalar.activation(lgx[u], lgg[u].unsqueeze(3).to_broadcast([P, 2, HA, DA]), ACT.Copy)                             .then_inc(lgx_r[u], 1)
                    for u in range(2):
                        act.wait_ge(P_cp[u], PU * i + P_GCT + 1 + 1)
                        nc.scalar.activation(gcT[u], gcT[u], ACT.Exp).then_inc(gct_r[u], 1)
                    for u in range(2):
                        t_copy(u, [kT[u]], T_CX)
                    for u in range(2):
                        rs(i, u, mv2_r, rstd2_r, link)
                    for u in range(2):
                        t_copy(u, [QT[:, :, ds(2 * i + u, 1), :].squeeze(2) if not last else QT[:, :, 2 * i + u, :], qT[u]], T_Q)
                    assert last or link.n == CHAIN

                passes(act, step)

            @block.vector
            def _(dve):
                nc.vector.memset(eps_ap[:, 0:1], LN_EPS)
                nc.vector.memset(eps_ap[:, 1:2], LN_EPS ** 2)
                nc.vector.memset(wvx[:, :, D:D + 2 * HA], 0.0).then_inc(ch_v, 1)
                def spacer():
                    nc.vector.memset(pad_v[:, pads[0] % 8:pads[0] % 8 + 1], 0.0)
                    pads[0] += 1

                pads = [0]
                for u in range(2):
                    for c in range(2):
                        ins = nc.vector.memset(v2[u][c], 0.0)

                def stats(i, u, done, link):
                    t0 = 4 * i + 2 * u
                    spacer()
                    for c in range(2):
                        ins = nc.vector.bn_stats(st[u][:, c, :], X[:, ds(t0 + c, 1)].rearrange("p o d -> p (o d)"))
                    link(ins)
                    spacer()
                    for c in range(2):
                        ins = nc.vector.bn_aggr(mv[u][:, c, :], st[u][:, c, :])
                    ins.then_inc(done[u], 1)

                def norm(i, u, dst, ready, done):
                    dve.wait_ge(ready[u], i + 1)
                    t0 = 4 * i + 2 * u
                    for c in range(2):
                        ins = nc.vector.tensor_scalar(dst[u][:, c, :], X[:, ds(t0 + c, 1)].rearrange("p o d -> p (o d)"),
                                                      mv[u][:, c, 0:1], rstd[u][:, c:c + 1], ALU.subtract, ALU.mult)
                    ins.then_inc(done[u], 1)

                link = Chain(dve, ch_v, 1)
                dve.wait_ge(ld_x, 16)
                for u in range(2):
                    stats(0, u, mv_r, link)
                for u in range(2):
                    norm(0, u, xna, rstd_r, xn_r)
                dve.wait_ge(ld_cst, 16)
                dve.wait_ge(ld_w, 16 * 9)
                nc.vector.tensor_scalar(swb, hm16, swc, None, ALU.mult).then_inc(w_ready, 1)
                nc.vector.tensor_tensor(wg6[:, 2:4, :], wg6[:, 2:4, :], wg6[:, 4:6, :], ALU.add)
                dve.wait_ge(ch_v, 1)
                for k in range(KC):
                    nc.vector.tensor_scalar(wvx[:, k, D + k * HC:D + (k + 1) * HC], hm16, gwc, None, ALU.mult)
                dve.wait_ge(w_full, 1)
                nc.vector.tensor_copy(wvx[:, :, D + HA:D + 2 * HA], bank(0, KC, HA)).then_inc(w_ready, 1)
                dve.wait_ge(ld_xr, 16)
                HEAD, CHAIN = 3, 16

                def step(i, last):
                    link = Chain(dve, ch_v, HEAD + i * CHAIN)

                    def blocks(u, m):
                        c, j = m // 2, m % 2
                        if m == 0:
                            dve.wait_ge(P_cp[u], PU * i + P_QT + 1 + 1)
                        if m >= 2:
                            dve.wait_ge(S_full[u], SU * i + 2 * (m - 2) + 2)
                        q = qT[u][:, j, c * P:(c + 1) * P].unsqueeze(1).to_broadcast([P, HC, P])
                        nc.vector.tensor_tensor(qblk[u][:, m % 2], q, hm16.unsqueeze(2).to_broadcast([P, HC, P]),
                                                ALU.mult).then_inc(qb_r[u], 1)

                    for m in range(2):
                        for u in range(2):
                            blocks(u, m)
                    for u in range(2):
                        dve.wait_ge(eg_r[u], i + 1)
                        link(nc.vector.tensor_scalar(eg[u], eg[u], 1.0, None, ALU.add))
                        link(nc.vector.reciprocal(eg[u], eg[u]))
                        nc.vector.tensor_scalar(coef[u], eg[u][:, :, 0:HA], 1e-6, None, ALU.max).then_inc(g_r[u], 1)

                    def masked(u, n):
                        dve.wait_ge(S_full[u], SU * i + n + 1)
                        if n >= 2:
                            dve.wait_ge(av_d[u], SU * i + n - 1)
                        nc.vector.tensor_tensor(am[u][:, n % 2], bank(4 * u + 2, 4, P),
                                                tri.unsqueeze(1).to_broadcast([P, 4, P]), ALU.mult) \
                            .then_inc(S_cp[u], 1)

                    for u in range(2):
                        masked(u, 0)
                    for u in range(2):
                        dve.wait_ge(P_full[u], PU * i + P_CUM + 1)
                        ins = nc.vector.tensor_scalar(gc[u], bank(4 * u + 1, 2, HA), -30.0, 30.0, ALU.max, ALU.min)
                        ins.then_inc(P_cp[u], 1)
                        dve.wait_ge(lg_r[u], i + 1)
                        link(nc.vector.tensor_tensor(coef[u], vx[u][:, :, D + HA:D + 2 * HA], eg[u][:, :, HA:2 * HA],
                                                     ALU.mult))
                    for u in range(2):
                        dve.wait_ge(gc_r[u], i + 1)
                        link(nc.vector.tensor_scalar(gc[u], gc[u], 1e-6, None, ALU.add))
                        link(nc.vector.reciprocal(eg[u][:, :, 0:HA], gc[u]))
                        link(nc.vector.tensor_tensor(coef[u], coef[u], eg[u][:, :, 0:HA], ALU.mult))
                        for c in range(2):
                            ins = nc.vector.tensor_tensor(packed(v2[u][c]),
                                                          vx[u][:, c, 0:D].rearrange("p (a s e) -> p a s e", s=2, e=DA),
                                                          coef[u][:, c, :].rearrange("p (a s) -> p a s", s=2).unsqueeze(3)
                                                          .to_broadcast([P, HA // 2, 2, DA]), ALU.mult)
                        ins.then_inc(vp_r[u], 1)
                    for n in range(1, SU):
                        if n in (2, 4):
                            for u in range(2):
                                blocks(u, n // 2 + 1)
                        for u in range(2):
                            masked(u, n)
                        if n == 3 and not last:
                            for u in range(2):
                                stats(i + 1, u, mv_r, link)
                        if n == 5 and not last:
                            for u in range(2):
                                norm(i + 1, u, xna, rstd_r, xn_r)
                        if n == 1:
                            for u in range(2):
                                dve.wait_ge(P_full[u], PU * i + P_STATE + 1)
                                ins = nc.vector.tensor_tensor(sm[u], bank(4 * u + 1, KC, P),
                                                              blkm.unsqueeze(1).to_broadcast([P, KC, P]), ALU.mult)
                                ins.then_inc(P_cp[u], 1)
                    for u in range(2):
                        dve.wait_ge(P_full[u], PU * i + P_GCT + 1)
                        nc.vector.tensor_scalar(gcT[u], bank(4 * u + 1, KC, S), -30.0, 30.0, ALU.max, ALU.min) \
                            .then_inc(P_cp[u], 1)
                    for u in range(2):
                        dve.wait_ge(gct_r[u], i + 1)
                        dve.wait_ge(av_d[u], SU * i + SU)
                        nc.vector.scalar_tensor_tensor(xnT[u], gcT[u], 1e-6, bank(4 * u + 3, KC, S), ALU.add, ALU.mult) \
                            .then_inc(att_r[u], 1)
                    for u in range(2):
                        dve.wait_ge(P_full[u], PU * i + P_OUT + 1)
                        xt = X[:, ds(4 * i + 2 * u, 2), :]
                        nc.vector.tensor_tensor(xt, bank(4 * u + 1, 2, D), xt, ALU.add).then_inc(P_cp[u], 1)
                        dve.wait_ge(P_cp[u], PU * i + P_OUT + 1 + 1)
                    for u in range(2):
                        stats(i, u, mv2_r, link)
                    for u in range(2):
                        norm(i, u, xn, rstd2_r, q_r)
                    for u in range(2):
                        dve.wait_ge(P_full[u], PU * i + P_GATE + 1)
                        for c in range(2):
                            o = GT[:, c, :, :, ds(2 * i + u, 1)].rearrange("p g h o -> p (g h) o")
                            ins = nc.vector.tensor_tensor(o, bank(4 * u + 1, 2, 2 * HX)[:, c, :].unsqueeze(2),
                                                          gbias.unsqueeze(2), ALU.add)
                        ins.then_inc(P_cp[u], 1)
                    assert last or link.n == CHAIN, link.n

                passes(dve, step)

        QBLK = U[:, 0:KC * XC * B * S].rearrange("p (j h b s) -> p j h b s", j=KC, h=XC, b=B)
        KHv = KH[:, :].rearrange("p (s h b) -> p s h b", h=HX, b=B)
        qblk_v, qblk_a, late_cp, filled = sem("qblk_v"), sem("qblk_a"), sem("late_cp"), sem("filled")
        turned, prod = sem("turned"), sem("prod")
        pet_r, kh_cp = sems("pet_r"), sems("kh_cp")
        NPAIR = (NBLK + 1) // 2
        NGRP = (NBLK + GRP - 1) // GRP

        def tiles(q):
            return range(2 * q, min(2 * q + 2, NBLK))

        def gathered(n):
            g = n // GRP
            return sum(16 * (min(NBLK, (k + 1) * GRP) - k * GRP) for k in range(g % NGS, g + 1, NGS))

        def turn_copy(copy, wait, q):
            wait(turned, q + 1)
            if q >= 3:
                wait(prod, q - 2)
            w = len(tiles(q)) * KC * P
            copy(PET[:, q % 3, 0:w], bank(q % 4, 512)[:, 0:w]).then_inc(pet_r[q % 2], 1)

        QP = P // 2

        NPIECE = 2 * XC

        def query_parts(k):
            part, end, h = k // NPIECE, k // XC % 2, k % XC
            return part, (slice(S - (part + 1) * QP, S - part * QP) if end else slice(part * QP, (part + 1) * QP)), h

        def mixed(g):
            return [bank(4 + 2 * (g % 2) + k, GRP // 2, HX * B, 2) for k in range(2)]

        def group_copy(copy, wait, g):
            n = min(NBLK, (g + 1) * GRP)
            wait(prod, (n + 1) // 2)
            w = (n - g * GRP) * HX * B
            if g >= NMIX:
                copy(KH[:, g * 512:g * 512 + w], bank(4 + 2 * (g % 2), 512)[:, 0:w]).then_inc(kh_cp[g % 2], 1)
                return
            out = KH[:, g * 512:(g + 1) * 512].rearrange("p (n x) -> p n x", n=GRP)
            for k in range(2):
                ins = copy(out[:, k * 4:k * 4 + 4], mixed(g)[k][:, :, :, 1])
            ins.then_inc(late_cp, 1)
            wait(late_cp, g + 1)
            for k in range(2):
                n0, n1 = max(1, g * GRP + 4 * k), g * GRP + 4 * k + 4
                w = n1 - n0
                ins = nc.vector.copy_predicated(out[:, 4 * k + 4 - w:4 * k + 4],
                                                tri.bitcast(I32)[:, n0 - 1:n1 - 1].unsqueeze(2).to_broadcast([P, w, HX * B]),
                                                mixed(g)[k][:, 4 - w:4, :, 0])
            ins.then_inc(kh_cp[g % 2], 1)

        def copies(copy, wait, e, query_piece):
            for k in range(NPIECE):
                query_piece(k)
            for q in range(NPAIR + 4):
                if q < NPAIR and q % 2 == e:
                    turn_copy(copy, wait, q)
                    if 1 <= q // 2 - 1 <= NPIECE:
                        query_piece(NPIECE + q // 2 - 2)
                g = (q - 6) // 4
                if q >= 6 and q % 4 == 2 and g < NGRP - 1 and (1 if g < NMIX else g % 2) == e:
                    group_copy(copy, wait, g)
            if (NGRP - 1) % 2 == e:
                group_copy(copy, wait, NGRP - 1)

        with nc.Block() as block:
            @block.sync
            def _(sp):
                sp.dma_start(rows_dram.rearrange("(n p) d -> p n d", p=P),
                             cst[:, C_W - ROW:C_W].unsqueeze(1).to_broadcast([P, NT, ROW])).then_inc(filled, 16)
                sp.wait_ge(filled, 16)

            @block.gpsimd
            def _(pool):
                for n in range(NPRE + NRING, NBLK):
                    pool.wait_ge(turned, rows_before(n) // 2 + 1)
                    gather(pool, n)

            @block.tensor
            def _(pe):
                def turn(q):
                    n0 = 2 * q
                    if n0 % GRP == 0:
                        pe.wait_ge(gat[n0 // GRP % NGS], gathered(n0))
                    if q >= 4:
                        pe.wait_ge(pet_r[q % 2], (q - 4) // 2 + 1)
                    o = bank(q % 4, 2, KC, P)
                    for n in tiles(q):
                        src = rows_of(n)
                        for j in range(KC):
                            mm = pe.transpose(o[:, n % 2, j, :], src[:, j * P:(j + 1) * P], ident)
                    mm.then_inc(turned, 1)

                def products(q):
                    pe.wait_ge(pet_r[q % 2], q // 2 + 1)
                    g = 2 * q // GRP
                    if 2 * q % GRP == 0 and g >= 2:
                        pe.wait_ge(kh_cp[g % 2], g // 2)
                    pet = PET[:, q % 3, :].rearrange("p (n j m) -> p n j m", n=2, j=KC)
                    for n in tiles(q):
                        for j in range(KC):
                            if n >= P:
                                slot = n % GRP * KC + j
                                r = min(4, GRP * KC - slot)
                                o = bank(4 + 2 * (g % 2), GRP * KC, XC * B)[:, slot:slot + r]
                                rhs = QBLK[:, j, :, :, n - 1].rearrange("p h b -> p (h b)").unsqueeze(1).to_broadcast([P, r, XC * B])
                            else:
                                o = mixed(g)[n % GRP // 4].rearrange("p n (j h b) s -> p n j h b s", j=KC, h=XC)[:, n % 4, j]
                                if n == 0:
                                    rhs = QBLK[:, j, :, :, S - 1:S].to_broadcast([P, XC, B, 2])
                                else:
                                    rhs = QBLK[:, j, :, :, n - 1:S - n + 1:S - 2 * n]
                            mm = pe.matmul(o, pet[:, n % 2, j, :], rhs, start=True, stop=True, skip_group_check=True)
                    mm.then_inc(prod, 1)

                for q in range(NPAIR + 2):
                    if q < NPAIR:
                        turn(q)
                    if q >= 2 and (q == 2 or (q - 2) * 2 % QP == 0 and (q - 2) * 2 <= P - QP):
                        pe.wait_ge(qblk_v, (q - 2) * 2 // QP + 1)
                        pe.wait_ge(qblk_a, (q - 2) * 2 // QP + 1)
                    if q >= 2:
                        products(q - 2)

            @block.scalar
            def _(act):
                def query_piece(k):
                    part, sl, h = query_parts(k)
                    ins = nc.scalar.activation(QBLK[:, 1, h, :, sl], QT[:, 1, :, sl], ACT.Copy, scale=hm32[:, h:h + 1])
                    if k % NPIECE == NPIECE - 1:
                        ins.then_inc(qblk_a, 1)

                copies(lambda o, a: nc.scalar.activation(o, a, ACT.Copy), act.wait_ge, 0, query_piece)

            @block.vector
            def _(dve):
                def query_piece(k):
                    part, sl, h = query_parts(k)
                    ins = nc.vector.tensor_scalar(QBLK[:, 0, h, :, sl], QT[:, 0, :, sl], hm32[:, h:h + 1], None, ALU.mult)
                    if k % NPIECE == NPIECE - 1:
                        ins.then_inc(qblk_v, 1)

                copies(nc.vector.tensor_copy, dve.wait_ge, 1, query_piece)

        R = HX * B
        cr = Carve(RING[:, 4096:], NRING * D - 4096)
        r_t, r_l, r_F, r_a, r_M, r_ml, r_rev, r_one = [cr(S)[0:R] for _ in range(8)]
        r_full, r_ch, r_ab, r_ln, r_nm, r_am = sem("r_full"), sem("r_ch"), sem("r_ab"), sem("r_ln"), sem("r_nm"), sem("r_am")
        r_tt, r_dma, r_ach = sem("r_tt"), sem("r_dma"), sem("r_ach")
        cp = Carve(PET[:, :, :].rearrange("p a b -> p (a b)"), 3 * 512)
        v1 = [cp(2, HX, DX + 1) for _ in range(2)]
        lnwb = cp(D)
        rwT, rngc, rnbc, rbb = cp(KC, E), cp(KC), cp(KC), cp(E)
        kept = cp.at - (KC * E + 2 * KC + E)
        m_ld = sem("m_ld")
        with nc.Block() as block:
            @block.tensor
            def _(pe):
                for g in range(2):
                    for c in range(2):
                        mm = pe.transpose(bank(0, 2, 2, P)[0:R, g, c, :], GT[:, c, g].rearrange("p h b -> p (h b)"), ident)
                mm.then_inc(r_full, 1)
                pe.wait_ge(r_am, 1)
                pe.transpose(bank(1, 2, R)[:, 0], r_a[:, 0:P], ident[0:R, 0:R])
                pe.transpose(bank(1, 2, R)[:, 1], r_rev[:, 0:P], ident[0:R, 0:R]).then_inc(r_tt, 1)
                pe.transpose(bank(2, 2, R)[:, 0], r_ml[:, 0:P], ident[0:R, 0:R])
                pe.transpose(bank(2, 2, R)[:, 1], r_ml[:, P:S], ident[0:R, 0:R]).then_inc(r_tt, 1)

            @block.scalar
            def _(act):
                act.wait_ge(r_full, 1)
                nc.scalar.activation(r_t, bank(0, 2, S)[0:R, 1, :], ACT.Abs).then_inc(r_ab, 1)
                act.wait_ge(r_ab, 1)
                nc.scalar.activation(r_l, r_t, ACT.Exp, scale=-1.0).then_inc(r_ach, 1)
                act.wait_ge(r_ach, 1)
                nc.scalar.activation(r_l, r_l, ACT.Ln, bias=ones[0:R, 0:1]).then_inc(r_ln, 1)
                act.wait_ge(r_tt, 2)
                nc.scalar.activation(EX[:, :, :], bank(2, 2, R), ACT.Exp, scale=-1.0)

            @block.vector
            def _(dve):
                link = Chain(dve, r_ch)
                ig, fg = bank(0, 2, S)[0:R, 0, :], bank(0, 2, S)[0:R, 1, :]
                nc.vector.memset(r_one, 1.0)
                dve.wait_ge(r_full, 1)
                dve.wait_ge(r_ln, 1)
                link(nc.vector.scalar_tensor_tensor(r_t, fg, 0.0, r_l, ALU.min, ALU.subtract))
                link(nc.vector.tensor_tensor_scan(r_F, r_one, r_t, 0.0, ALU.mult, ALU.add))
                link(nc.vector.tensor_tensor(r_a, ig, r_F, ALU.subtract))
                nc.vector.tensor_tensor_scan(r_M, r_a, r_a, -3.0e38, ALU.max, ALU.max).then_inc(r_nm, 1)
                dve.wait_ge(r_nm, 1)
                nc.vector.tensor_tensor(r_ml, r_F, r_M, ALU.add)
                nc.vector.tensor_copy(r_rev[:, 0:P], r_a[:, S - 1:P - 1:-1]).then_inc(r_am, 1)
                dve.wait_ge(r_tt, 1)
                nc.vector.tensor_scalar(AT[:, :, :], bank(1, 2, R), -1.0, None, ALU.mult)

            @block.sync
            def _(sp):
                sp.dma_start(lnwb, lnw_d.partition_broadcast(P)).then_inc(m_ld, 16)
                sp.dma_start(rwT, rw_d.rearrange("(k p) n -> p k n", p=P)).then_inc(m_ld, 16)
                sp.dma_start(rngc, rng_d).then_inc(m_ld, 16)
                sp.dma_start(rnbc, rnb_d).then_inc(m_ld, 16)
                sp.dma_start(rbb, rb_d.partition_broadcast(P)).then_inc(m_ld, 16)
                sp.wait_ge(m_ld, 16 * 5)
                sp.wait_ge(r_nm, 1)
                sp.dma_start(m_dram, r_M).then_inc(r_dma, 16)
                sp.wait_ge(r_dma, 16)

        co = Carve(RING, NRING * D)
        cq = Carve(QT[:, :, :, :].rearrange("p j b s -> p (j b s)"), KC * B * S)
        NVX = DX + 1
        mx = [co(2, HX, DX) for _ in range(2)]
        mk = [co(KC, S) for _ in range(2)]
        nm = [co(XC, S) for _ in range(2)]
        Dm = [cq(XC, S + P) for _ in range(2)]
        tmp = [co(2, 512) for _ in range(2)]
        pst = [cq(2, HX) for _ in range(2)]
        hmu = [cq(2, HX) for _ in range(2)]
        stage[0] = late
        m_cst = sem("m_cst")
        mx_r, nm_r, v1_r = sems("mx_r"), sems("nm_r"), sems("v1_r")
        A_full, B_full, A_cp, B_cp = sems("A_full"), sems("B_full"), sems("A_cp"), sems("B_cp")
        ex_r, dec_r, c_r, pv_r = sems("ex_r"), sems("dec_r"), sems("c_r"), sems("pv_r")
        h_cp, var_r, mrs_r, hn_r, x2_r = sems("h_cp"), sems("var_r"), sems("mrs_r"), sems("hn_r"), sems("x2_r")
        m_ch, m_ach = sem("m_ch"), sem("m_ach")
        AU, BU = 4, 3

        with nc.Block() as block:
            @block.sync
            def _(sp):
                prime(sp, A_full, v1_r, ex_r, pv_r, h_cp, A_cp, B_cp, x2_r)
                m_v = m_dram.rearrange("(h b) s -> b h s", b=B)
                with sp.Fori(0, B // 2) as i:
                    for u in range(2):
                        sp.wait_ge(A_full[u], AU * i + 1)
                        sp.sem_inc(sp_on, 1)
                        sp.wait_ge(v1_r[u], i + 1)
                        sp.sem_inc(sp_on, 1)
                        sp.dma_start(mx[u][:, 0].rearrange("p h d -> p (h d)"),
                                     ctx_d[ds(2 * i + u, 1), 0:P].rearrange("o p d -> p (o d)")).then_inc(mx_r[u], 16)
                        sp.dma_start(mx[u][:, 1].rearrange("p h d -> p (h d)"),
                                     ctxr_d[ds(2 * i + u, 1)].rearrange("o p d -> p (o d)")).then_inc(mx_r[u], 16)
                        for j in range(KC):
                            sp.wait_ge(ex_r[j], 2 * i + u + 1)
                            sp.sem_inc(sp_on, 1)
                            sp.dma_start(nm[j], m_v[ds(2 * i + u, 1), j * XC:(j + 1) * XC].rearrange("o h s -> (o h) s")
                                         .partition_broadcast(P)).then_inc(nm_r[j], 16)
                retire(sp)

            @block.gpsimd
            def _(pool):
                nc.gpsimd.tensor_scalar(lnwb, lnwb, 1.0, None, ALU.add).then_inc(m_cst, 1)
                for u in range(2):
                    ins = nc.gpsimd.memset(v1[u][:, :, :, DX:NVX], 1.0)
                ins.then_inc(m_cst, 1)

                def mask(i, u, j):
                    pool.wait_ge(ex_r[j], 2 * i + u + 1 + 1)
                    nc.gpsimd.tensor_tensor(Dm[j][:, :, 0:P], Dm[j][:, :, 0:P],
                                            tri.unsqueeze(1).to_broadcast([P, XC, P]), ALU.mult)
                    nc.gpsimd.tensor_tensor(Dm[j][:, :, S:S + P], Dm[j][:, :, S:S + P],
                                            trirev.unsqueeze(1).to_broadcast([P, XC, P]), ALU.mult) \
                        .then_inc(dec_r[j], 1)

                def residual(i, u):
                    pool.wait_ge(hn_r[u], i + 1)
                    h = tmp[u].rearrange("p a b -> p (a b)")[:, 0:2 * D].rearrange("p (c d) -> p c d", c=2)
                    xt = X[:, ds(4 * i + 2 * u, 2), :]
                    nc.gpsimd.tensor_tensor(xt, xt, h, ALU.add).then_inc(x2_r[u], 1)

                mask(0, 0, 0)
                mask(0, 0, 1)

                def step(i, last):
                    mask(i, 1, 0)
                    mask(i, 1, 1)
                    residual(i, 0)
                    if not last:
                        mask(i + 1, 0, 0)
                        mask(i + 1, 0, 1)
                    residual(i, 1)

                passes(pool, step)

            @block.tensor
            def _(pe):
                def keys(i, u):
                    pe.wait_ge(mx_r[u], 32 * i + 32)
                    pe.wait_ge(A_cp[u], AU * i + 1)
                    for k in range(KC):
                        for c in range(2):
                            mm = pe.transpose(bank(4 * u, KC, 2, P)[:, k, c, :],
                                              mx[u][:, c].rearrange("p h d -> p (h d)")[:, k * P:(k + 1) * P], ident)
                    mm.then_inc(A_full[u], 1)

                def score(i, u, m):
                    j, q, b = m // 3, m % 3, ds(2 * i + u, 1)
                    if m % 2 == 0:
                        pe.wait_ge(A_cp[u], AU * i + m // 2 + 1 + 1)
                    else:
                        pe.wait_ge(A_cp[u], AU * i + 1 + 1)
                        pe.wait_ge(B_cp[u], BU * i + m // 2 + 1)
                    o = bank(4 * u + m % 2, 512)
                    if q < 2:
                        rhs = QBLK[:, j, 2 * q:2 * q + 2, b, :].rearrange("p h o s -> p h (o s)")
                        lhs = mk[u][:, j, 0:P]
                    else:
                        rhs = QBLK[:, j, :, b, P:S].rearrange("p h o s -> p h (o s)")
                        lhs = mk[u][:, j, P:S]
                    pe.matmul(o, lhs, rhs, start=True, stop=True).then_inc((B_full if m % 2 else A_full)[u], 1)

                def values(i, u, j):
                    pe.wait_ge(c_r[j], 3 * (2 * i + u) + 3)
                    pe.wait_ge(v1_r[u], i + 1 + 1)
                    if j == 0:
                        pe.wait_ge(h_cp[u], i + 1)
                    for hh in range(XC):
                        h = j * XC + hh
                        for c in range(2):
                            o = bank(4 * u + 2 + c, HX, NVX)[:, h, :]
                            mm = pe.matmul(o, Dm[j][:, hh, c * P:(c + 1) * P], v1[u][:, 0, h, :],
                                           start=True, stop=(c == 0), skip_group_check=True)
                        mm = pe.matmul(o, Dm[j][:, hh, S:S + P], v1[u][:, 1, h, :],
                                       start=False, stop=True, skip_group_check=True)
                    mm.then_inc(pv_r[j], 1)

                keys(0, 0)
                score(0, 0, 0)
                score(0, 0, 1)

                def step(i, last):
                    keys(i, 1)
                    score(i, 0, 2)
                    score(i, 0, 3)
                    values(i, 0, 0)
                    score(i, 0, 4)
                    score(i, 0, 5)
                    score(i, 1, 0)
                    score(i, 1, 1)
                    values(i, 0, 1)
                    score(i, 1, 2)
                    score(i, 1, 3)
                    if not last:
                        keys(i + 1, 0)
                    values(i, 1, 0)
                    score(i, 1, 4)
                    if not last:
                        score(i + 1, 0, 0)
                        score(i + 1, 0, 1)
                    score(i, 1, 5)
                    values(i, 1, 1)

                passes(pe, step)

            @block.scalar
            def _(act):
                def keys(i, u):
                    act.wait_ge(A_full[u], AU * i + 1 + 1)
                    nc.scalar.activation(mk[u], bank(4 * u, KC, S), ACT.Copy, scale=float(DX) ** -0.5) \
                        .then_inc(A_cp[u], 1)

                def vals(i, u):
                    act.wait_ge(h_cp[u], i + 1)
                    nc.scalar.activation(v1[u][:, :, :, 0:DX], mx[u], ACT.Copy).then_inc(v1_r[u], 1)

                def decay(i, u, j, link):
                    act.wait_ge(nm_r[j], 16 * (2 * i + u + 1))
                    act.wait_ge(pv_r[j], 2 * i + u + 1)
                    for hh in range(XC):
                        hb = (j * XC + hh) * B
                        nc.scalar.activation(Dm[j][:, hh, 0:S], nm[j][:, hh, :], ACT.Relu,
                                             bias=AT[:, 0, ds(hb + 2 * i + u, 1)])
                        ins = nc.scalar.activation(Dm[j][:, hh, S:S + P], nm[j][:, hh, P:S], ACT.Relu,
                                                   bias=AT[:, 1, ds(hb + 2 * i + u, 1)])
                    link(ins)
                    nc.scalar.activation(Dm[j], Dm[j], ACT.Exp, scale=-1.0).then_inc(ex_r[j], 1)

                def rs(i, u, link):
                    act.wait_ge(var_r[u], i + 1)
                    link(nc.scalar.activation(hmu[u], hmu[u], ACT.Ln, bias=eps_ap[:, 0:1], scale=1.0 / DX))
                    nc.scalar.activation(hmu[u], hmu[u], ACT.Exp, scale=-0.5).then_inc(mrs_r[u], 1)

                link = Chain(act, m_ach)
                keys(0, 0)
                decay(0, 0, 0, link)
                vals(0, 0)
                decay(0, 0, 1, link)
                HEAD, STEP = link.n, 6

                def step(i, last):
                    link = Chain(act, m_ach, HEAD + i * STEP)
                    keys(i, 1)
                    decay(i, 1, 0, link)
                    vals(i, 1)
                    decay(i, 1, 1, link)
                    if not last:
                        keys(i + 1, 0)
                    rs(i, 0, link)
                    if not last:
                        decay(i + 1, 0, 0, link)
                        vals(i + 1, 0)
                        decay(i + 1, 0, 1, link)
                    rs(i, 1, link)
                    assert last or link.n == STEP, link.n

                passes(act, step)

            @block.vector
            def _(dve):
                def weights(i, u, m):
                    j, q = m // 3, m % 3
                    b = ds(2 * i + u, 1)
                    cpd = (B_cp if m % 2 else A_cp)[u]
                    dve.wait_ge((B_full if m % 2 else A_full)[u], (BU if m % 2 else AU) * i + m // 2 + 3 - 2 * (m % 2))
                    if q < 2:
                        kh = KHv[:, 1:S + 1, j * XC + 2 * q:j * XC + 2 * q + 2, b].rearrange("p s h o -> p h (s o)")
                        n, w, d = 2, S, Dm[j][:, 2 * q:2 * q + 2, 0:S]
                    else:
                        kh = KHv[:, 0:P, j * XC:(j + 1) * XC, b].rearrange("p s h o -> p h (s o)")
                        n, w, d = XC, P, Dm[j][:, :, S:S + P]
                    if m == 0:
                        dve.wait_ge(x2_r[u], i + 1)
                    tt = tmp[u][:, m % 2, :].rearrange("p (h s) -> p h s", h=n)
                    sc = bank(4 * u + m % 2, n, w)
                    if q == 2:
                        nc.vector.tensor_tensor(tt[:, :, ::-1], sc[:, :, ::-1], kh, ALU.add).then_inc(cpd, 1)
                    else:
                        nc.vector.tensor_tensor(tt, sc, kh, ALU.add).then_inc(cpd, 1)
                    dve.wait_ge(cpd, (BU if m % 2 else AU) * i + m // 2 + 3 - m % 2)
                    if q == 0:
                        dve.wait_ge(dec_r[j], 2 * i + u + 1)
                    nc.vector.tensor_tensor(d, tt, d, ALU.mult).then_inc(c_r[j], 1)

                def finish(i, u, link):
                    for j in range(KC):
                        dve.wait_ge(pv_r[j], 2 * i + u + 2)
                    h = tmp[u].rearrange("p a b -> p (a b)")[:, 0:2 * D].rearrange("p (c h d) -> p c h d", c=2, h=HX)
                    exv = EX[:, :, :].rearrange("p c (h b) -> p c h b", b=B)[:, :, :, ds(2 * i + u, 1)].rearrange("p c h o -> p c (h o)")
                    for c in range(2):
                        ins = nc.vector.tensor_scalar(pst[u][:, c], bank(4 * u + 2 + c, HX, NVX)[:, :, DX], -1.0, None, ALU.mult)
                    link(ins)
                    for c in range(2):
                        ins = nc.vector.tensor_tensor(pst[u][:, c], bank(4 * u + 2 + c, HX, NVX)[:, :, DX], pst[u][:, c], ALU.max)
                    link(ins)
                    link(nc.vector.tensor_tensor(pst[u], pst[u], exv, ALU.max))
                    link(nc.vector.tensor_scalar(pst[u], pst[u], MLSTM_EPS, None, ALU.add))
                    link(nc.vector.reciprocal(pst[u], pst[u]))
                    for c in range(2):
                        ins = nc.vector.tensor_tensor(h[:, c], bank(4 * u + 2 + c, HX, NVX)[:, :, 0:DX],
                                                      pst[u][:, c].unsqueeze(2).to_broadcast([P, HX, DX]), ALU.mult)
                    ins.then_inc(h_cp[u], 1)
                    dve.wait_ge(h_cp[u], i + 1 + 1)
                    hf = h.rearrange("p c h d -> p (c h) d")
                    hmf = hmu[u].rearrange("p c h -> p (c h)")
                    link(nc.vector.tensor_reduce(out=hmf, in_=hf, op=ALU.add, axis=AX))
                    link(nc.vector.tensor_scalar(hmf, hmf, 1.0 / DX, None, ALU.mult))
                    link(nc.vector.tensor_tensor(hf, hf, hmf.unsqueeze(2).to_broadcast([P, 2 * HX, DX]), ALU.subtract))
                    sq = tmp[u].rearrange("p a b -> p (a b)")[:, 2 * D:4 * D].rearrange("p (h d) -> p h d", d=DX)
                    link(nc.vector.tensor_tensor(sq, hf, hf, ALU.mult))
                    nc.vector.tensor_reduce(out=hmf, in_=sq, op=ALU.add, axis=AX).then_inc(var_r[u], 1)

                def scale(i, u, link):
                    h = tmp[u].rearrange("p a b -> p (a b)")[:, 0:2 * D]
                    hf, hc = h.rearrange("p (h d) -> p h d", d=DX), h.rearrange("p (c d) -> p c d", c=2)
                    hmf = hmu[u].rearrange("p c h -> p (c h)")
                    dve.wait_ge(mrs_r[u], i + 1)
                    link(nc.vector.tensor_tensor(hf, hf, hmf.unsqueeze(2).to_broadcast([P, 2 * HX, DX]), ALU.mult))
                    nc.vector.tensor_tensor(hc, hc, lnwb.unsqueeze(1).to_broadcast([P, 2, D]), ALU.mult).then_inc(hn_r[u], 1)

                def unit(i, u, j):
                    for m in range(3):
                        weights(i, u, 3 * j + m)

                dve.wait_ge(m_cst, 2)
                unit(0, 0, 0)
                STEP = 20

                def step(i, last):
                    link = Chain(dve, m_ch, i * STEP)
                    unit(i, 0, 1)
                    unit(i, 1, 0)
                    finish(i, 0, link)
                    weights(i, 1, 3)
                    scale(i, 0, link)
                    weights(i, 1, 4)
                    weights(i, 1, 5)
                    if not last:
                        unit(i + 1, 0, 0)
                    finish(i, 1, link)
                    scale(i, 1, link)
                    assert link.n == STEP, link.n

                passes(dve, step)

        early.close()

        cf = Carve(QT[:, :, :, :].rearrange("p j b s -> p (j b s)"), KC * B * S)
        cl = Carve(PET[:, :, :].rearrange("p a b -> p (a b)"), kept)
        cl2 = Carve(GT[:, :, :, :, :].rearrange("p a b c d -> p (a b c d)"), 512)
        cw = Carve(U, U_W)
        w1s = cw(E, KC, I)
        b1s, lgs, lbs = cw(E, I // P), cw(E, KC), cw(E, KC)
        w2s = KH[:, 0:E * (I // P) * D].rearrange("p (e n d) -> p e n d", e=E, n=I // P)
        ZR = RING[:, 0:T * ROW].rearrange("p (t w) -> p t w", w=ROW)
        combT = QT[:, 0, :, :].rearrange("p b s -> p (b s)")
        FS = 4
        hid = [cf(2, D) for _ in range(FS)]
        zs = [cf(KC, S) for _ in range(FS)]
        fst = [cw(2, 6) for _ in range(FS)]
        fmv = [cw(2, 2) for _ in range(FS)]
        frs = [cw(2) for _ in range(FS)]
        rwp, rnbb = cw(KC, E), cw(KC, P)
        open_, base = cw(NT, E), cw(E)
        ntile, tile_end, tile_f, slot_f = cw(E), cw(E), cw(NT), cw(2 * T)
        LG, LG2, EQ = cl(T, E), cl(T, E), cl(T, E)
        OH = [cl(T, E) for _ in range(2)]
        picked, count, upto, slot_of = cl(T, E), cl(E, T), cl(E, T), cl(T, E)
        over = LG2.rearrange("p t e -> p (t e)").rearrange("p (e t) -> p e t", e=E)
        M1, M2, IX, PR = cl(T), cl(T), cl(T), cl(T)
        b2s = cl2(D)
        comb = ZR[:, :, D + 1:ROW]
        f_ld, f_w, f_rb = sem("f_ld"), sem("f_w"), sem("f_rb")
        fmv_r, frs_r, zt_r = sems("fmv_r", FS), sems("frs_r", FS), sems("zt_r", FS)
        FT_full, FT_cp, FL_full, FL_cp = sems("FT_full", FS), sems("FT_cp", FS), sems("FL_full", FS), sems("FL_cp", FS)
        zr_r = sems("zr_r", FS)
        f_ch, f_ach, f_df, f_ex, f_cb = sem("f_ch"), sem("f_ach"), sem("f_df"), sem("f_ex"), sem("f_cb")
        f_ct, f_cc, f_bb, f_pk, f_ps, f_sl = sem("f_ct"), sem("f_cc"), sem("f_bb"), sem("f_pk"), sem("f_ps"), sem("f_sl")
        f_wt, f_sc, f_x, f_st = sem("f_wt"), sem("f_sc"), sem("f_x"), sem("f_st")
        NI = I // P
        cg = Carve(RING, NRING * D)
        z_in = [cg(D) for _ in range(2)]
        meta = [cg(1 + E) for _ in range(2)]
        hT = [cg(KC, P) for _ in range(2)]
        w1c = [QT[:, u].rearrange("p b s -> p (b s)").rearrange("p (k n) -> p k n", k=KC) for u in range(2)]
        gel = [cg(NI, P) for _ in range(2)]
        ysb = [cg(D) for _ in range(2)]
        b1c = [cw(NI) for _ in range(2)]
        tok = slots[:, 0:2]
        Z_full, h_r, w1_v, w1_a, U_full, gel_r, Y_full, y_r, put = counters = [
            sem(n) for n in ("Z_full", "h_r", "w1_v", "w1_a", "U_full", "gel_r", "Y_full", "y_r", "put")]
        z_ld, meta_ld, scat = sems("z_ld"), sems("meta_ld"), sem("scat")
        pool_pad = cg(8)

        def done(m):
            return m + 3

        def each_tile(eng, step, ahead=0):
            pairs = (NT - 3) // 2
            with eng.Fori(0, pairs) as i:
                for u in range(2):
                    step(2 * i + u, u, i)
            for n in range(2 * pairs, NT):
                step(n, n % 2, n // 2)

        def live(n):
            return not isinstance(n, int) or n < NT

        def one(n):
            return ds(n, 1)

        with nc.Block() as block:
            @block.sync
            def _(sp):
                prime(sp, FT_cp, FL_cp, zr_r, counters, counters)
                sp.dma_start(b2s[0:E], b2_d).then_inc(f_ld, 16)
                sp.dma_start(b1s, b1_d.rearrange("e p n -> p e n")).then_inc(f_wt, 16)
                sp.dma_start(lgs, lg_d.rearrange("e p n -> p e n")).then_inc(f_wt, 16)
                sp.dma_start(lbs, lb_d.rearrange("e p n -> p e n")).then_inc(f_wt, 16)
                for e in range(E):
                    sp.dma_start(w1s[:, e], w1_d[e].rearrange("(k p) n -> p k n", p=P)).then_inc(f_wt, 16)
                    sp.dma_start(w2s[:, e], w2_d[e].rearrange("(k p) n -> p k n", p=P)).then_inc(f_wt, 16)
                sp.wait_ge(f_x, 1)
                sp.dma_start(out_d[0:B * S].rearrange("(t p) d -> p t d", p=P), X[:, :, :]).then_inc(f_st, 16)
                sp.dma_start(out_d[B * S:B * S + P], X[:, 0]).then_inc(f_st, 16)
                sp.wait_ge(f_st, 32)
                sp.wait_ge(f_wt, 16 * (3 + 2 * E))

            @block.gpsimd
            def _(pool):
                pool.wait_ge(f_sl, 1)
                pool.wait_ge(f_cb, 1)
                for u in range(FS):
                    pool.wait_ge(zr_r[u], B // FS + 1)
                for k in range(2 * T):
                    pool.indirect_dma_start(out=rows_dram, out_offset=bass.IndirectOffsetOnAxis(ap=slots[:, k:k + 1], axis=0),
                                            in_=ZR[:, k % T, :], in_offset=None).then_inc(f_sc, 16)
                pool.wait_ge(f_sc, 16 * 2 * T)

            @block.tensor
            def _(pe):
                pe.wait_ge(f_w, 1)
                for k in range(KC):
                    mm = pe.matmul(bank(7, E), rnbb[:, k, :], rwT[:, k, :], start=(k == 0), stop=(k == KC - 1))
                mm.then_inc(f_rb, 1)
                with pe.Fori(0, B // FS) as i:
                    for u in range(FS):
                        pe.wait_ge(zt_r[u], i + 1)
                        pe.wait_ge(FT_cp[u], i + 1)
                        for k in range(KC):
                            for c in range(2):
                                mm = pe.transpose(bank(u, KC, 2, P)[:, k, c], hid[u][:, c, k * P:(k + 1) * P], ident)
                        mm.then_inc(FT_full[u], 1)
                    for u in range(FS):
                        pe.wait_ge(FT_cp[u], i + 1 + 1)
                        pe.wait_ge(FL_cp[u], i + 1)
                        for c in range(2):
                            for k in range(KC):
                                mm = pe.matmul(bank(4 + u, 2, E)[:, c], zs[u][:, k, c * P:(c + 1) * P], rwp[:, k, :],
                                               start=(k == 0), stop=(k == KC - 1))
                        mm.then_inc(FL_full[u], 1)
                pe.wait_ge(f_pk, 1)
                pe.matmul(bank(0, T * E), tri, picked.rearrange("p t e -> p (t e)"), start=True, stop=True)
                pe.matmul(bank(1, T * E), ones, picked.rearrange("p t e -> p (t e)"), start=True, stop=True).then_inc(f_ps, 1)
                pe.wait_ge(f_cb, 1)
                pe.wait_ge(f_ld, 16)
                for t in range(T):
                    mm = pe.transpose(bank(4 + t // 4, 4, P)[0:E, t % 4], comb[:, t, :], ident)
                mm.then_inc(f_ct, 1)
                pe.wait_ge(f_cc, 1)
                pe.wait_ge(f_sl, 1)
                for t in range(T):
                    mm = pe.matmul(bank(t // 2, 2, D)[:, t % 2], combT[0:E, t * P:(t + 1) * P], b2s[0:E],
                                   start=True, stop=True)
                mm.then_inc(f_bb, 1)

            @block.scalar
            def _(act):
                with act.Fori(0, B // FS) as i:
                    link = Chain(act, f_ach, FS * i)
                    for u in range(FS):
                        act.wait_ge(fmv_r[u], i + 1)
                        link(nc.scalar.activation(frs[u], fmv[u][:, :, 1], ACT.Ln, scale=1 + LN_EPS, bias=eps_ap[:, 1:2]))
                        nc.scalar.activation(frs[u], frs[u], ACT.Exp, scale=-0.5).then_inc(frs_r[u], 1)
                    for u in range(FS):
                        act.wait_ge(FT_full[u], i + 1)
                        nc.scalar.activation(zs[u], bank(u, KC, S), ACT.Copy).then_inc(FT_cp[u], 1)
                    for u in range(FS):
                        nc.scalar.activation(ZR[:, ds(2 * FS * i + 2 * u, 2), 0:D], hid[u], ACT.Copy).then_inc(zr_r[u], 1)
                act.wait_ge(f_df, 1)
                nc.scalar.activation(M2, M2, ACT.Exp).then_inc(f_ex, 1)
                act.wait_ge(f_ct, 1)
                for k in range(4):
                    ins = nc.scalar.activation(combT[0:E, k * 512:(k + 1) * 512], bank(4 + k, 512)[0:E], ACT.Copy)
                ins.then_inc(f_cc, 1)

            @block.vector
            def _(dve):
                pads = [0]

                def spacer():
                    nc.vector.memset(pad_v[:, pads[0] % 8:pads[0] % 8 + 1], 0.0)
                    pads[0] += 1

                nc.vector.tensor_copy(ZR[:, :, D], cst[:, C_TOK:C_TOK + T])
                for k in range(KC):
                    nc.vector.tensor_scalar(rnbb[:, k, :], ones, rnbc[:, k:k + 1], None, ALU.mult)
                    ins = nc.vector.tensor_scalar(rwp[:, k, :], rwT[:, k, :], rngc[:, k:k + 1], None, ALU.mult)
                ins.then_inc(f_w, 1)
                dve.wait_ge(f_rb, 1)
                nc.vector.tensor_tensor(rbb, bank(7, E), rbb, ALU.add)
                FCHAIN = FS
                with dve.Fori(0, B // FS) as i:
                    link = Chain(dve, f_ch, FCHAIN * i)

                    def tokens(u, c):
                        return X[:, ds(2 * FS * i + 2 * u + c, 1)].rearrange("p o d -> p (o d)")

                    for u in range(FS):
                        spacer()
                        for c in range(2):
                            ins = nc.vector.bn_stats(fst[u][:, c, :], tokens(u, c))
                        link(ins)
                        spacer()
                        for c in range(2):
                            ins = nc.vector.bn_aggr(fmv[u][:, c, :], fst[u][:, c, :])
                        ins.then_inc(fmv_r[u], 1)
                    for u in range(FS):
                        dve.wait_ge(frs_r[u], i + 1)
                        dve.wait_ge(FT_cp[u], i + 1)
                        dve.wait_ge(zr_r[u], i + 1)
                        for c in range(2):
                            ins = nc.vector.tensor_scalar(hid[u][:, c, :], tokens(u, c), fmv[u][:, c, 0:1],
                                                          frs[u][:, c:c + 1], ALU.subtract, ALU.mult)
                        ins.then_inc(zt_r[u], 1)
                    for u in range(FS):
                        dve.wait_ge(FL_full[u], i + 1)
                        nc.vector.tensor_tensor(LG[:, ds(2 * FS * i + 2 * u, 2), :], bank(4 + u, 2, E),
                                                rbb.unsqueeze(1).to_broadcast([P, 2, E]), ALU.add).then_inc(FL_cp[u], 1)
                    assert link.n == FCHAIN, link.n
                for u in range(FS):
                    dve.wait_ge(FL_cp[u], B // FS + 1)
                link = Chain(dve, f_ch, FCHAIN * (B // FS))
                iota = cst[:, C_IOTA:C_IOTA + E].unsqueeze(1).to_broadcast([P, T, E])

                def wide(a):
                    return a.unsqueeze(2).to_broadcast([P, T, E])

                src = LG
                for k, m in enumerate((M1, M2)):
                    link(nc.vector.tensor_reduce(out=m, in_=src, op=ALU.max, axis=AX))
                    link(nc.vector.tensor_tensor(EQ, src, wide(m), ALU.is_ge))
                    link(nc.vector.tensor_tensor(EQ, EQ, iota, ALU.mult))
                    link(nc.vector.tensor_reduce(out=IX, in_=EQ, op=ALU.min, axis=AX))
                    link(nc.vector.tensor_tensor(OH[k], iota, wide(IX), ALU.is_equal))
                    if k == 0:
                        link(nc.vector.tensor_scalar(LG2, OH[0], -3.0e38, None, ALU.mult))
                        link(nc.vector.tensor_tensor(LG2, LG2, LG, ALU.add))
                        src = LG2
                nc.vector.tensor_tensor(picked, OH[0], OH[1], ALU.add).then_inc(f_pk, 1)
                nc.vector.tensor_tensor(M2, M2, M1, ALU.subtract).then_inc(f_df, 1)
                dve.wait_ge(f_ps, 1)
                link(nc.vector.tensor_copy(count, bank(1, T, E).rearrange("p t e -> p e t")))
                link(nc.vector.tensor_tensor_scan(upto.rearrange("p e t -> p (e t)"), cst[:, C_RESET:C_RESET + E * T],
                                                  count.rearrange("p e t -> p (e t)"), 0.0, ALU.mult, ALU.add))
                link(nc.vector.tensor_tensor(over, upto[:, :, T - 1:T].to_broadcast([P, E, T]),
                                             cst[:, C_CNT:C_CNT + T].unsqueeze(1).to_broadcast([P, E, T]), ALU.is_gt))
                link(nc.vector.tensor_reduce(out=ntile, in_=over, op=ALU.add, axis=AX))
                link(nc.vector.tensor_tensor_scan(tile_end, ones[:, 0:E], ntile, 0.0, ALU.mult, ALU.add))
                link(nc.vector.tensor_tensor(open_, tile_end.unsqueeze(1).to_broadcast([P, NT, E]),
                                             cst[:, C_TILE:C_TILE + NT].unsqueeze(2).to_broadcast([P, NT, E]), ALU.is_le))
                link(nc.vector.tensor_reduce(out=tile_f, in_=open_, op=ALU.add, axis=AX))
                nc.vector.tensor_scalar(tile_e[:, :], tile_f, float(E - 1), None, ALU.min)
                link(nc.vector.tensor_tensor(base, tile_end, ntile, ALU.subtract))
                link(nc.vector.tensor_scalar(base, base, float(P), -1.0, ALU.mult, ALU.add))
                link(nc.vector.tensor_tensor(upto, upto, count, ALU.subtract))
                link(nc.vector.tensor_tensor(slot_of, upto.rearrange("p e t -> p t e"),
                                             base.unsqueeze(1).to_broadcast([P, T, E]), ALU.add))
                link(nc.vector.tensor_tensor(slot_of, bank(0, T, E), slot_of, ALU.add))
                for k in range(2):
                    link(nc.vector.tensor_tensor(EQ, OH[k], slot_of, ALU.mult))
                    link(nc.vector.tensor_reduce(out=slot_f[:, k * T:(k + 1) * T], in_=EQ, op=ALU.add, axis=AX))
                nc.vector.tensor_copy(slots[:, :], slot_f).then_inc(f_sl, 1)
                dve.wait_ge(f_ex, 1)
                link(nc.vector.tensor_scalar(PR, M2, 1.0, None, ALU.add))
                link(nc.vector.reciprocal(PR, PR))
                link(nc.vector.tensor_tensor(M2, M2, PR, ALU.mult))
                link(nc.vector.tensor_tensor(OH[0], OH[0], wide(PR), ALU.mult))
                link(nc.vector.tensor_tensor(OH[1], OH[1], wide(M2), ALU.mult))
                nc.vector.tensor_tensor(comb, OH[0], OH[1], ALU.add).then_inc(f_cb, 1)
                dve.wait_ge(f_bb, 1)
                for t in range(0, T, 2):
                    ins = nc.vector.tensor_tensor(X[:, t:t + 2, :], bank(t // 2, 2, D), X[:, t:t + 2, :], ALU.add)
                ins.then_inc(f_x, 1)

            @block.sync
            def _(sp):
                def load_z(n, u):
                    sp.dma_start(z_in[u], rows_dram[ds(n * P, P), 0:D]).then_inc(z_ld[u], 16)

                def load_meta(n, u):
                    sp.dma_start(meta[u], rows_dram[ds(n * P, P), D:ROW]).then_inc(meta_ld[u], 16)

                sp.wait_ge(f_sc, 16 * 2 * T)
                load_z(0, 0)
                load_z(1, 1)

                def step(n, u, i):
                    sp.wait_ge(y_r, done(n - 2))
                    sp.sem_inc(sp_on, 1)
                    load_meta(n, u)
                    if live(n + 2):
                        sp.wait_ge(Z_full, done(n))
                        sp.sem_inc(sp_on, 1)
                        load_z(n + 2, u)

                each_tile(sp, step)
                sp.wait_ge(scat, 16 * NT)

            @block.gpsimd
            def _(pool):
                def step(n, u, i):
                    pool.wait_ge(y_r, done(n))
                    nc.gpsimd.tensor_tensor(pool_pad[:, 2 * u:2 * u + 1], ones[:, 0:1], ones[:, 1:2], ALU.mult)
                    pool.indirect_dma_start(out=out_d, out_offset=bass.IndirectOffsetOnAxis(ap=tok[:, u:u + 1], axis=0),
                                            in_=ysb[u], in_offset=None, bounds_check=B * S + P - 1, oob_is_err=True,
                                            compute_op=ALU.add).then_inc(scat, 16)
                    pool.wait_ge(scat, 16 * (n + 1))
                    nc.gpsimd.tensor_tensor(pool_pad[:, 2 * u + 1:2 * u + 2], ones[:, 0:1], ones[:, 1:2], ALU.mult) \
                        .then_inc(put, 1)

                each_tile(pool, step)

            @block.tensor
            def _(pe):
                def turn_z(n, u, i):
                    pe.wait_ge(z_ld[u], 16 * (i + 1))
                    pe.wait_ge(h_r, done(n - 1))
                    for k in range(KC):
                        mm = pe.transpose(bank(0, 2, KC, P)[:, u, k], z_in[u][:, k * P:(k + 1) * P], ident)
                    mm.then_inc(Z_full, 1)

                def up(n, u, i):
                    pe.wait_ge(w1_v, done(n))
                    pe.wait_ge(w1_a, done(n))
                    pe.wait_ge(h_r, done(n))
                    pe.wait_ge(gel_r, done(n - 2))
                    for c in range(NI):
                        for k in range(KC):
                            mm = pe.matmul(bank(1 + 2 * u + c // 4, 4, P)[:, c % 4], w1c[u][:, k, c * P:(c + 1) * P],
                                           hT[u][:, k, :], start=(k == 0), stop=(k == KC - 1))
                    mm.then_inc(U_full, 1)

                def down(n, u, i):
                    e = pe.value_load(tile_e[0:1, one(n)], min_val=0, max_val=E - 1)
                    pe.wait_ge(gel_r, done(n))
                    pe.wait_ge(y_r, done(n - 1))
                    for c in range(NI):
                        mm = pe.matmul(bank(7, 2, D)[:, u], gel[u][:, c, :],
                                       w2s[:, one(e), c, :].rearrange("p o n -> p (o n)"),
                                       start=(c == 0), stop=(c == NI - 1))
                    mm.then_inc(Y_full, 1)

                pe.wait_ge(f_x, 1)
                pe.wait_ge(f_wt, 16 * (3 + 2 * E))
                turn_z(0, 0, 0)
                turn_z(1, 1, 0)
                up(0, 0, 0)

                def step(n, u, i):
                    if live(n + 1):
                        up(n + 1, 1 - u, i + u)
                    if live(n + 2):
                        turn_z(n + 2, u, i + 1)
                    down(n, u, i)

                each_tile(pe, step)

            @block.scalar
            def _(act):
                def weights(n, u, i):
                    e = act.value_load(tile_e[0:1, one(n)], min_val=0, max_val=E - 1)
                    act.wait_ge(U_full, done(n - 2))
                    nc.scalar.activation(w1c[u][:, 1], w1s[:, one(e), 1].rearrange("p o n -> p (o n)"), ACT.Copy) \
                        .then_inc(w1_a, 1)

                act.preload_act_table(ACT.Gelu)
                act.wait_ge(f_wt, 16 * (3 + 2 * E))
                act.wait_ge(f_bb, 1)
                weights(0, 0, 0)
                weights(1, 1, 0)

                def step(n, u, i):
                    act.wait_ge(U_full, done(n))
                    act.wait_ge(Y_full, done(n - 2))
                    for c in range(NI):
                        ins = nc.scalar.activation(gel[u][:, c, :], bank(1 + 2 * u + c // 4, 4, P)[:, c % 4], ACT.Gelu,
                                                   bias=b1c[u][:, c:c + 1])
                    ins.then_inc(gel_r, 1)
                    if live(n + 2):
                        weights(n + 2, u, i + 1)

                each_tile(act, step)

            @block.vector
            def _(dve):
                def weights(n, u, i):
                    e = dve.value_load(tile_e[0:1, one(n)], min_val=0, max_val=E - 1)
                    dve.wait_ge(U_full, done(n - 2))
                    nc.vector.tensor_scalar(w1c[u][:, 0], w1s[:, one(e), 0].rearrange("p o n -> p (o n)"), 1.0, None,
                                            ALU.mult)
                    dve.wait_ge(gel_r, done(n - 2))
                    nc.vector.tensor_scalar(b1c[u], b1s[:, one(e), :].rearrange("p o n -> p (o n)"), 1.0, None,
                                            ALU.mult).then_inc(w1_v, 1)

                def hidden(n, u, i):
                    e = dve.value_load(tile_e[0:1, one(n)], min_val=0, max_val=E - 1)
                    dve.wait_ge(Z_full, done(n))
                    dve.wait_ge(U_full, done(n - 2))
                    for k in range(KC):
                        ins = nc.vector.tensor_scalar(hT[u][:, k, :], bank(0, 2, KC, P)[:, u, k],
                                                      lgs[:, one(e), k], lbs[:, one(e), k], ALU.mult, ALU.add)
                    ins.then_inc(h_r, 1)

                dve.wait_ge(f_wt, 16 * (3 + 2 * E))
                for n in range(2):
                    weights(n, n, 0)
                for n in range(2):
                    hidden(n, n, 0)

                def step(n, u, i):
                    if live(n + 2):
                        weights(n + 2, u, i + 1)
                        hidden(n + 2, u, i + 1)
                    e = dve.value_load(tile_e[0:1, one(n)], min_val=0, max_val=E - 1)
                    dve.wait_ge(meta_ld[u], 16 * (i + 1))
                    dve.wait_ge(put, done(n - 1))
                    nc.vector.tensor_scalar(tok[:, u:u + 1], meta[u][:, 0:1], 0.0, None, ALU.add)
                    dve.wait_ge(Y_full, done(n))
                    nc.vector.tensor_scalar(ysb[u], bank(7, 2, D)[:, u], meta[u][:, ds(e + 1, 1)], None,
                                            ALU.mult).then_inc(y_r, 1)

                each_tile(dve, step)


def kernel(**inputs):
    import concourse.bacc as bacc
    from concourse.bass_utils import run_bass_kernel_spmd

    v = {k: np.asarray(a) for k, a in inputs.items()}
    wg = np.concatenate([v["L0_xattn_igate_w"], v["L0_xattn_fgate_w"]], 0).T
    arrays = {
        "x": v["x"], "ctx": v["ctx_1024"], "ctxr": v["ctx_1024"][:, :P - 1:-1],
        "idx": hop_layout(v["itok_SxS2_0_2016"]), "cst": constants(),
        "wqT": v["L0_attn_Wq"].T, "wkT": v["L0_attn_Wk"].T, "wvT": v["L0_attn_Wv"].T, "woT": v["L0_attn_Wo"].T,
        "wk": v["L0_attn_Wk"], "gw": np.tile(v["L0_attn_gw"].reshape(DA, 1), (HC, 1)),
        "sw": np.tile(v["L0_attn_sw"].reshape(DA, 1), (HC, 1)), "wg": wg,
        "gb": np.concatenate([v["L0_xattn_igate_b"], v["L0_xattn_fgate_b"]]), "rpe": v["L0_xattn_rpe"],
        "lnw": v["L0_xattn_ln_w"], "lnb": v["L0_xattn_ln_b"],
        "rng": v["L0_ffn_rn_g"].reshape(KC, P).T, "rnb": v["L0_ffn_rn_b"].reshape(KC, P).T,
        "rw": v["L0_ffn_router_w"].T, "rb": v["L0_ffn_router_b"],
        "lg": v["L0_ffn_ln_g"].reshape(E, KC, P).transpose(0, 2, 1),
        "lb": v["L0_ffn_ln_b"].reshape(E, KC, P).transpose(0, 2, 1),
        "w1": v["L0_ffn_w1"], "b1": v["L0_ffn_b1"].reshape(E, I // P, P).transpose(0, 2, 1),
        "w2": v["L0_ffn_w2"], "b2": v["L0_ffn_b2"],
    }
    arrays = {f"in_{k}": np.ascontiguousarray(a) for k, a in arrays.items()}
    nc = bacc.Bacc("TRN2", target_bir_lowering=False, num_devices=1)
    args = [nc.dram_tensor(k, a.shape, mybir.dt.from_np(a.dtype), kind="ExternalInput").ap() for k, a in arrays.items()]
    out = nc.dram_tensor("out", (B * S + P, D), F32, kind="ExternalOutput").ap()
    build(nc, *args, out)
    return run_bass_kernel_spmd(nc, [arrays], core_ids=[0]).results[0]["out"][0:B * S].reshape(B, S, D)
```
